# Optimizing a Trainium2 kernel written in Bass

```python
import numpy as np
import jax
import jax.numpy as jnp

def _softmax(x, axis=-1):
    return jax.nn.softmax(x, axis=axis)

def _gelu(x):
    return jax.nn.gelu(x, approximate=True)

def _silu(x):
    return jax.nn.silu(x)

def _sigmoid(x):
    return jax.nn.sigmoid(x)

def _layernorm(x, axis=-1, eps=1e-05):
    m = jnp.mean(x, axis=axis, keepdims=True)
    v = jnp.var(x, axis=axis, keepdims=True)
    return (x - m) / jnp.sqrt(v + eps)

def _scatter_add(tgt, idx, src, axis=0):
    return tgt.at[idx].add(src)

def _segment_sum(src, seg, n):
    return jax.ops.segment_sum(src, seg, n)
kernel_name = 'mk_audio_tower_d1_tok_aud1d768_r4_2fd6ad'

def setup_inputs(seed: int=0):
    np.random.seed(seed)
    _w = jnp.asarray

    def _rec_inputs():
        import jax
        import jax.numpy as jnp
        _rk = jax.random.key(seed)
        x = -0.000869125 + 1.00042 * jax.random.normal(jax.random.fold_in(_rk, 1), (64, 4000), jnp.float32)
        return x
    x = _rec_inputs()

    def _L0_tok_setup():
        import jax, jax.numpy as jnp
        import numpy as np
        CONVS = [(128, 10, 5)] + [(128, 3, 2)] * 4 + [(128, 2, 2)] * 2

        def _fp32_layernorm(x, g, b, eps=1e-05):
            xf = x.astype(jnp.float32)
            mu = xf.mean(-1, keepdims=True)
            var = xf.var(-1, keepdims=True)
            y = (xf - mu) * jax.lax.rsqrt(var + eps) * g.astype(jnp.float32) + b.astype(jnp.float32)
            return y.astype(x.dtype)

        def _conv1d(x, w, stride):
            return jax.lax.conv_general_dilated(x, w, (stride,), 'VALID', dimension_numbers=('NCH', 'OIH', 'NCH'))
        key = jax.random.key(seed)
        keys = jax.random.split(key, 16)
        inp = {'x': jax.random.normal(keys[0], (8, 40000), jnp.float32)}
        in_d = 1
        for i, (dim, k, s) in enumerate(CONVS):
            fan_in = in_d * k
            inp[f'conv_w{i}'] = jax.random.normal(keys[1 + i], (dim, in_d, k), jnp.float32) * np.float32(np.sqrt(2.0 / fan_in))
            inp[f'ln_g{i}'] = jnp.ones((dim,), jnp.float32)
            inp[f'ln_b{i}'] = jnp.zeros((dim,), jnp.float32)
            in_d = dim
        inp['fln_g'] = jnp.ones((128,), jnp.float32)
        inp['fln_b'] = jnp.zeros((128,), jnp.float32)
        inp['proj_w'] = jax.random.normal(keys[9], (128, 192), jnp.float32) * np.float32(0.02)
        inp['proj_b'] = jnp.zeros((192,), jnp.float32)
        return inp
    _L0_tok_all = _L0_tok_setup()
    _L0_tok_in = {k: v for k, v in _L0_tok_all.items() if k in ('conv_w0', 'ln_g0', 'ln_b0', 'conv_w1', 'ln_g1', 'ln_b1', 'conv_w2', 'ln_g2', 'ln_b2', 'conv_w3', 'ln_g3', 'ln_b3', 'conv_w4', 'ln_g4', 'ln_b4', 'conv_w5', 'ln_g5', 'ln_b5', 'conv_w6', 'ln_g6', 'ln_b6', 'fln_g', 'fln_b', 'proj_w', 'proj_b')}
    del _L0_tok_all

    def _L0_attn_setup():
        import jax, jax.numpy as jnp
        import numpy as np
        EMBED_DIM = 192
        NUM_HEADS = 12
        HEAD_DIM = EMBED_DIM // NUM_HEADS
        SEG_LEN = 64
        DILATION = 1

        def _dilated_mask(seq_len):
            idx = jnp.arange(seq_len)
            seg_id = idx // SEG_LEN
            on_stride = idx % SEG_LEN % DILATION == 0
            valid = (seg_id[:, None] == seg_id[None, :]) & on_stride[:, None] & on_stride[None, :]
            return jnp.where(valid, 0.0, -jnp.inf).astype(jnp.float32)
        key = jax.random.key(seed)
        ks = jax.random.split(key, 9)
        B, S, E = (2, 512, EMBED_DIM)
        w = lambda k: jax.random.normal(k, (E, E), jnp.float32) * 0.02
        b = lambda k: jax.random.normal(k, (E,), jnp.float32) * 0.02
        return {'x': jax.random.normal(ks[0], (B, S, E), jnp.float32), 'Wq': w(ks[1]), 'bq': b(ks[2]), 'Wk': w(ks[3]), 'bk': b(ks[4]), 'Wv': w(ks[5]), 'bv': b(ks[6]), 'Wo': w(ks[7]), 'bo': b(ks[8])}
    _L0_attn_all = _L0_attn_setup()
    _L0_attn_in = {k: v for k, v in _L0_attn_all.items() if k in ('Wq', 'bq', 'Wk', 'bk', 'Wv', 'bv', 'Wo', 'bo')}
    del _L0_attn_all

    def _L0_ffn_setup():
        import jax, jax.numpy as jnp
        import numpy as np
        B, S, D = (4, 256, 192)
        E = 8
        H = 192
        HS = 768
        TOPK_ROUTED = 2
        key = jax.random.key(seed)
        ks = jax.random.split(key, 10)
        w = lambda k, shape: jax.random.normal(k, shape, dtype=jnp.float32) * 0.02
        return {'x': jax.random.normal(ks[0], (B, S, D), dtype=jnp.float32), 'router_w': w(ks[1], (D, E)), 'w_gate': w(ks[2], (E, D, H)), 'w_up': w(ks[3], (E, D, H)), 'w_down': w(ks[4], (E, H, D)), 'ws_gate': w(ks[5], (D, HS)), 'ws_up': w(ks[6], (D, HS)), 'ws_down': w(ks[7], (HS, D)), 'sg_w': w(ks[8], (D, 1)), 'sg_b': jnp.zeros((1,), jnp.float32)}
    _L0_ffn_all = _L0_ffn_setup()
    _L0_ffn_in = {k: v for k, v in _L0_ffn_all.items() if k in ('router_w', 'w_gate', 'w_up', 'w_down', 'ws_gate', 'ws_up', 'ws_down', 'sg_w', 'sg_b')}
    del _L0_ffn_all
    return {'x': x, 'L0_tok_conv_w0': _L0_tok_in['conv_w0'], 'L0_tok_ln_g0': _L0_tok_in['ln_g0'], 'L0_tok_ln_b0': _L0_tok_in['ln_b0'], 'L0_tok_conv_w1': _L0_tok_in['conv_w1'], 'L0_tok_ln_g1': _L0_tok_in['ln_g1'], 'L0_tok_ln_b1': _L0_tok_in['ln_b1'], 'L0_tok_conv_w2': _L0_tok_in['conv_w2'], 'L0_tok_ln_g2': _L0_tok_in['ln_g2'], 'L0_tok_ln_b2': _L0_tok_in['ln_b2'], 'L0_tok_conv_w3': _L0_tok_in['conv_w3'], 'L0_tok_ln_g3': _L0_tok_in['ln_g3'], 'L0_tok_ln_b3': _L0_tok_in['ln_b3'], 'L0_tok_conv_w4': _L0_tok_in['conv_w4'], 'L0_tok_ln_g4': _L0_tok_in['ln_g4'], 'L0_tok_ln_b4': _L0_tok_in['ln_b4'], 'L0_tok_conv_w5': _L0_tok_in['conv_w5'], 'L0_tok_ln_g5': _L0_tok_in['ln_g5'], 'L0_tok_ln_b5': _L0_tok_in['ln_b5'], 'L0_tok_conv_w6': _L0_tok_in['conv_w6'], 'L0_tok_ln_g6': _L0_tok_in['ln_g6'], 'L0_tok_ln_b6': _L0_tok_in['ln_b6'], 'L0_tok_fln_g': _L0_tok_in['fln_g'], 'L0_tok_fln_b': _L0_tok_in['fln_b'], 'L0_tok_proj_w': _L0_tok_in['proj_w'], 'L0_tok_proj_b': _L0_tok_in['proj_b'], 'L0_attn_Wq': _L0_attn_in['Wq'], 'L0_attn_bq': _L0_attn_in['bq'], 'L0_attn_Wk': _L0_attn_in['Wk'], 'L0_attn_bk': _L0_attn_in['bk'], 'L0_attn_Wv': _L0_attn_in['Wv'], 'L0_attn_bv': _L0_attn_in['bv'], 'L0_attn_Wo': _L0_attn_in['Wo'], 'L0_attn_bo': _L0_attn_in['bo'], 'L0_ffn_router_w': _L0_ffn_in['router_w'], 'L0_ffn_w_gate': _L0_ffn_in['w_gate'], 'L0_ffn_w_up': _L0_ffn_in['w_up'], 'L0_ffn_w_down': _L0_ffn_in['w_down'], 'L0_ffn_ws_gate': _L0_ffn_in['ws_gate'], 'L0_ffn_ws_up': _L0_ffn_in['ws_up'], 'L0_ffn_ws_down': _L0_ffn_in['ws_down'], 'L0_ffn_sg_w': _L0_ffn_in['sg_w'], 'L0_ffn_sg_b': _L0_ffn_in['sg_b']}

def reference(x, L0_tok_conv_w0, L0_tok_ln_g0, L0_tok_ln_b0, L0_tok_conv_w1, L0_tok_ln_g1, L0_tok_ln_b1, L0_tok_conv_w2, L0_tok_ln_g2, L0_tok_ln_b2, L0_tok_conv_w3, L0_tok_ln_g3, L0_tok_ln_b3, L0_tok_conv_w4, L0_tok_ln_g4, L0_tok_ln_b4, L0_tok_conv_w5, L0_tok_ln_g5, L0_tok_ln_b5, L0_tok_conv_w6, L0_tok_ln_g6, L0_tok_ln_b6, L0_tok_fln_g, L0_tok_fln_b, L0_tok_proj_w, L0_tok_proj_b, L0_attn_Wq, L0_attn_bq, L0_attn_Wk, L0_attn_bk, L0_attn_Wv, L0_attn_bv, L0_attn_Wo, L0_attn_bo, L0_ffn_router_w, L0_ffn_w_gate, L0_ffn_w_up, L0_ffn_w_down, L0_ffn_ws_gate, L0_ffn_ws_up, L0_ffn_ws_down, L0_ffn_sg_w, L0_ffn_sg_b):
    import jax
    import jax.numpy as jnp

    def _L0_tok_ref(x, conv_w0, ln_g0, ln_b0, conv_w1, ln_g1, ln_b1, conv_w2, ln_g2, ln_b2, conv_w3, ln_g3, ln_b3, conv_w4, ln_g4, ln_b4, conv_w5, ln_g5, ln_b5, conv_w6, ln_g6, ln_b6, fln_g, fln_b, proj_w, proj_b):
        import jax, jax.numpy as jnp
        import numpy as np
        CONVS = [(128, 10, 5)] + [(128, 3, 2)] * 4 + [(128, 2, 2)] * 2

        def _fp32_layernorm(x, g, b, eps=1e-05):
            xf = x.astype(jnp.float32)
            mu = xf.mean(-1, keepdims=True)
            var = xf.var(-1, keepdims=True)
            y = (xf - mu) * jax.lax.rsqrt(var + eps) * g.astype(jnp.float32) + b.astype(jnp.float32)
            return y.astype(x.dtype)

        def _conv1d(x, w, stride):
            return jax.lax.conv_general_dilated(x, w, (stride,), 'VALID', dimension_numbers=('NCH', 'OIH', 'NCH'))
        conv_ws = [conv_w0, conv_w1, conv_w2, conv_w3, conv_w4, conv_w5, conv_w6]
        ln_gs = [ln_g0, ln_g1, ln_g2, ln_g3, ln_g4, ln_g5, ln_g6]
        ln_bs = [ln_b0, ln_b1, ln_b2, ln_b3, ln_b4, ln_b5, ln_b6]
        strides = [s for _, _, s in CONVS]
        h = x[:, None, :]
        for w, g, b, s in zip(conv_ws, ln_gs, ln_bs, strides):
            h = _conv1d(h, w, s)
            h = jnp.swapaxes(h, -2, -1)
            h = _fp32_layernorm(h, g, b)
            h = jnp.swapaxes(h, -2, -1)
            h = jax.nn.gelu(h, approximate=False)
        h = jnp.swapaxes(h, 1, 2)
        norm_h = _fp32_layernorm(h, fln_g, fln_b)
        out = norm_h @ proj_w + proj_b
        return out

    def _L0_attn_ref(x, Wq, bq, Wk, bk, Wv, bv, Wo, bo):
        import jax, jax.numpy as jnp
        import numpy as np
        EMBED_DIM = 192
        NUM_HEADS = 12
        HEAD_DIM = EMBED_DIM // NUM_HEADS
        SEG_LEN = 64
        DILATION = 1

        def _dilated_mask(seq_len):
            idx = jnp.arange(seq_len)
            seg_id = idx // SEG_LEN
            on_stride = idx % SEG_LEN % DILATION == 0
            valid = (seg_id[:, None] == seg_id[None, :]) & on_stride[:, None] & on_stride[None, :]
            return jnp.where(valid, 0.0, -jnp.inf).astype(jnp.float32)
        B, S, E = x.shape
        H, D = (NUM_HEADS, HEAD_DIM)

        def proj(W, b):
            return (x @ W.T + b).reshape(B, S, H, D).transpose(0, 2, 1, 3)
        q = proj(Wq, bq)
        k = proj(Wk, bk)
        v = proj(Wv, bv)
        mask = _dilated_mask(S)
        scores = jnp.einsum('bhqd,bhkd->bhqk', q, k) / jnp.sqrt(jnp.float32(D))
        attn = jax.nn.softmax(scores + mask, axis=-1)
        ctx = jnp.einsum('bhqk,bhkd->bhqd', attn, v)
        ctx = ctx.transpose(0, 2, 1, 3).reshape(B, S, E)
        return ctx @ Wo.T + bo

    def _L0_ffn_ref(x, router_w, w_gate, w_up, w_down, ws_gate, ws_up, ws_down, sg_w, sg_b):
        import jax, jax.numpy as jnp
        import numpy as np
        B, S, D = (4, 256, 192)
        E = 8
        H = 192
        HS = 768
        TOPK_ROUTED = 2
        probs = jax.nn.softmax(x @ router_w, axis=-1)
        gates, idx = jax.lax.top_k(probs, TOPK_ROUTED)
        gates = gates / jnp.sum(gates, axis=-1, keepdims=True)
        n_exp = router_w.shape[1]
        dense_g = jnp.sum(jax.nn.one_hot(idx, n_exp, dtype=x.dtype) * gates[..., None], axis=-2)
        g = jax.nn.silu(jnp.einsum('bsd,edh->bseh', x, w_gate))
        u = jnp.einsum('bsd,edh->bseh', x, w_up)
        expert_out = jnp.einsum('bseh,ehd->bsed', g * u, w_down)
        routed = jnp.einsum('bse,bsed->bsd', dense_g, expert_out)
        shared = jax.nn.silu(x @ ws_gate) * (x @ ws_up) @ ws_down
        alpha = jax.nn.sigmoid(x @ sg_w + sg_b)
        return alpha * shared + (1.0 - alpha) * routed
    h = _L0_tok_ref(x, L0_tok_conv_w0, L0_tok_ln_g0, L0_tok_ln_b0, L0_tok_conv_w1, L0_tok_ln_g1, L0_tok_ln_b1, L0_tok_conv_w2, L0_tok_ln_g2, L0_tok_ln_b2, L0_tok_conv_w3, L0_tok_ln_g3, L0_tok_ln_b3, L0_tok_conv_w4, L0_tok_ln_g4, L0_tok_ln_b4, L0_tok_conv_w5, L0_tok_ln_g5, L0_tok_ln_b5, L0_tok_conv_w6, L0_tok_ln_g6, L0_tok_ln_b6, L0_tok_fln_g, L0_tok_fln_b, L0_tok_proj_w, L0_tok_proj_b)
    h = h + _L0_attn_ref(_layernorm(h, axis=-1), L0_attn_Wq, L0_attn_bq, L0_attn_Wk, L0_attn_bk, L0_attn_Wv, L0_attn_bv, L0_attn_Wo, L0_attn_bo)
    h = h + _L0_ffn_ref(_layernorm(h, axis=-1), L0_ffn_router_w, L0_ffn_w_gate, L0_ffn_w_up, L0_ffn_w_down, L0_ffn_ws_gate, L0_ffn_ws_up, L0_ffn_ws_down, L0_ffn_sg_w, L0_ffn_sg_b)
    return h

_drawn_inputs = setup_inputs


def setup_inputs(seed=0):
    import zlib

    import numpy as np

    out = dict(_drawn_inputs(seed))
    spreads = {'L0_tok_ln_g0': (1.0, 0.2),
     'L0_tok_ln_b0': (0.0, 0.1),
     'L0_tok_ln_g1': (1.0, 0.2),
     'L0_tok_ln_b1': (0.0, 0.1),
     'L0_tok_ln_g2': (1.0, 0.2),
     'L0_tok_ln_b2': (0.0, 0.1),
     'L0_tok_ln_g3': (1.0, 0.2),
     'L0_tok_ln_b3': (0.0, 0.1),
     'L0_tok_ln_g4': (1.0, 0.2),
     'L0_tok_ln_b4': (0.0, 0.1),
     'L0_tok_ln_g5': (1.0, 0.2),
     'L0_tok_ln_b5': (0.0, 0.1),
     'L0_tok_ln_g6': (1.0, 0.2),
     'L0_tok_ln_b6': (0.0, 0.1),
     'L0_tok_fln_g': (1.0, 0.2),
     'L0_tok_fln_b': (0.0, 0.1),
     'L0_tok_proj_b': (0.0, 0.1)}
    factors = {'L0_attn_Wq': 8.0,
     'L0_attn_bq': 8.0,
     'L0_attn_Wk': 8.0,
     'L0_attn_bk': 8.0,
     'L0_attn_bv': 2.821,
     'L0_ffn_router_w': 5.6,
     'L0_ffn_w_gate': 4.971,
     'L0_ffn_w_up': 5.074,
     'L0_ffn_w_down': 4.88,
     'L0_ffn_sg_w': 5.194}
    for name, (base, spread) in spreads.items():
        noise = np.random.default_rng([zlib.crc32(name.encode()), seed]).standard_normal(out[name].shape)
        drawn = base * np.exp(spread * noise) if base else spread * noise
        out[name] = jnp.asarray(drawn.astype(out[name].dtype))
    for name, factor in factors.items():
        out[name] = (out[name] * factor).astype(out[name].dtype)
    return out
```

```python
from contextlib import ExitStack
from typing import NamedTuple

import concourse.bass as bass
import numpy as np
from concourse import mybir

F32 = mybir.dt.float32
BF16 = mybir.dt.bfloat16
ALU = mybir.AluOpType
ACT = mybir.ActivationFunctionType
AX = mybir.AxisListType

P = 128
CLIPS, SAMPLES, FRAMES = 64, 4000, 12
TAPS0, STRIDE0 = 10, 5
HALF_START = 1920
HALF_SAMPLES = 2005
CHUNK = 20
CHUNK_SAMPLES = STRIDE0 * (CHUNK - 1) + TAPS0
CHUNK_STEP = STRIDE0 * CHUNK
ITERS = 10
RING0, RING1, STEP2 = 40, 20, 10
BATCH_T = 8
TAPS = {1: 3, 2: 3, 3: 3, 4: 3, 5: 2, 6: 2}
TILES = {3: 49, 4: 24, 5: 12, 6: 6}
BLOCK0 = {1: 0, 2: 3, 3: 6, 4: 9, 5: 12, 6: 14}
BLOCKS, EARLY_BLOCKS = 16, 6
EPS = 1e-5
E, HEADS, HD = 192, 12, 16
TOK = CLIPS * FRAMES
TT, NT = 96, 8
FT, NF = 128, 6
HALF = TOK // 2
EXPERTS = 8
HC, ROUTED_HC = 18, 12

SLOTS = [(1, 0, 4, 0), (2, 4, 4, 1), (1, 4, 4, 0), (2, 8, 2, 1),
         (1, 8, 4, 0), (1, 12, 4, 0), (2, 0, 4, 0), (1, 16, 4, 0)]
NS = len(SLOTS)
C1_SLOT = [0, 2, 4, 5, 7]
C2_FIRST, C2_MID, C2_LAST = 6, 1, 3
BANK = [0, 1, 2, 0, 1, 2, 0, 1]
BANK_USED = [2, 2, 5, 3, 3, 3, 3, 3]
BATCH = {0: 1, 2: 2, 3: 3, 5: 4, 6: 5}
FIRST_SLOTS = [s for s in range(NS) if SLOTS[s][3] == 0]
CH_STAGE, CH_TURN, CH_COPY, CH_GRAM, CH_QUAD, CH_SPLIT = (
    {0: 2, 3: 3}, {1: 2, 4: 3}, {2: 2, 5: 3}, {2: 2, 5: 3}, {3: 2, 6: 3}, {4: 2, 7: 3})
SPLIT_STEPS = 5
CONSTS = 5

TOK_CONSTS = 3
ATT_LOADS = 14
QKV_GROUPS = 16

CHUNK_ORDER = list(range(ROUTED_HC, HC)) + list(range(ROUTED_HC))
DOWN_BLOCKS = ROUTED_HC // 3 * 4 + HC - ROUTED_HC
DOWN = [(list(range(ROUTED_HC, HC)), list(range(DOWN_BLOCKS - (HC - ROUTED_HC), DOWN_BLOCKS)), 2 * (HC - ROUTED_HC))]
for _e in range(EXPERTS):
    _c, _b = 3 * (_e // 2) + _e % 2, 4 * (_e // 2) + 2 * (_e % 2)
    DOWN.append(([_c, _c + 1], [_b, _b + 1], 2 * (HC - ROUTED_HC) + 2 * (_c + 2)))


def ffn_order():
    out, down = [], 0
    for v in range(2 * HC):
        out.append(("hidden", v))
        if down < len(DOWN) and DOWN[down][2] + 1 <= v:
            out.append(("down", down))
            down += 1
    return out + [("down", d) for d in range(down, len(DOWN))]


FFN_ORDER = ffn_order()


def number(i, s):
    if isinstance(i, int) and i == 0:
        return FIRST_SLOTS.index(s)
    return i * NS + (s - (NS - len(FIRST_SLOTS)))


class Group(NamedTuple):
    n: object
    layer: int
    inputs: list
    wrap: int
    out: object
    tiles: int
    bank: int
    par: int
    fed: tuple
    bank_free: object
    out_free: tuple
    batch: object


def group(i, s):
    first = isinstance(i, int) and i == 0
    if first and s not in FIRST_SLOTS:
        return None
    layer, t0, tiles, back = SLOTS[s]
    n = number(i, s)
    used = n - BANK_USED[s]
    if first:
        same = [number(0, z) for z in FIRST_SLOTS if z < s and BANK[z] == BANK[s]]
        used = same[-1] if same else None
    par = n % 2 if first else s % 2
    if layer == 1:
        q = t0 // 4
        inputs = [(2 * t - 2) % RING0 for t in range(t0, t0 + 4)]
        if q == 4:
            free = (number(i, C2_FIRST),)
        elif first:
            free = ()
        else:
            free = (number_before(i, C2_FIRST) if q == 0 else number(i, C2_MID if q < 3 else C2_LAST),)
        return Group(n, 1, inputs, RING0, t0, tiles, BANK[s], par, (), used, free, 5 * i + q + 1)
    inputs = [(2 * m - 1) % RING1 for m in range(t0, t0 + tiles)]
    q = (2 * (t0 + tiles - 1) + 1) // 4
    fed = number(i, C1_SLOT[q]) if back == 0 else number_before(i, C1_SLOT[q])
    return Group(n, 2, inputs, RING1, (i - back) * STEP2 + t0, tiles, BANK[s], par, (fed,), used, (), None)


def number_before(i, s):
    if isinstance(i, int):
        return number(i - 1, s)
    return i * NS + (s - (NS - len(FIRST_SLOTS)) - NS)


BEFORE_TAIL = len(FIRST_SLOTS) + NS * (ITERS - 1)


def tail():
    late = 4
    todo = [(2, 4, 4), (2, 8, 2)] + [(k, t, min(4, TILES[k] - t)) for k in (3, 4, 5, 6)
                                     for t in range(0, TILES[k], 4)]
    made = {}
    for it in range(ITERS):
        for m in range(STEP2):
            s = C2_FIRST if m < 4 else (C2_MID if m < 8 else C2_LAST)
            if s == C2_FIRST or it < ITERS - 1:
                made[2, STEP2 * it + m] = number(it if s == C2_FIRST else it + 1, s)
    order = []
    while todo:
        best = None
        for k, (layer, t, tiles) in enumerate(todo):
            if any(z[0] == layer for z in todo[:k]):
                continue
            if layer == 2:
                need = number(ITERS - 1, C1_SLOT[3 if t == 4 else 4])
            else:
                top = 2 * (t + tiles - 1) + TAPS[layer] - 1 + (layer == 3)
                need = made.get((layer - 1, top))
            if need is None:
                continue
            age = BEFORE_TAIL + len(order) - need
            rank = (age >= late, layer if age >= late else age)
            if best is None or rank > best[0]:
                best = (rank, k, need)
        _, k, need = best
        layer, t, tiles = todo.pop(k)
        n = BEFORE_TAIL + len(order)
        base = STEP2 * (ITERS - 1) if layer == 2 else 0
        if layer == 2:
            inputs = [(2 * m - 1) % RING1 for m in range(t, t + tiles)]
        else:
            inputs = [2 * m + (layer == 3) for m in range(t, t + tiles)]
        order.append(Group(n, layer, inputs, RING1 if layer == 2 else 0, base + t, tiles,
                           (2 + len(order)) % 3, n % 2, (need,), n - 3, (), None))
        for m in range(tiles):
            made[layer, base + t + m] = n
    return order


TAIL = tail()
GROUPS = BEFORE_TAIL + len(TAIL)


def back(i, s, d):
    if isinstance(i, int) and i == 0:
        at = FIRST_SLOTS.index(s) - d
        return group(0, FIRST_SLOTS[at]) if at >= 0 else None
    z = (s - d) % NS
    if z <= s:
        return group(i, z)
    if isinstance(i, int):
        return group(i - 1, z)
    g = group(i, z)
    less = lambda v: None if v is None else v - NS
    return g._replace(n=number_before(i, z), fed=tuple(map(less, g.fed)), bank_free=less(g.bank_free),
                      out_free=tuple(map(less, g.out_free)),
                      out=g.out - STEP2 if g.layer == 2 else g.out)


def audio_tower(nc: bass.Bass, x, conv_w, w0_rows, pick_term, shift, columns, ident, ident_b, proj, proj_b, wq, wk, wv, wo,
                router, gate, up, down, clip_rows, clip_mask, head_rows, rank, out):
    with ExitStack() as ctx:
        def sb(name, shape, dt=F32):
            return ctx.enter_context(nc.sbuf_tensor(name, shape, dt))

        def sem(name):
            return ctx.enter_context(nc.semaphore(name))

        shared = sb("shared", [P, DOWN_BLOCKS * E])
        wd_sb = shared[:, :].rearrange("p (b e) -> p b e", e=E)
        cw = shared[:, 0:BLOCKS * P].rearrange("p (k c) -> p k c", c=P)
        x_sb = shared[:, BLOCKS * P:BLOCKS * P + HALF_SAMPLES]
        cmean = sb("cmean", [P, BLOCKS])
        w0 = sb("w0", [P, P])
        w0mean = sb("w0mean", [P, 1])
        w0rest = sb("w0rest", [P, P])
        w0term = sb("w0term", [P, 3, P], BF16)
        w0_stack = sb("w0_stack", [P, P], BF16)
        pick_sb = sb("pick_sb", [P, 3])
        w0T = sb("w0T", [P, TAPS0])
        gram = sb("gram", [TAPS0, TAPS0])
        shift_sb = sb("shift_sb", [TAPS0, 2 * CHUNK_STEP])
        gband = sb("gband", [CHUNK_SAMPLES, CHUNK * TAPS0])
        col = sb("col", [P, 16])
        id_f = sb("id_f", [P, P])
        id_b = sb("id_b", [P, P], BF16)
        neg_half, eps = sb("neg_half", [P, CHUNK]), sb("eps", [P, 4])
        stage = sb("stage", [P, 2, CHUNK_SAMPLES])
        stageT = sb("stageT", [CHUNK_SAMPLES, P])
        quad = sb("quad", [P, CHUNK, TAPS0])
        var0 = sb("var0", [P, CHUNK])
        vare0 = sb("vare0", [P, CHUNK])
        rstd0 = sb("rstd0", [P, CHUNK])
        xs = sb("xs", [P, CHUNK, TAPS0])
        xrest = sb("xrest", [P, CHUNK, TAPS0])
        terms = sb("terms", [P, RING0, 64], BF16)
        termsT = sb("termsT", [P, 512], BF16)
        sq = sb("sq", [P, 2, 512])
        var = sb("var", [P, 2, 4])
        vare = sb("vare", [P, 2, 4])
        rstd = sb("rstd", [P, 2, 4])
        yn = sb("yn", [P, 2, 512])
        early = sb("early", [P, RING0 * P])
        x1 = sb("x1", [P, RING1 * P])
        x2 = sb("x2", [P, HC * TOK])
        x3 = sb("x3", [P, TILES[3] * P])
        x6 = sb("x6", [P, TILES[6] * P])
        acts = {0: early, 1: x1, 2: x2, 3: x3, 4: early[:, 0:TILES[4] * P],
                5: early[:, TILES[4] * P:(TILES[4] + TILES[5]) * P], 6: x6}

        proj_sb, proj_b_sb, ones = sb("proj_sb", [P, E]), sb("proj_b_sb", [1, E]), sb("ones", [1, TT])
        wq_sb, wk_sb, wv_sb, wo_sb, wr_sb, wg_sb, wu_sb = (
            (sb(n + "_a", [P, w]), sb(n + "_b", [65, w])) for n, w in
            (("wq", 3 * P), ("wk", 3 * P), ("wv", E), ("wo", E), ("wr", EXPERTS + 1), ("wg", HC * P), ("wu", HC * P)))
        clip_rows_sb, clip_mask_sb = sb("clip_rows_sb", [8, HALF], BF16), sb("clip_mask_sb", [8, HALF], BF16)
        head_rows_sb = sb("head_rows_sb", [8, P], BF16)
        rank_sb = sb("rank_sb", [P, NF * EXPERTS])
        stat, mv = sb("stat", [P, NT, 6]), sb("mv", [P, NT, 2])
        vtok, rtok = sb("vtok", [P, NT]), sb("rtok", [P, NT])
        nT = x3[:, 0:TOK]
        h1, h2, y = (x3[0:TT, TOK + k * NT * E:TOK + (k + 1) * NT * E].rearrange("p (a e) -> p a e", e=E) for k in range(3))
        acc = early[:, 0:NF * E].rearrange("p (f e) -> p f e", e=E)
        qT = early[:, NF * E:NF * E + 3 * TOK].rearrange("p (c t) -> p c t", t=TOK)
        yT_a = early[:, NF * E + 3 * TOK:NF * E + 4 * TOK]
        yT_b = sb("yT_b", [65, TOK])
        kT = x1[:, 0:3 * TOK].rearrange("p (c t) -> p c t", t=TOK)
        att = x2[0:TT, 0:2 * HEADS * TT].rearrange("p (two h k) -> p two h k", two=2, k=TT)
        attT = x2[0:TT, 2 * HEADS * TT:3 * HEADS * TT].rearrange("p (h k) -> p h k", k=TT)
        vext = x2[0:TT, 3 * HEADS * TT:3 * HEADS * TT + NT * HEADS * (HD + 1)].rearrange(
            "p (a h d) -> p a h d", h=HEADS, d=HD + 1)
        hidden = x2[:, 0:HC * TOK].rearrange("p (c t) -> p c t", t=TOK)
        top, rsum = sb("top", [TT, HEADS]), sb("rsum", [TT, HEADS])
        heads_out = sb("heads_out", [TT, E])
        logits = sb("logits", [P, NF, EXPERTS + 1])
        prob, key, first, second, gates = (sb(n, [P, NF, EXPERTS]) for n in ("prob", "key", "first", "second", "gates"))
        small = sb("small", [P, 8, NF])
        silu = sq[:, :, 0:HALF]

        ps = ctx.enter_context(nc.psum_tensor("ps", [P, 8, 512], F32))
        prod = [ps[:, b, :] for b in range(3)]
        turn = ps[:, 3, :]
        c0_ps = ps[:, 4:6, :]
        term_ps = ps[:, 6, :].bitcast(BF16)
        chunk_ps = ps[:, 7, :]

        x_in, w0_in, cw_in, cw2_in, col_in = (sem(n) for n in ("x_in", "w0_in", "cw_in", "cw2_in", "col_in"))
        consts = sem("consts")
        w0_step = sem("w0_step")
        w0_turned, gram_made, gband_made, gband_ready = (
            sem(n) for n in ("w0_turned", "gram_made", "gband_made", "gband_ready"))
        cmean_step, cw_ready = sem("cmean_step"), sem("cw_ready")
        staged, stage_turned, stage_copied, gram_x = (
            sem(n) for n in ("staged", "stage_turned", "stage_copied", "gram_x"))
        quad_made, var0_made, vare0_made, rstd0_made, split_step = (
            sem(n) for n in ("quad_made", "var0_made", "vare0_made", "rstd0_made", "split_step"))
        terms_turned, terms_copied, conv0_done, act0_done = (
            sem(n) for n in ("terms_turned", "terms_copied", "conv0_done", "act0_done"))
        conv_done, sq_done, var_done, rstd_step, rstd_done, norm_done, turned, act_done = (
            sem(n) for n in ("conv_done", "sq_done", "var_done", "rstd_step", "rstd_done", "norm_done",
                             "turned", "act_done"))
        proj_in, att_in, ffn_in, down_in = (sem(n) for n in ("proj_in", "att_in", "ffn_in", "down_in"))
        fln_turned, fln_stats, fln_norm, fln_back, fln_done = (
            sem(n) for n in ("fln_turned", "fln_stats", "fln_norm", "fln_back", "fln_done"))
        tok_consts, tok_var, tok_rstd = sem("tok_consts"), sem("tok_var"), sem("tok_rstd")
        proj_done, h1_ready, h2_ready = sem("proj_done"), sem("h1_ready"), sem("h2_ready")
        ln_stats, ln_norm, ln_turned, yTa_ready, yTb_ready = (
            sem(n) for n in ("ln_stats", "ln_norm", "ln_turned", "yTa_ready", "yTb_ready"))
        qkv_done, qkv_by_act, qkv_by_dve = sem("qkv_done"), sem("qkv_by_act"), sem("qkv_by_dve")
        scores_done, top_done, shifted, exp_done = (sem(n) for n in ("scores_done", "top_done", "shifted", "exp_done"))
        att_turned, att_copied, values_done, rsum_done, heads_done, heads_turned, heads_copied = (
            sem(n) for n in ("att_turned", "att_copied", "values_done", "rsum_done", "heads_done", "heads_turned",
                             "heads_copied"))
        out_done = sem("out_done")
        router_done, router_step, router_exp, gates_ready = (
            sem(n) for n in ("router_done", "router_step", "router_exp", "gates_ready"))
        h2_moved = sem("h2_moved")
        hid_done, silu_done, hid_ready = sem("hid_done"), sem("silu_done"), sem("hid_ready")
        down_done, acc_done = sem("down_done"), sem("acc_done")
        stored = sem("stored")

        def window(c):
            s = stage[:, c, :]
            return bass.AP(tensor=s.tensor, offset=s.offset, ap=[list(s.ap[0]), [STRIDE0, CHUNK], [1, TAPS0]])

        def tiles(buf, first, n):
            return buf[:, bass.ds(first * P, n * P)] if not isinstance(first, int) else buf[:, first * P:(first + n) * P]

        def wait(eng, s, value):
            if not isinstance(value, int) or value > 0:
                eng.wait_ge(s, value)

        def qkv_copy(g, copy):
            b = (4 + g) % 8
            if g < 12:
                dst, t = (qT if g < 6 else kT), g % 2
                return copy(dst[:, (g % 6) // 2, HALF * t:HALF * t + HALF], ps[:, b, 0:HALF])
            return copy(vext[:, 2 * (g - 12):2 * (g - 12) + 2, :, 0:HD],
                        ps[0:TT, b, 0:2 * E].rearrange("p (a h d) -> p a h d", h=HEADS, d=HD))

        moved = nc.dram_tensor("moved", (TOK, E), F32).ap()
        W0_SPLIT = 10
        block = ctx.enter_context(nc.Block())

        @block.sync
        def _(sp):
            for h in range(2):
                sp.dma_start(x_sb[64 * h:64 * h + 64, :],
                             x[:, HALF_START * h:HALF_START * h + HALF_SAMPLES]).then_inc(x_in, 16)
            for t, src in ((w0, w0_rows), (pick_sb, pick_term), (shift_sb, shift), (id_f, ident), (id_b, ident_b)):
                sp.dma_start(t[:, :], src).then_inc(w0_in, 16)
            sp.dma_start(col[:, :], columns).then_inc(col_in, 16)
            sp.dma_start(cw[:, 0:EARLY_BLOCKS, :], conv_w[:, 0:EARLY_BLOCKS, :]).then_inc(cw_in, 16)
            sp.dma_start(cw[:, EARLY_BLOCKS:, :], conv_w[:, EARLY_BLOCKS:, :]).then_inc(cw2_in, 16)
            for t, src in ((proj_sb, proj), (proj_b_sb, proj_b)):
                sp.dma_start(t[:, :], src).then_inc(proj_in, 16)
            for pair, src in ((wq_sb, wq), (wk_sb, wk), (wv_sb, wv), (wo_sb, wo), (wr_sb, router)):
                sp.dma_start(pair[0][:, :], src[0:P, :]).then_inc(att_in, 16)
                sp.dma_start(pair[1][:, :], src[P:, :]).then_inc(att_in, 16)
            for t, src in ((clip_rows_sb, clip_rows), (clip_mask_sb, clip_mask), (head_rows_sb, head_rows), (rank_sb, rank)):
                sp.dma_start(t[:, :], src).then_inc(att_in, 16)
            for pair, src in ((wg_sb, gate), (wu_sb, up)):
                sp.dma_start(pair[0][:, :], src[0:P, :]).then_inc(ffn_in, 16)
                sp.dma_start(pair[1][:, :], src[P:, :]).then_inc(ffn_in, 16)
            sp.wait_ge(act_done, GROUPS)
            sp.dma_start(wd_sb, down).then_inc(down_in, 16)
            sp.wait_ge(h2_ready, NT // 2)
            sp.dma_start(moved.rearrange("(a p) e -> p a e", p=TT), h2).then_inc(h2_moved, 16)
            sp.wait_ge(h2_moved, 16)
            sp.dma_start(acc, moved.rearrange("(f p) e -> p f e", p=FT)).then_inc(h2_moved, 16)
            for k in range(NF // 2):
                sp.wait_ge(acc_done, NF * EXPERTS + 2 * (k + 1))
                sp.dma_start(out.rearrange("(f p) e -> p f e", p=FT)[:, 2 * k:2 * k + 2, :],
                             acc[:, 2 * k:2 * k + 2, :]).then_inc(stored, 16)
            sp.wait_ge(stored, 16 * (NF // 2))

        @block.tensor
        def _(pe):
            def chunk_turn(c, par):
                pe.wait_ge(staged, c + 1)
                wait(pe, quad_made, c)
                nc.tensor.transpose(chunk_ps[0:CHUNK_SAMPLES, 0:P], stage[:, par, :], id_f[:, :]).then_inc(stage_turned, 1)

            def chunk_gram(c):
                pe.wait_ge(stage_copied, c + 1)
                nc.tensor.matmul(chunk_ps[:, P:P + CHUNK * TAPS0], stageT[:, :], gband[:, :],
                                 start=True, stop=True).then_inc(gram_x, 1)

            def batch_turn(b, m, chunks):
                pe.wait_ge(split_step, SPLIT_STEPS * chunks)
                wait(pe, terms_copied, m)
                t0 = BATCH_T * (b % 5)
                for k in range(BATCH_T // 2):
                    last = nc.tensor.transpose(term_ps[:, P * k:P * k + P],
                                               terms[:, t0 + 2 * k:t0 + 2 * k + 2, :].rearrange("p t k -> p (t k)"), id_b[:, :])
                last.then_inc(terms_turned, 1)

            def batch_multiply(m):
                pe.wait_ge(terms_copied, m + 1)
                wait(pe, act0_done, m)
                nc.tensor.matmul(c0_ps[:, 0, :], w0_stack[0:64, :], termsT[0:64, :], start=True, stop=True)
                nc.tensor.matmul(c0_ps[:, 1, :], w0_stack[64:128, :], termsT[64:128, :],
                                 start=True, stop=True).then_inc(conv0_done, 1)

            def multiply(g):
                if g.batch is not None:
                    pe.wait_ge(act0_done, g.batch)
                for n in g.fed:
                    pe.wait_ge(act_done, n + 1)
                if g.bank_free is not None:
                    pe.wait_ge(norm_done, g.bank_free + 1)
                src, taps = acts[g.layer - 1], TAPS[g.layer]
                for t, first in enumerate(g.inputs):
                    for k in range(taps):
                        at = (first + k) % g.wrap if g.wrap else first + k
                        last = nc.tensor.matmul(prod[g.bank][:, P * t:P * t + P], src[:, P * at:P * at + P],
                                                cw[:, BLOCK0[g.layer] + k, :], start=(k == 0), stop=(k == taps - 1))
                last.then_inc(conv_done, 1)

            def turn_group(g):
                pe.wait_ge(norm_done, g.n + 1)
                wait(pe, act_done, g.n)
                for t in range(g.tiles):
                    last = nc.tensor.transpose(turn[:, P * t:P * t + P], yn[:, g.par, P * t:P * t + P], id_f[:, :])
                last.then_inc(turned, 1)

            def step(i, s, last):
                m = 5 * i + BATCH[s] if s in BATCH and not (last and BATCH[s] == 5) else None
                if m is not None:
                    b = BATCH[s]
                    batch_turn(b, m, 2 * i + (1 if b < 2 else 2 if b < 5 else 3))
                g = group(i, s)
                if g is not None:
                    multiply(g)
                    g2 = back(i, s, 2)
                    if g2 is not None:
                        turn_group(g2)
                if m is not None:
                    batch_multiply(m)
                if not last:
                    if s in CH_TURN:
                        chunk_turn(2 * i + CH_TURN[s], CH_TURN[s] % 2)
                    if s in CH_GRAM:
                        chunk_gram(2 * i + CH_GRAM[s])

            pe.wait_ge(w0_in, 5 * 16)
            pe.wait_ge(w0_step, 3)
            nc.tensor.transpose(chunk_ps[:, 0:TAPS0], w0[0:TAPS0, :], id_f[0:TAPS0, 0:TAPS0]).then_inc(w0_turned, 1)
            pe.wait_ge(gram_made, 1)
            nc.tensor.matmul(chunk_ps[0:TAPS0, 32:32 + TAPS0], w0T[:, :], w0T[:, :], start=True, stop=True).then_inc(w0_turned, 1)
            pe.wait_ge(gram_made, 2)
            for t in range(CHUNK):
                at = CHUNK_STEP - STRIDE0 - STRIDE0 * t
                last = nc.tensor.matmul(chunk_ps[0:CHUNK_SAMPLES, P + TAPS0 * t:P + TAPS0 * t + TAPS0],
                                        shift_sb[:, at:at + CHUNK_SAMPLES], gram[:, :], start=True, stop=True)
            last.then_inc(gband_made, 1)
            pe.wait_ge(gband_ready, 1)
            for c in range(2):
                chunk_turn(c, c)
                chunk_gram(c)
            pe.wait_ge(w0_step, W0_SPLIT)
            batch_turn(0, 0, 1)
            batch_multiply(0)
            pe.wait_ge(consts, CONSTS)
            pe.wait_ge(cw_ready, 1)
            for s in range(NS):
                step(0, s, False)
            with pe.Fori(1, ITERS - 1) as i:
                for s in range(NS):
                    step(i, s, False)
            for s in range(NS):
                step(ITERS - 1, s, True)
            pe.wait_ge(cw_ready, 2)
            turned_to = BEFORE_TAIL - 2
            every = [group(ITERS - 1, NS - 2), group(ITERS - 1, NS - 1)] + TAIL
            for k, g in enumerate(TAIL):
                while turned_to <= max(g.fed):
                    turn_group(every[turned_to - BEFORE_TAIL + 2])
                    turned_to += 1
                multiply(g)
                while turned_to <= g.n - 2:
                    turn_group(every[turned_to - BEFORE_TAIL + 2])
                    turned_to += 1
            while turned_to < GROUPS:
                turn_group(every[turned_to - BEFORE_TAIL + 2])
                turned_to += 1


            pe.wait_ge(act_done, GROUPS)
            for j in range(6):
                last = nc.tensor.transpose(ps[:, j // 4, P * (j % 4):P * (j % 4) + P], x6[:, P * j:P * j + P], id_f[:, :])
                if j in (3, 5):
                    last.then_inc(fln_turned, 1)
            pe.wait_ge(fln_norm, 1)
            for j in range(6):
                last = nc.tensor.transpose(ps[:, 2 + j // 4, P * (j % 4):P * (j % 4) + P],
                                           yn[:, j // 4, P * (j % 4):P * (j % 4) + P], id_f[:, :])
                if j in (3, 5):
                    last.then_inc(fln_back, 1)
            pe.wait_ge(fln_done, 2)
            pe.wait_ge(proj_in, 32)
            pe.wait_ge(tok_consts, TOK_CONSTS)
            for a in range(NT):
                o = ps[0:TT, 4 + a // 2, E * (a % 2):E * (a % 2) + E]
                nc.tensor.matmul(o, nT[:, TT * a:TT * a + TT], proj_sb[:, :], start=True, stop=False)
                last = nc.tensor.matmul(o, ones[:, :], proj_b_sb[:, :], start=False, stop=True)
                if a % 2:
                    last.then_inc(proj_done, 1)

            def turn_tokens(which):
                for t in range(2):
                    pe.wait_ge(ln_norm, NT * which + 4 * (t + 1))
                    for a in range(4 * t, 4 * t + 4):
                        at = TT * (a % 4)
                        nc.tensor.transpose(ps[:, t, at:at + TT], y[:, a, 0:P], id_f[0:TT, 0:TT])
                        last = nc.tensor.transpose(ps[0:E - P, 2 + t, at:at + TT], y[:, a, P:E], id_f[0:TT, 0:TT])
                    last.then_inc(ln_turned, 1)
            turn_tokens(0)
            pe.wait_ge(att_in, ATT_LOADS * 16)
            pe.wait_ge(yTa_ready, 2)
            pe.wait_ge(yTb_ready, 2)
            for g in range(QKV_GROUPS):
                o = ps[:, (4 + g) % 8, :]
                if g < 4:
                    pe.wait_ge(h1_ready, g + 1)
                if g >= 8:
                    pe.wait_ge(qkv_by_act if g % 2 == 0 else qkv_by_dve, (g - 8) // 2 + 1)
                if g < 12:
                    w, rows = (wq_sb, clip_rows_sb) if g < 6 else (wk_sb, clip_mask_sb)
                    c, t = (g % 6) // 2, g % 2
                    tok = slice(HALF * t, HALF * t + HALF)
                    nc.tensor.matmul(o[:, 0:HALF], w[0][:, P * c:P * c + P], yT_a[:, tok], start=True, stop=False)
                    nc.tensor.matmul(o[:, 0:HALF], w[1][:, P * c:P * c + P], yT_b[:, tok], start=False, stop=False)
                    last = nc.tensor.matmul(o[:, 0:HALF], head_rows_sb[:, :], rows[:, :], start=False, stop=True)
                else:
                    for a in (2 * (g - 12), 2 * (g - 12) + 1):
                        v = o[0:TT, E * (a % 2):E * (a % 2) + E]
                        nc.tensor.matmul(v, yT_a[:, TT * a:TT * a + TT], wv_sb[0][:, :], start=True, stop=False)
                        last = nc.tensor.matmul(v, yT_b[:, TT * a:TT * a + TT], wv_sb[1][:, :], start=False, stop=True)
                last.then_inc(qkv_done, 1)
            pe.wait_ge(qkv_by_act, QKV_GROUPS // 2)
            pe.wait_ge(qkv_by_dve, QKV_GROUPS // 2)
            for step_a in range(NT + 3):
                a = step_a
                if a < NT:
                    wait(pe, shifted, a)
                    tok = slice(TT * a, TT * a + TT)
                    for c in range(3):
                        for r in range(4):
                            last = nc.tensor.matmul(ps[0:TT, r, TT * c:TT * c + TT], qT[32 * r:32 * r + 32, c, tok],
                                                    kT[32 * r:32 * r + 32, c, tok], start=True, stop=True)
                    last.then_inc(scores_done, 1)
                a = step_a - 1
                if 0 <= a < NT:
                    pe.wait_ge(exp_done, a + 1)
                    wait(pe, att_copied, a)
                    for h in range(HEADS):
                        last = nc.tensor.transpose(ps[0:TT, 4 + h // 4, TT * (h % 4):TT * (h % 4) + TT],
                                                   att[:, a % 2, h, :], id_f[0:TT, 0:TT])
                    last.then_inc(att_turned, 1)
                a = step_a - 3
                if 0 <= a < NT:
                    pe.wait_ge(heads_done, a + 1)
                    nc.tensor.transpose(ps[:, 7, 256:256 + TT], heads_out[:, 0:P], id_f[0:TT, 0:TT])
                    nc.tensor.transpose(ps[0:E - P, 7, 256 + TT:256 + 2 * TT], heads_out[:, P:E],
                                        id_f[0:TT, 0:TT]).then_inc(heads_turned, 1)
                a = step_a - 2
                if 0 <= a < NT:
                    pe.wait_ge(att_copied, a + 1)
                    wait(pe, heads_copied, 2 * a)
                    for h in range(HEADS):
                        head = 4 * (h % 3) + h // 3
                        last = nc.tensor.matmul(ps[0:TT, 7, (HD + 1) * h:(HD + 1) * (h + 1)], attT[:, h, :],
                                                vext[:, a, head, :], start=True, stop=True)
                    last.then_inc(values_done, 1)
            pe.wait_ge(heads_copied, 2 * NT)
            for a in range(NT):
                o = ps[0:TT, a // 2, E * (a % 2):E * (a % 2) + E]
                nc.tensor.matmul(o, yT_a[:, TT * a:TT * a + TT], wo_sb[0][:, :], start=True, stop=False)
                last = nc.tensor.matmul(o, yT_b[:, TT * a:TT * a + TT], wo_sb[1][:, :], start=False, stop=True)
                if a % 2:
                    last.then_inc(out_done, 1)
            pe.wait_ge(h2_ready, NT // 2)
            turn_tokens(1)
            pe.wait_ge(yTa_ready, 4)
            pe.wait_ge(yTb_ready, 4)
            for f in range(NF):
                o = ps[:, 4, (EXPERTS + 1) * f:(EXPERTS + 1) * (f + 1)]
                nc.tensor.matmul(o, yT_a[:, FT * f:FT * f + FT], wr_sb[0][:, :], start=True, stop=False)
                last = nc.tensor.matmul(o, yT_b[:, FT * f:FT * f + FT], wr_sb[1][:, :], start=False, stop=True)
            last.then_inc(router_done, 1)
            pe.wait_ge(ffn_in, 64)
            pe.wait_ge(down_in, 16)

            def hidden_units(v):
                c, t = CHUNK_ORDER[v // 2], v % 2
                wait(pe, hid_ready, v - 1)
                tok = slice(HALF * t, HALF * t + HALF)
                for k, w in enumerate((wg_sb, wu_sb)):
                    o = ps[:, 2 * (v % 2) + k, 0:HALF]
                    nc.tensor.matmul(o, w[0][:, P * c:P * c + P], yT_a[:, tok], start=True, stop=False)
                    last = nc.tensor.matmul(o, w[1][:, P * c:P * c + P], yT_b[:, tok], start=False, stop=True)
                last.then_inc(hid_done, 1)

            def down_products(d):
                chunks, blocks, need = DOWN[d]
                pe.wait_ge(hid_ready, need)
                for f in range(NF):
                    if f % 2 == 0:
                        if d == 0:
                            pe.wait_ge(router_step, 1)
                        else:
                            pe.wait_ge(acc_done, NF * (d - 1) + f + 2)
                    o = ps[:, 4 + f // 2, E * (f % 2):E * (f % 2) + E]
                    for k, (c, b) in enumerate(zip(chunks, blocks)):
                        last = nc.tensor.matmul(o, hidden[:, c, FT * f:FT * f + FT], wd_sb[:, b, :],
                                                start=(k == 0), stop=(k == len(chunks) - 1))
                    if f % 2:
                        last.then_inc(down_done, 1)
            for kind, k in FFN_ORDER:
                (hidden_units if kind == "hidden" else down_products)(k)

        @block.scalar
        def _(act):
            def square(g):
                act.wait_ge(conv_done, g.n + 1)
                wait(act, var_done, g.n - 1)
                nc.scalar.activation(sq[:, g.par, 0:g.tiles * P], prod[g.bank][:, 0:g.tiles * P], ACT.Square,
                                     scale=P ** -0.5).then_inc(sq_done, 1)

            def gelu(g):
                act.wait_ge(turned, g.n + 1)
                for n in g.out_free:
                    act.wait_ge(conv_done, n + 1)
                nc.scalar.activation(tiles(acts[g.layer], g.out, g.tiles), turn[:, 0:g.tiles * P], ACT.Gelu,
                                     bias=col[:, 8 + g.layer:9 + g.layer], scale=col[:, g.layer:g.layer + 1]).then_inc(act_done, 1)

            def gelu0(b, m, free):
                act.wait_ge(conv0_done, m + 1)
                if free is not None:
                    act.wait_ge(conv_done, free + 1)
                t0 = BATCH_T * (b % 5)
                ring = early[:, t0 * P:(t0 + BATCH_T) * P].rearrange("p (k two l) -> p two k l", two=2, l=P)
                nc.scalar.activation(ring, c0_ps[:, :, :].rearrange("p two (k l) -> p two k l", l=P), ACT.Gelu,
                                     bias=col[:, 8:9], scale=col[:, 0:1]).then_inc(act0_done, 1)

            def step(i, s, last):
                g = group(i, s)
                if g is not None and (g1 := back(i, s, 1)) is not None:
                    square(g1)
                z = s - 1
                if z in BATCH and not (last and BATCH[z] == 5):
                    b = BATCH[z]
                    if b == 5:
                        free = number(i, C1_SLOT[1])
                    elif b == 4:
                        free = number(i, C1_SLOT[0])
                    else:
                        free = None if isinstance(i, int) and i == 0 else number_before(i, C1_SLOT[b + 1])
                    gelu0(b, 5 * i + b, free)
                if g is not None and (g3 := back(i, s, 3)) is not None:
                    gelu(g3)

            act.wait_ge(col_in, 16)
            act.wait_ge(consts, CONSTS)
            gelu0(0, 0, None)
            for s in range(NS):
                step(0, s, False)
            with act.Fori(1, ITERS - 1) as i:
                for s in range(NS):
                    step(i, s, False)
            for s in range(NS):
                step(ITERS - 1, s, True)
            squared, acted = BEFORE_TAIL - 1, BEFORE_TAIL - 3
            every = [group(ITERS - 1, NS - 3 + k) for k in range(3)] + TAIL
            for g in TAIL:
                while squared < g.n:
                    square(every[squared - BEFORE_TAIL + 3])
                    squared += 1
                while acted <= max(max(g.fed), g.n - 3):
                    gelu(every[acted - BEFORE_TAIL + 3])
                    acted += 1
            square(TAIL[-1])
            while acted < GROUPS:
                gelu(every[acted - BEFORE_TAIL + 3])
                acted += 1


            ordered = nT.rearrange("p (b h j) -> p j h b", h=2, j=6)
            for t, (a, b) in enumerate(((0, 4), (4, 6))):
                act.wait_ge(fln_back, t + 1)
                for j in range(a, b):
                    last = nc.scalar.activation(ordered[:, j, :, :],
                                                ps[:, 2 + t, P * (j - a):P * (j - a) + P].rearrange("p (h b) -> p h b", h=2),
                                                ACT.Identity, bias=col[:, 15:16], scale=col[:, 7:8])
                last.then_inc(fln_done, 1)
            for k in range(NT // 2):
                act.wait_ge(proj_done, k + 1)
                nc.scalar.activation(h1[:, 2 * k:2 * k + 2, :], ps[0:TT, 4 + k, 0:2 * E].rearrange("p (a e) -> p a e", e=E),
                                     ACT.Copy).then_inc(h1_ready, 1)

            def copy_tokens(which):
                for t in range(2):
                    act.wait_ge(ln_turned, 2 * which + t + 1)
                    nc.scalar.activation(yT_a[:, HALF * t:HALF * t + HALF], ps[:, t, 0:HALF], ACT.Copy).then_inc(yTa_ready, 1)
            copy_tokens(0)
            for g in range(0, QKV_GROUPS, 2):
                act.wait_ge(qkv_done, g + 1)
                qkv_copy(g, lambda o, i: nc.scalar.activation(o, i, ACT.Copy)).then_inc(qkv_by_act, 1)
            for step_a in range(NT + 3):
                a = step_a
                if a < NT:
                    act.wait_ge(shifted, a + 1)
                    nc.scalar.activation(att[:, a % 2, :, :], att[:, a % 2, :, :], ACT.Exp, scale=HD ** -0.5).then_inc(exp_done, 1)
                a = step_a - 3
                if 0 <= a < NT:
                    act.wait_ge(heads_turned, a + 1)
                    nc.scalar.activation(yT_a[:, TT * a:TT * a + TT], ps[:, 7, 256:256 + TT], ACT.Copy).then_inc(heads_copied, 1)
                    nc.scalar.activation(yT_b[0:E - P, TT * a:TT * a + TT], ps[0:E - P, 7, 256 + TT:256 + 2 * TT],
                                         ACT.Copy).then_inc(heads_copied, 1)
                a = step_a - 1
                if 0 <= a < NT:
                    act.wait_ge(att_turned, a + 1)
                    wait(act, values_done, a)
                    nc.scalar.activation(attT[:, :, :].rearrange("p (b h) k -> p b (h k)", b=3), ps[0:TT, 4:7, 0:4 * TT],
                                         ACT.Copy).then_inc(att_copied, 1)
            copy_tokens(1)
            act.wait_ge(router_step, 3)
            nc.scalar.activation(prob[:, :, :], prob[:, :, :], ACT.Exp).then_inc(router_exp, 1)
            nc.scalar.activation(small[:, 1, :], logits[:, :, EXPERTS], ACT.Exp, scale=-1.0).then_inc(router_exp, 1)
            for v in range(2 * HC):
                act.wait_ge(hid_done, v + 1)
                wait(act, hid_ready, v - 1)
                nc.scalar.activation(silu[:, v % 2, :], ps[:, 2 * (v % 2), 0:HALF], ACT.Silu).then_inc(silu_done, 1)

        @block.gpsimd
        def _(pool):
            def stage_chunk(c, par):
                wait(pool, split_step, SPLIT_STEPS * (c - 2) + 1)
                pool.tensor_copy(stage[:, par, :], x_sb[:, bass.ds(c * CHUNK_STEP, CHUNK_SAMPLES)]
                                 if not isinstance(c, int) else x_sb[:, c * CHUNK_STEP:c * CHUNK_STEP + CHUNK_SAMPLES]).then_inc(staged, 1)

            def rstd_chunk(c):
                pool.wait_ge(vare0_made, c + 1)
                wait(pool, split_step, SPLIT_STEPS * (c - 1) + 1)
                pool.tensor_tensor(rstd0[:, :], vare0[:, :], neg_half[:, :], ALU.pow).then_inc(rstd0_made, 1)

            def rstd_group(g):
                pool.wait_ge(var_done, g.n + 1)
                t = g.tiles
                pool.tensor_tensor(vare[:, g.par, 0:t], var[:, g.par, 0:t], eps[:, 0:t], ALU.add).then_inc(rstd_step, 1)
                pool.wait_ge(rstd_step, g.n + 1)
                wait(pool, norm_done, g.n - 1)
                pool.tensor_tensor(rstd[:, g.par, 0:t], vare[:, g.par, 0:t], neg_half[:, 0:t], ALU.pow).then_inc(rstd_done, 1)

            def step(i, s, last):
                if group(i, s) is not None and (g1 := back(i, s, 1)) is not None:
                    rstd_group(g1)
                if not last:
                    if s in CH_STAGE:
                        stage_chunk(2 * i + CH_STAGE[s], CH_STAGE[s] % 2)
                    if s in CH_QUAD:
                        rstd_chunk(2 * i + CH_QUAD[s])

            pool.memset(neg_half[:, :], -0.5).then_inc(consts, 1)
            pool.memset(eps[:, :], EPS).then_inc(consts, 1)
            pool.memset(terms[:, :, :], 0.0).then_inc(consts, 1)
            pool.memset(early[:, (RING0 - 2) * P:RING0 * P], 0.0).then_inc(consts, 1)
            pool.memset(x1[:, (RING1 - 1) * P:RING1 * P], 0.0).then_inc(consts, 1)
            pool.wait_ge(x_in, 32)
            pool.wait_ge(consts, CONSTS)
            stage_chunk(0, 0)
            stage_chunk(1, 1)
            rstd_chunk(0)
            rstd_chunk(1)
            for s in range(NS):
                step(0, s, False)
            with pool.Fori(1, ITERS - 1) as i:
                for s in range(NS):
                    step(i, s, False)
            for s in range(NS):
                step(ITERS - 1, s, True)
            for g in [group(ITERS - 1, NS - 1)] + TAIL:
                rstd_group(g)


            pool.wait_ge(act_done, GROUPS)
            pool.memset(ones[:, :], 1.0).then_inc(tok_consts, 1)
            pool.memset(yT_b[64:65, :], 1.0).then_inc(tok_consts, 1)
            pool.wait_ge(tok_consts, 2)
            pool.memset(vext, 1.0).then_inc(tok_consts, 1)

            def rstd_tokens(k, sem_in, at, rows, n):
                pool.wait_ge(sem_in, at)
                pool.tensor_scalar(vtok[0:rows, 0:n], mv[0:rows, 0:n, 1], 1.0, EPS, ALU.mult, ALU.add).then_inc(tok_var, 1)
                pool.wait_ge(tok_var, k + 1)
                pool.tensor_tensor(rtok[0:rows, 0:n], vtok[0:rows, 0:n], neg_half[0:rows, 0:n], ALU.pow).then_inc(tok_rstd, 1)
            rstd_tokens(0, fln_stats, 2, P, 6)
            rstd_tokens(1, ln_stats, 2, TT, NT)
            rstd_tokens(2, ln_stats, 4, TT, NT)

        @block.vector
        def _(dve):
            def copy_terms(m):
                dve.wait_ge(terms_turned, m + 1)
                wait(dve, conv0_done, m)
                nc.vector.tensor_copy(termsT[:, :], term_ps[:, 0:512]).then_inc(terms_copied, 1)

            def copy_stage(c):
                dve.wait_ge(stage_turned, c + 1)
                wait(dve, gram_x, c)
                nc.vector.tensor_copy(stageT[:, :], chunk_ps[0:CHUNK_SAMPLES, 0:P]).then_inc(stage_copied, 1)

            def quad_chunk(c, par):
                dve.wait_ge(gram_x, c + 1)
                wait(dve, vare0_made, c)
                nc.vector.tensor_tensor(quad[:, :, :], chunk_ps[:, P:P + CHUNK * TAPS0].rearrange("p (t k) -> p t k", k=TAPS0),
                                        window(par), ALU.mult).then_inc(quad_made, 1)
                dve.wait_ge(quad_made, c + 1)
                nc.vector.tensor_reduce(var0[:, :], quad[:, :, :], AX.X, ALU.add).then_inc(var0_made, 1)
                dve.wait_ge(var0_made, c + 1)
                wait(dve, rstd0_made, c)
                nc.vector.tensor_scalar(vare0[:, :], var0[:, :], 0.0, EPS, ALU.max, ALU.add).then_inc(vare0_made, 1)

            def split_chunk(c, par, used):
                dve.wait_ge(rstd0_made, c + 1)
                k = SPLIT_STEPS * c
                wait(dve, split_step, k)
                nc.vector.tensor_tensor(xs[:, :, :], window(par), rstd0[:, :].unsqueeze(2).to_broadcast([P, CHUNK, TAPS0]),
                                        ALU.mult).then_inc(split_step, 1)
                dve.wait_ge(split_step, k + 1)
                if used is not None:
                    dve.wait_ge(terms_turned, used)
                t = terms[:, CHUNK * par:CHUNK * par + CHUNK, :]

                def section(a, n):
                    return t[:, :, TAPS0 * a:TAPS0 * (a + n)].rearrange("p t (s k) -> p t s k", k=TAPS0)

                def again(v, n):
                    return v[:, :, :].unsqueeze(2).to_broadcast([P, CHUNK, n, TAPS0])
                nc.vector.tensor_copy(section(0, 3), again(xs, 3)).then_inc(split_step, 1)
                dve.wait_ge(split_step, k + 2)
                nc.vector.tensor_tensor(xrest[:, :, :], xs[:, :, :], t[:, :, 0:TAPS0], ALU.subtract).then_inc(split_step, 1)
                dve.wait_ge(split_step, k + 3)
                nc.vector.tensor_copy(section(3, 2), again(xrest, 2)).then_inc(split_step, 1)
                dve.wait_ge(split_step, k + 4)
                nc.vector.tensor_tensor(t[:, :, 5 * TAPS0:6 * TAPS0], xrest[:, :, :], t[:, :, 3 * TAPS0:4 * TAPS0],
                                        ALU.subtract).then_inc(split_step, 1)

            def sum_group(g):
                dve.wait_ge(sq_done, g.n + 1)
                wait(dve, rstd_step, g.n - 1)
                nc.vector.tensor_reduce(var[:, g.par, 0:g.tiles], sq[:, g.par, 0:g.tiles * P].rearrange("p (t c) -> p t c", c=P),
                                        AX.X, ALU.add).then_inc(var_done, 1)

            def norm_group(g):
                dve.wait_ge(rstd_done, g.n + 1)
                wait(dve, turned, g.n - 1)
                t = g.tiles
                nc.vector.tensor_tensor(yn[:, g.par, 0:t * P].rearrange("p (t c) -> p t c", c=P),
                                        prod[g.bank][:, 0:t * P].rearrange("p (t c) -> p t c", c=P),
                                        rstd[:, g.par, 0:t].unsqueeze(2).to_broadcast([P, t, P]), ALU.mult).then_inc(norm_done, 1)

            def step(i, s, last):
                if s in BATCH and not (last and BATCH[s] == 5):
                    copy_terms(5 * i + BATCH[s])
                g = group(i, s)
                g1 = back(i, s, 1) if g is not None else None
                if g1 is not None:
                    sum_group(g1)
                if not last:
                    if s in CH_COPY:
                        copy_stage(2 * i + CH_COPY[s])
                    if s in CH_QUAD:
                        quad_chunk(2 * i + CH_QUAD[s], CH_QUAD[s] % 2)
                if g1 is not None:
                    norm_group(g1)
                if not last and s in CH_SPLIT:
                    c = CH_SPLIT[s]
                    split_chunk(2 * i + c, c % 2, 5 * i + (3 if c == 2 else 5))

            dve.wait_ge(w0_in, 5 * 16)
            done = [0]

            def w0_next(ins):
                done[0] += 1
                ins.then_inc(w0_step, 1)
                dve.wait_ge(w0_step, done[0])
            w0_next(nc.vector.tensor_reduce(w0mean[:, :], w0[:, :], AX.X, ALU.add))
            w0_next(nc.vector.tensor_scalar(w0mean[:, :], w0mean[:, :], -1.0 / P, None, ALU.mult))
            w0_next(nc.vector.tensor_scalar(w0[:, :], w0[:, :], w0mean[:, 0:1], None, ALU.add))
            dve.wait_ge(w0_turned, 1)
            nc.vector.tensor_copy(w0T[:, :], chunk_ps[:, 0:TAPS0]).then_inc(gram_made, 1)
            dve.wait_ge(w0_turned, 2)
            nc.vector.tensor_scalar(gram[:, :], chunk_ps[0:TAPS0, 32:32 + TAPS0], 1.0 / P, None, ALU.mult).then_inc(gram_made, 1)
            dve.wait_ge(gband_made, 1)
            nc.vector.tensor_copy(gband[:, :], chunk_ps[0:CHUNK_SAMPLES, P:P + CHUNK * TAPS0]).then_inc(gband_ready, 1)
            w0_next(nc.vector.tensor_copy(w0term[:, 0, :], w0[:, :]))
            w0_next(nc.vector.tensor_tensor(w0rest[:, :], w0[:, :], w0term[:, 0, :], ALU.subtract))
            w0_next(nc.vector.tensor_copy(w0term[:, 1, :], w0rest[:, :]))
            w0_next(nc.vector.tensor_tensor(w0term[:, 2, :], w0rest[:, :], w0term[:, 1, :], ALU.subtract))
            w0_next(nc.vector.tensor_scalar(w0_stack[:, :], w0term[:, 0, :], pick_sb[:, 0:1], None, ALU.mult))
            for k in (1, 2):
                w0_next(nc.vector.scalar_tensor_tensor(w0_stack[:, :], w0term[:, k, :], pick_sb[:, k:k + 1], w0_stack[:, :],
                                                       ALU.mult, ALU.add))
            assert done[0] == W0_SPLIT
            copy_stage(0)
            quad_chunk(0, 0)
            copy_stage(1)
            quad_chunk(1, 1)
            dve.wait_ge(consts, CONSTS)
            split_chunk(0, 0, None)
            split_chunk(1, 1, None)
            copy_terms(0)

            def centre(a, b, base):
                nc.vector.tensor_reduce(cmean[:, a:b], cw[:, a:b, :], AX.X, ALU.add).then_inc(cmean_step, 1)
                dve.wait_ge(cmean_step, base + 1)
                nc.vector.tensor_scalar(cmean[:, a:b], cmean[:, a:b], -1.0 / P, None, ALU.mult).then_inc(cmean_step, 1)
                dve.wait_ge(cmean_step, base + 2)
                for k in range(a, b):
                    last = nc.vector.tensor_scalar(cw[:, k, :], cw[:, k, :], cmean[:, k:k + 1], None, ALU.add)
                last.then_inc(cw_ready, 1)
            dve.wait_ge(cw_in, 16)
            centre(0, EARLY_BLOCKS, 0)
            for s in range(NS):
                step(0, s, False)
            dve.wait_ge(cw2_in, 16)
            centre(EARLY_BLOCKS, BLOCKS, 2)
            with dve.Fori(1, ITERS - 1) as i:
                for s in range(NS):
                    step(i, s, False)
            for s in range(NS):
                step(ITERS - 1, s, True)
            for g in [group(ITERS - 1, NS - 1)] + TAIL:
                sum_group(g)
                norm_group(g)

            for j in range(6):
                if j in (0, 4):
                    dve.wait_ge(fln_turned, 1 + j // 4)
                last = nc.vector.bn_stats(stat[:, j, :], ps[:, j // 4, P * (j % 4):P * (j % 4) + P])
            last.then_inc(fln_stats, 1)
            dve.wait_ge(fln_stats, 1)
            for j in range(6):
                last = nc.vector.bn_aggr(mv[:, j, :], stat[:, j, :])
            last.then_inc(fln_stats, 1)
            dve.wait_ge(tok_rstd, 1)
            for j in range(6):
                last = nc.vector.tensor_scalar(yn[:, j // 4, P * (j % 4):P * (j % 4) + P],
                                               ps[:, j // 4, P * (j % 4):P * (j % 4) + P], mv[:, j, 0:1], rtok[:, j:j + 1],
                                               ALU.subtract, ALU.mult)
            last.then_inc(fln_norm, 1)

            def norm_tokens(which, h, ready):
                for a in range(NT):
                    if a % 2 == 0:
                        dve.wait_ge(ready, a // 2 + 1)
                    last = nc.vector.bn_stats(stat[0:TT, a, :], h[:, a, :])
                last.then_inc(ln_stats, 1)
                dve.wait_ge(ln_stats, 2 * which + 1)
                for a in range(NT):
                    last = nc.vector.bn_aggr(mv[0:TT, a, :], stat[0:TT, a, :])
                last.then_inc(ln_stats, 1)
                dve.wait_ge(tok_rstd, which + 2)
                for a in range(NT):
                    nc.vector.tensor_scalar(y[:, a, :], h[:, a, :], mv[0:TT, a, 0:1], rtok[0:TT, a:a + 1],
                                            ALU.subtract, ALU.mult).then_inc(ln_norm, 1)
                for t in range(2):
                    dve.wait_ge(ln_turned, 2 * which + t + 1)
                    nc.vector.tensor_copy(yT_b[0:E - P, HALF * t:HALF * t + HALF], ps[0:E - P, 2 + t, 0:HALF]).then_inc(yTb_ready, 1)
            norm_tokens(0, h1, h1_ready)
            dve.wait_ge(tok_consts, TOK_CONSTS)
            for g in range(1, QKV_GROUPS, 2):
                dve.wait_ge(qkv_done, g + 1)
                qkv_copy(g, nc.vector.tensor_copy).then_inc(qkv_by_dve, 1)
            for step_a in range(NT + 2):
                a = step_a
                if a < NT:
                    dve.wait_ge(scores_done, a + 1)
                    s4 = ps[0:TT, 0:4, 0:3 * TT].rearrange("p r (c k) -> p r c k", k=TT)
                    t4 = top[:, :].rearrange("p (r c) -> p r c", c=3)
                    wait(dve, shifted, a)
                    nc.vector.tensor_reduce(t4, s4, AX.X, ALU.max).then_inc(top_done, 1)
                    dve.wait_ge(top_done, a + 1)
                    wait(dve, att_turned, a - 1)
                    nc.vector.tensor_tensor(att[:, a % 2, :, :].rearrange("p (r c) k -> p r c k", c=3), s4,
                                            t4.unsqueeze(3).to_broadcast([TT, 4, 3, TT]), ALU.subtract).then_inc(shifted, 1)
                a = step_a - 2
                if 0 <= a < NT:
                    dve.wait_ge(values_done, a + 1)
                    o = ps[0:TT, 7, 0:HEADS * (HD + 1)].rearrange("p (h d) -> p h d", d=HD + 1)
                    wait(dve, heads_done, a)
                    nc.vector.reciprocal(rsum[:, :], o[:, :, HD]).then_inc(rsum_done, 1)
                    dve.wait_ge(rsum_done, a + 1)
                    wait(dve, heads_turned, a)
                    nc.vector.tensor_tensor(heads_out[:, :].rearrange("p (c r d) -> p r c d", r=4, d=HD),
                                            o[:, :, 0:HD].rearrange("p (r c) d -> p r c d", c=3),
                                            rsum[:, :].rearrange("p (r c) -> p r c", c=3).unsqueeze(3).to_broadcast([TT, 4, 3, HD]),
                                            ALU.mult).then_inc(heads_done, 1)
            for k in range(NT // 2):
                dve.wait_ge(out_done, k + 1)
                nc.vector.tensor_tensor(h2[:, 2 * k:2 * k + 2, :], ps[0:TT, k, 0:2 * E].rearrange("p (a e) -> p a e", e=E),
                                        h1[:, 2 * k:2 * k + 2, :], ALU.add).then_inc(h2_ready, 1)
            norm_tokens(1, h2, h2_ready)

            steps = [0]

            def router_next(ins):
                steps[0] += 1
                ins.then_inc(router_step, 1)
                dve.wait_ge(router_step, steps[0])

            def wide(v):
                return v.unsqueeze(2).to_broadcast([P, NF, EXPERTS])
            ranks = rank_sb[:, :].rearrange("p (f e) -> p f e", e=EXPERTS)
            best, alpha, m1, k1, m2, k2, rest = (small[:, k, :] for k in (0, 1, 2, 3, 4, 5, 6))
            dve.wait_ge(router_done, 1)
            router_next(nc.vector.tensor_copy(logits[:, :, :], ps[:, 4, 0:NF * (EXPERTS + 1)].rearrange("p (f e) -> p f e", e=EXPERTS + 1)))
            router_next(nc.vector.tensor_reduce(best, logits[:, :, 0:EXPERTS], AX.X, ALU.max))
            router_next(nc.vector.tensor_tensor(prob[:, :, :], logits[:, :, 0:EXPERTS], wide(best), ALU.subtract))
            dve.wait_ge(router_exp, 2)
            router_next(nc.vector.tensor_scalar(alpha, alpha, 1.0, None, ALU.add))
            router_next(nc.vector.reciprocal(alpha, alpha))
            for value, k, chosen, left in ((m1, k1, first, prob), (m2, k2, second, key)):
                router_next(nc.vector.tensor_reduce(value, left[:, :, :], AX.X, ALU.max))
                router_next(nc.vector.tensor_tensor(chosen[:, :, :], left[:, :, :], wide(value), ALU.is_ge))
                router_next(nc.vector.tensor_tensor(chosen[:, :, :], chosen[:, :, :], ranks, ALU.mult))
                router_next(nc.vector.tensor_reduce(k, chosen[:, :, :], AX.X, ALU.max))
                router_next(nc.vector.tensor_tensor(chosen[:, :, :], chosen[:, :, :], wide(k), ALU.is_equal))
                if chosen is first:
                    router_next(nc.vector.scalar_tensor_tensor(key[:, :, :], first[:, :, :], -2.0, prob[:, :, :], ALU.mult, ALU.add))
            router_next(nc.vector.tensor_tensor(rest, m1, m2, ALU.add))
            router_next(nc.vector.reciprocal(rest, rest))
            router_next(nc.vector.tensor_scalar(best, alpha, -1.0, 1.0, ALU.mult, ALU.add))
            router_next(nc.vector.tensor_tensor(rest, rest, best, ALU.mult))
            router_next(nc.vector.tensor_tensor(first[:, :, :], first[:, :, :], second[:, :, :], ALU.add))
            router_next(nc.vector.tensor_tensor(gates[:, :, :], first[:, :, :], prob[:, :, :], ALU.mult))
            router_next(nc.vector.tensor_tensor(gates[:, :, :], gates[:, :, :], wide(rest), ALU.mult))

            def gate_units(v):
                c, t = CHUNK_ORDER[v // 2], v % 2
                dve.wait_ge(silu_done, v + 1)
                nc.vector.tensor_tensor(hidden[:, c, HALF * t:HALF * t + HALF], ps[:, 2 * (v % 2) + 1, 0:HALF], silu[:, v % 2, :],
                                        ALU.mult).then_inc(hid_ready, 1)

            def add_down(d):
                for f in range(NF):
                    if f % 2 == 0:
                        dve.wait_ge(down_done, NF // 2 * d + f // 2 + 1)
                    if d == 0:
                        dve.wait_ge(h2_moved, 32)
                        weight = small[:, 1, f:f + 1]
                    else:
                        dve.wait_ge(acc_done, NF * (d - 1) + f + 1)
                        weight = gates[:, f, d - 1:d]
                    nc.vector.scalar_tensor_tensor(acc[:, f, :], ps[:, 4 + f // 2, E * (f % 2):E * (f % 2) + E], weight, acc[:, f, :],
                                                   ALU.mult, ALU.add).then_inc(acc_done, 1)
            for kind, k in FFN_ORDER:
                (gate_units if kind == "hidden" else add_down)(k)


def layout(a):
    f, b16 = np.float32, mybir.dt.np(BF16)
    w0 = a["L0_tok_conv_w0"][:, 0, :].T
    rows, pick = np.zeros((P, P), f), np.zeros((P, 3), f)
    for side in (0, 64):
        for section, term in enumerate((0, 1, 2, 0, 1, 0)):
            at = side + TAPS0 * section
            rows[at:at + TAPS0] = w0
            pick[at:at + TAPS0, term] = 1
    shift = np.zeros((TAPS0, 2 * CHUNK_STEP), f)
    shift[:, CHUNK_STEP - STRIDE0:CHUNK_STEP - STRIDE0 + TAPS0] = np.eye(TAPS0, dtype=f)
    names = [f"ln_g{k}" for k in range(7)] + ["fln_g"] + [f"ln_b{k}" for k in range(7)] + ["fln_b"]

    def with_bias(w, bias):
        return np.concatenate([w, bias[None, :]])

    def by_head(w):
        out = np.zeros((w.shape[0], HEADS, 32), f)
        out[:, :, 0:HD] = w.reshape(w.shape[0], HEADS, HD)
        return out.reshape(w.shape[0], HEADS * 32)

    def beside(w, shared):
        w = np.concatenate([w.transpose(1, 0, 2).reshape(E, EXPERTS * E), shared], axis=1)
        return np.concatenate([w, np.zeros((1, w.shape[1]), f)])

    router = np.concatenate([a["L0_ffn_router_w"], a["L0_ffn_sg_w"]], axis=1)
    router_bias = np.concatenate([np.zeros(EXPERTS, f), a["L0_ffn_sg_b"]])
    down = np.zeros((P, DOWN_BLOCKS, E), f)
    routed = a["L0_ffn_w_down"].reshape(ROUTED_HC, P, E)
    for pair in range(EXPERTS // 2):
        down[:, 4 * pair] = routed[3 * pair]
        down[0:64, 4 * pair + 1] = routed[3 * pair + 1, 0:64]
        down[64:, 4 * pair + 2] = routed[3 * pair + 1, 64:]
        down[:, 4 * pair + 3] = routed[3 * pair + 2]
    down[:, 4 * (EXPERTS // 2):] = a["L0_ffn_ws_down"].reshape(HC - ROUTED_HC, P, E).transpose(1, 0, 2)
    clip = np.arange(HALF) // FRAMES % 8
    same = clip[None, :] == np.arange(8)[:, None]
    head_rows = np.zeros((8, P), b16)
    for r in range(4):
        head_rows[np.arange(8), 32 * r + HD + np.arange(8)] = 1
    return {
        "x": a["x"],
        "conv_w": np.concatenate([a[f"L0_tok_conv_w{k}"].transpose(1, 2, 0) for k in range(1, 7)], axis=1),
        "w0_rows": rows, "pick_term": pick, "shift": shift,
        "columns": np.stack([a[f"L0_tok_{n}"] for n in names], axis=1),
        "ident": np.eye(P, dtype=f), "ident_b": np.eye(P, dtype=b16),
        "proj": a["L0_tok_proj_w"], "proj_b": a["L0_tok_proj_b"][None, :],
        "wq": by_head(with_bias(a["L0_attn_Wq"].T, a["L0_attn_bq"])),
        "wk": by_head(with_bias(a["L0_attn_Wk"].T, a["L0_attn_bk"])),
        "wv": with_bias(a["L0_attn_Wv"].T, a["L0_attn_bv"]),
        "wo": with_bias(a["L0_attn_Wo"].T, a["L0_attn_bo"]),
        "router": with_bias(router, router_bias),
        "gate": beside(a["L0_ffn_w_gate"], a["L0_ffn_ws_gate"]),
        "up": beside(a["L0_ffn_w_up"], a["L0_ffn_ws_up"]),
        "down": down,
        "clip_rows": same.astype(b16), "clip_mask": np.where(same, 0.0, -2.0 ** 100).astype(b16),
        "head_rows": head_rows,
        "rank": np.tile(np.arange(EXPERTS, 0, -1, dtype=f), (P, NF)),
    }


def kernel(**inputs):
    import concourse.bacc as bacc
    from concourse.bass_utils import run_bass_kernel_spmd as run
    arrays = {k: np.ascontiguousarray(v) for k, v in layout({k: np.asarray(v) for k, v in inputs.items()}).items()}
    nc = bacc.Bacc("TRN2", target_bir_lowering=False, num_devices=1)
    ins = {k: nc.dram_tensor(f"in_{k}", v.shape, mybir.dt.from_np(v.dtype), kind="ExternalInput").ap()
           for k, v in arrays.items()}
    out = nc.dram_tensor("out", (TOK, E), F32, kind="ExternalOutput").ap()
    audio_tower(nc, **ins, out=out)
    r = run(nc, [{f"in_{k}": v for k, v in arrays.items()}], core_ids=[0])
    return r.results[0]["out"].reshape(CLIPS, FRAMES, E)
```

```python
from contextlib import ExitStack
from typing import NamedTuple

import concourse.bass as bass
import numpy as np
from concourse import mybir

F32 = mybir.dt.float32
BF16 = mybir.dt.bfloat16
ALU = mybir.AluOpType
ACT = mybir.ActivationFunctionType
AX = mybir.AxisListType

P = 128
CLIPS, SAMPLES, FRAMES = 64, 4000, 12
TAPS0, STRIDE0 = 10, 5
HALF_START = 1920
HALF_SAMPLES = 2005
FIRST_SAMPLES = 205
CHUNK = 20
CHUNK_SAMPLES = STRIDE0 * (CHUNK - 1) + TAPS0
CHUNK_STEP = STRIDE0 * CHUNK
SHIFT_AT = (CHUNK // 6) * 6 * STRIDE0
ITERS = 10
RING0, RING1, STEP2 = 40, 20, 10
BATCH_T = 8
TAPS = {1: 3, 2: 3, 3: 3, 4: 3, 5: 2, 6: 2}
TILES = {3: 49, 4: 24, 5: 12, 6: 6}
BLOCK0 = {1: 0, 2: 3, 3: 6, 4: 9, 5: 12, 6: 14}
BLOCKS, EARLY_BLOCKS = 16, 6
EPS = 1e-5
E, HEADS, HD = 192, 12, 16
TOK = CLIPS * FRAMES
CLIPS_T = 8
TT, NT = 96, 8
MASK = -2.0 ** 100
T_ROWS = E - P + 1 + CLIPS_T
AT_OUT = 3 * TT
FT, NF = 128, 6
HALF = TOK // 2
EXPERTS = 8
HC, ROUTED_HC = 18, 12

SLOTS = [(1, 0, 4, 0), (2, 4, 4, 1), (1, 4, 4, 0), (2, 8, 2, 1),
         (1, 8, 4, 0), (1, 12, 4, 0), (2, 0, 4, 0), (1, 16, 4, 0)]
NS = len(SLOTS)
C1_SLOT = [0, 2, 4, 5, 7]
C2_FIRST, C2_MID, C2_LAST = 6, 1, 3
BANKS = 4
BATCH = {0: 1, 2: 2, 3: 3, 5: 4, 6: 5}
FIRST_SLOTS = [s for s in range(NS) if SLOTS[s][3] == 0]
CH_STAGE, CH_GRAM, CH_QUAD, CH_SPLIT = {0: 2, 3: 3}, {1: 2, 4: 3}, {2: 2, 5: 3}, {5: 2, 7: 3}
CH_RSTD = {2: (2, 0), 4: (2, 1), 5: (3, 0), 6: (3, 1)}
SPLIT_STEPS = 5
CONSTS = 5
SECTIONS = 6
GROW = SECTIONS * TAPS0

ATT_LOADS = 11
QKV_GROUPS = 16

CHUNK_ORDER = list(range(ROUTED_HC, HC)) + list(range(ROUTED_HC))
DOWN_BLOCKS = ROUTED_HC // 3 * 4 + HC - ROUTED_HC
DOWN = [(list(range(ROUTED_HC, HC)), list(range(DOWN_BLOCKS - (HC - ROUTED_HC), DOWN_BLOCKS)), 2 * (HC - ROUTED_HC))]
for _e in range(EXPERTS):
    _c, _b = 3 * (_e // 2) + _e % 2, 4 * (_e // 2) + 2 * (_e % 2)
    DOWN.append(([_c, _c + 1], [_b, _b + 1], 2 * (HC - ROUTED_HC) + 2 * (_c + 2)))


def ffn_order():
    out, down = [], 0
    for v in range(2 * HC):
        out.append(("hidden", v))
        if down < len(DOWN) and DOWN[down][2] + 1 <= v:
            out.append(("down", down))
            down += 1
    return out + [("down", d) for d in range(down, len(DOWN))]


FFN_ORDER = ffn_order()


def number(i, s):
    if isinstance(i, int) and i == 0:
        return FIRST_SLOTS.index(s)
    return i * NS + (s - (NS - len(FIRST_SLOTS)))


class Group(NamedTuple):
    n: object
    layer: int
    inputs: list
    wrap: int
    out: object
    tiles: int
    bank: int
    par: int
    fed: tuple
    bank_free: object
    out_free: tuple
    batch: object


def group(i, s):
    first = isinstance(i, int) and i == 0
    if first and s not in FIRST_SLOTS:
        return None
    layer, t0, tiles, back = SLOTS[s]
    n = number(i, s)
    used = n - BANKS
    if first:
        used = n - BANKS if n >= BANKS else None
    at = n if first else s + len(FIRST_SLOTS)
    par, bank = at % 2, at % BANKS
    if layer == 1:
        q = t0 // 4
        inputs = [(2 * t - 2) % RING0 for t in range(t0, t0 + 4)]
        if q == 4:
            free = (number(i, C2_FIRST),)
        elif first:
            free = ()
        else:
            free = (number_before(i, C2_FIRST) if q == 0 else number(i, C2_MID if q < 3 else C2_LAST),)
        return Group(n, 1, inputs, RING0, t0, tiles, bank, par, (), used, free, 5 * i + q + 1)
    inputs = [(2 * m - 1) % RING1 for m in range(t0, t0 + tiles)]
    q = (2 * (t0 + tiles - 1) + 1) // 4
    fed = number(i, C1_SLOT[q]) if back == 0 else number_before(i, C1_SLOT[q])
    return Group(n, 2, inputs, RING1, (i - back) * STEP2 + t0, tiles, bank, par, (fed,), used, (), None)


def number_before(i, s):
    if isinstance(i, int):
        return number(i - 1, s)
    return i * NS + (s - (NS - len(FIRST_SLOTS)) - NS)


BEFORE_TAIL = len(FIRST_SLOTS) + NS * (ITERS - 1)


def tail():
    late = 4
    todo = [(2, 4, 4), (2, 8, 2)] + [(k, t, min(4, TILES[k] - t)) for k in (3, 4, 5, 6)
                                     for t in range(0, TILES[k], 4)]
    made = {}
    for it in range(ITERS):
        for m in range(STEP2):
            s = C2_FIRST if m < 4 else (C2_MID if m < 8 else C2_LAST)
            if s == C2_FIRST or it < ITERS - 1:
                made[2, STEP2 * it + m] = number(it if s == C2_FIRST else it + 1, s)
    order = []
    while todo:
        best = None
        for k, (layer, t, tiles) in enumerate(todo):
            if any(z[0] == layer for z in todo[:k]):
                continue
            if layer == 2:
                need = number(ITERS - 1, C1_SLOT[3 if t == 4 else 4])
            else:
                top = 2 * (t + tiles - 1) + TAPS[layer] - 1 + (layer == 3)
                need = made.get((layer - 1, top))
            if need is None:
                continue
            age = BEFORE_TAIL + len(order) - need
            rank = (age >= late, layer if age >= late else age)
            if best is None or rank > best[0]:
                best = (rank, k, need)
        _, k, need = best
        layer, t, tiles = todo.pop(k)
        n = BEFORE_TAIL + len(order)
        base = STEP2 * (ITERS - 1) if layer == 2 else 0
        if layer == 2:
            inputs = [(2 * m - 1) % RING1 for m in range(t, t + tiles)]
        else:
            inputs = [2 * m + (layer == 3) for m in range(t, t + tiles)]
        order.append(Group(n, layer, inputs, RING1 if layer == 2 else 0, base + t, tiles,
                           n % BANKS, n % 2, (need,), n - BANKS, (), None))
        for m in range(tiles):
            made[layer, base + t + m] = n
    return order


TAIL = tail()
GROUPS = BEFORE_TAIL + len(TAIL)


def back(i, s, d):
    if isinstance(i, int) and i == 0:
        at = FIRST_SLOTS.index(s) - d
        return group(0, FIRST_SLOTS[at]) if at >= 0 else None
    z = (s - d) % NS
    if z <= s:
        return group(i, z)
    if isinstance(i, int):
        return group(i - 1, z)
    g = group(i, z)
    less = lambda v: None if v is None else v - NS
    return g._replace(n=number_before(i, z), fed=tuple(map(less, g.fed)), bank_free=less(g.bank_free),
                      out_free=tuple(map(less, g.out_free)),
                      out=g.out - STEP2 if g.layer == 2 else g.out)


def audio_tower(nc: bass.Bass, x, conv_w, w0_rows, pick_term, diagonal, shift, columns, ident, ident_b, proj, proj_b, wq, wk, wv, wo,
                router, gate, up, down, token_rows, rank, out):
    with ExitStack() as ctx:
        def sb(name, shape, dt=F32):
            return ctx.enter_context(nc.sbuf_tensor(name, shape, dt))

        def sem(name):
            return ctx.enter_context(nc.semaphore(name))

        shared = sb("shared", [P, DOWN_BLOCKS * E])
        wd_sb = shared[:, :].rearrange("p (b e) -> p b e", e=E)
        cw = shared[:, 0:BLOCKS * P].rearrange("p (k c) -> p k c", c=P)
        x_sb = shared[:, BLOCKS * P:BLOCKS * P + HALF_SAMPLES]
        cmean = sb("cmean", [P, BLOCKS])
        w0 = sb("w0", [P, P])
        w0mean = sb("w0mean", [P, 1])
        w0rest = sb("w0rest", [P, P])
        w0term = sb("w0term", [P, 3, P], BF16)
        w0_stack = sb("w0_stack", [P, P], BF16)
        pick_sb = sb("pick_sb", [P, 3])
        w0T = sb("w0T", [P, GROW])
        diagonal_sb = sb("diagonal_sb", [GROW, GROW])
        gram = sb("gram", [GROW, GROW])
        shift_sb = sb("shift_sb", [GROW, SHIFT_AT + CHUNK_SAMPLES])
        table_warm = sb("table_warm", [P, 1])
        gband = sb("gband", [CHUNK_SAMPLES, CHUNK * TAPS0])
        col = sb("col", [P, 16])
        id_f = sb("id_f", [P, P])
        id_b = sb("id_b", [P, P], BF16)
        neg_half, eps = sb("neg_half", [P, CHUNK]), sb("eps", [P, 4])
        stage = sb("stage", [P, 2, CHUNK_SAMPLES])
        stageT = sb("stageT", [CHUNK_SAMPLES, P])
        quad = sb("quad", [P, CHUNK, TAPS0])
        var0 = sb("var0", [P, CHUNK])
        vare0 = sb("vare0", [P, CHUNK])
        rstd0 = sb("rstd0", [P, CHUNK])
        xs = sb("xs", [P, CHUNK, TAPS0])
        xrest = sb("xrest", [P, CHUNK, TAPS0])
        terms = sb("terms", [P, RING0, 64], BF16)
        termsT = sb("termsT", [P, 512], BF16)
        sq = sb("sq", [P, 2, 512])
        var = sb("var", [P, 2, 4])
        vare = sb("vare", [P, 2, 4])
        rstd = sb("rstd", [P, 2, 4])
        yn = sb("yn", [P, 2, 512])
        early = sb("early", [P, RING0 * P])
        x1 = sb("x1", [P, RING1 * P])
        x2 = sb("x2", [P, HC * TOK])
        x3 = sb("x3", [P, TILES[3] * P])
        x6 = sb("x6", [P, TILES[6] * P])
        acts = {0: early, 1: x1, 2: x2, 3: x3, 4: early[:, 0:TILES[4] * P],
                5: early[:, TILES[4] * P:(TILES[4] + TILES[5]) * P], 6: x6}

        proj_sb, proj_b_sb = sb("proj_sb", [P, E]), sb("proj_b_sb", [TT, E])
        wo_sb = sb("wo_sb", [P, 3, E])
        wq_sb, wk_sb, wv_sb, wr_sb, wg_sb, wu_sb = (
            (sb(n + "_a", [P, w]), sb(n + "_b", [T_ROWS if n in ("wq", "wk") else E - P + 1, w])) for n, w in
            (("wq", 3 * P), ("wk", 3 * P), ("wv", E), ("wr", EXPERTS + 1), ("wg", HC * P), ("wu", HC * P)))
        rank_sb = sb("rank_sb", [P, NF * EXPERTS])
        stat, mv = sb("stat", [P, NT, 6]), sb("mv", [P, NT, 2])
        vtok, rtok = sb("vtok", [P, NT]), sb("rtok", [P, NT])
        nT = x3[:, 0:TOK]
        h1, h2, y = (x3[0:TT, TOK + k * NT * E:TOK + (k + 1) * NT * E].rearrange("p (a e) -> p a e", e=E) for k in range(3))
        acc = early[:, 0:NF * E].rearrange("p (f e) -> p f e", e=E)
        qT = early[:, NF * E:NF * E + 3 * TOK].rearrange("p (c t) -> p c t", t=TOK)
        yT_a = early[:, NF * E + 3 * TOK:NF * E + 4 * TOK]
        yT_m = sb("yT_m", [T_ROWS, TOK])
        yT_b = yT_m[0:E - P + 1, :]
        kT = x1[:, 0:3 * TOK].rearrange("p (c t) -> p c t", t=TOK)
        att = x2[0:TT, 0:4 * HEADS * TT].rearrange("p (four h k) -> p four h k", four=4, k=TT)
        attT = x2[0:TT, 4 * HEADS * TT:5 * HEADS * TT].rearrange("p (h k) -> p h k", k=TT)
        vext = x2[0:TT, 5 * HEADS * TT:5 * HEADS * TT + NT * HEADS * 32].rearrange(
            "p (a h d) -> p a h d", h=HEADS, d=32)
        hidden = x2[:, 0:HC * TOK].rearrange("p (c t) -> p c t", t=TOK)
        top, total, rsum = sb("top", [TT, HEADS]), sb("total", [TT, HEADS]), sb("rsum", [TT, HEADS])
        logits = sb("logits", [P, NF, EXPERTS + 1])
        prob, key, first, second, gates = (sb(n, [P, NF, EXPERTS]) for n in ("prob", "key", "first", "second", "gates"))
        small = sb("small", [P, 8, NF])
        silu = sq[:, :, 0:HALF]

        ps = ctx.enter_context(nc.psum_tensor("ps", [P, 8, 512], F32))
        prod = [ps[:, b, :] for b in range(BANKS)]
        turn = ps[:, 4, :]
        c0_ps = ps[:, 5:7, :]
        chunk_ps = ps[:, 7, 0:CHUNK * TAPS0]
        term_ps = ps[:, 7, :].bitcast(BF16)[:, 512:]
        setup_ps = ps[:, 7, :]

        x_in, x_rest_in, w0_in, tables_in, cw_in, cw2_in, col_in = (sem(n) for n in ("x_in", "x_rest_in", "w0_in", "tables_in", "cw_in", "cw2_in", "col_in"))
        consts = sem("consts")
        w0_step = sem("w0_step")
        w0_turned, gram_made, gband_made, gband_ready = (
            sem(n) for n in ("w0_turned", "gram_made", "gband_made", "gband_ready"))
        cmean_step, cw_ready = sem("cmean_step"), sem("cw_ready")
        staged, stage_turned, stage_copied, gram_x = (
            sem(n) for n in ("staged", "stage_turned", "stage_copied", "gram_x"))
        quad_made, var0_made, vare0_made, rstd0_made, split_step = (
            sem(n) for n in ("quad_made", "var0_made", "vare0_made", "rstd0_made", "split_step"))
        terms_turned, terms_copied, conv0_done, act0_done = (
            sem(n) for n in ("terms_turned", "terms_copied", "conv0_done", "act0_done"))
        conv_done, sq_done, var_done, rstd_step, rstd_done, norm_done, turned, act_done = (
            sem(n) for n in ("conv_done", "sq_done", "var_done", "rstd_step", "rstd_done", "norm_done",
                             "turned", "act_done"))
        proj_in, att_in, ffn_in, down_in = (sem(n) for n in ("proj_in", "att_in", "ffn_in", "down_in"))
        fln_turned, fln_stats, fln_norm, fln_back, fln_done = (
            sem(n) for n in ("fln_turned", "fln_stats", "fln_norm", "fln_back", "fln_done"))
        v_ones, tok_var, tok_rstd = sem("v_ones"), sem("tok_var"), sem("tok_rstd")
        proj_done, h1_ready, h2_ready = sem("proj_done"), sem("h1_ready"), sem("h2_ready")
        ln_stats, ln_norm, ln_turned, yTa_ready, yTb_ready = (
            sem(n) for n in ("ln_stats", "ln_norm", "ln_turned", "yTa_ready", "yTb_ready"))
        qkv_done, qkv_by_act, qkv_by_dve = sem("qkv_done"), sem("qkv_by_act"), sem("qkv_by_dve")
        scores_done, top_done, shifted, exp_done = (sem(n) for n in ("scores_done", "top_done", "shifted", "exp_done"))
        total_done, rsum_done, scaled, att_turned, att_copied, values_done, values_copied = (
            sem(n) for n in ("total_done", "rsum_done", "scaled", "att_turned", "att_copied", "values_done",
                             "values_copied"))
        out_done = sem("out_done")
        router_done, router_step, router_exp, gates_ready = (
            sem(n) for n in ("router_done", "router_step", "router_exp", "gates_ready"))
        h2_moved = sem("h2_moved")
        hid_done, silu_done, hid_ready = sem("hid_done"), sem("silu_done"), sem("hid_ready")
        down_done, acc_done = sem("down_done"), sem("acc_done")
        stored = sem("stored")

        def window(c):
            s = stage[:, c, :]
            return bass.AP(tensor=s.tensor, offset=s.offset, ap=[list(s.ap[0]), [STRIDE0, CHUNK], [1, TAPS0]])

        def tiles(buf, first, n):
            return buf[:, bass.ds(first * P, n * P)] if not isinstance(first, int) else buf[:, first * P:(first + n) * P]

        def wait(eng, s, value):
            if not isinstance(value, int) or value > 0:
                eng.wait_ge(s, value)

        def qkv_copy(g, copy):
            b = (4 + g) % 8
            if g < 12:
                dst, t = (qT if g < 6 else kT), g % 2
                return copy(dst[:, (g % 6) // 2, HALF * t:HALF * t + HALF], ps[:, b, 0:HALF])
            return copy(vext[:, 2 * (g - 12):2 * (g - 12) + 2, :, 0:HD],
                        ps[0:TT, b, 0:2 * E].rearrange("p (a h d) -> p a h d", h=HEADS, d=HD))

        moved = nc.dram_tensor("moved", (TOK, E), F32).ap()
        W0_SPLIT = 10
        block = ctx.enter_context(nc.Block())

        @block.sync
        def _(sp):
            def samples(lo, hi, arrived):
                for h in range(2):
                    sp.dma_start(x_sb[64 * h:64 * h + 64, lo:hi], x[:, HALF_START * h + lo:HALF_START * h + hi]).then_inc(arrived, 16)
            for t, src in ((w0, w0_rows), (id_f, ident)):
                sp.dma_start(t[:, :], src).then_inc(w0_in, 16)
            samples(0, FIRST_SAMPLES, x_in)
            for t, src in ((diagonal_sb, diagonal), (shift_sb, shift), (pick_sb, pick_term), (id_b, ident_b)):
                sp.dma_start(t[:, :], src).then_inc(tables_in, 16)
            sp.dma_start(cw[:, 0:EARLY_BLOCKS, :], conv_w[:, 0:EARLY_BLOCKS, :]).then_inc(cw_in, 16)
            sp.dma_start(col[:, :], columns).then_inc(col_in, 16)
            samples(FIRST_SAMPLES, HALF_SAMPLES, x_rest_in)
            sp.dma_start(cw[:, EARLY_BLOCKS:, :], conv_w[:, EARLY_BLOCKS:, :]).then_inc(cw2_in, 16)
            for t, src in ((proj_sb, proj), (proj_b_sb, proj_b)):
                sp.dma_start(t[:, :], src).then_inc(proj_in, 16)
            for pair, src in ((wq_sb, wq), (wk_sb, wk), (wv_sb, wv), (wr_sb, router)):
                sp.dma_start(pair[0][:, :], src[0:P, :]).then_inc(att_in, 16)
                sp.dma_start(pair[1][:, :], src[P:, :]).then_inc(att_in, 16)
            for t, src in ((wo_sb[:, :, :], wo), (yT_m[E - P:, :], token_rows), (rank_sb[:, :], rank)):
                sp.dma_start(t, src).then_inc(att_in, 16)
            for pair, src in ((wg_sb, gate), (wu_sb, up)):
                sp.dma_start(pair[0][:, :], src[0:P, :]).then_inc(ffn_in, 16)
                sp.dma_start(pair[1][:, :], src[P:, :]).then_inc(ffn_in, 16)
            sp.wait_ge(act_done, GROUPS)
            sp.dma_start(wd_sb, down).then_inc(down_in, 16)
            sp.wait_ge(h2_ready, NT)
            sp.dma_start(moved.rearrange("(a p) e -> p a e", p=TT), h2).then_inc(h2_moved, 16)
            sp.wait_ge(h2_moved, 16)
            sp.dma_start(acc, moved.rearrange("(f p) e -> p f e", p=FT)).then_inc(h2_moved, 16)
            for k in range(NF // 2):
                sp.wait_ge(acc_done, NF * EXPERTS + 2 * (k + 1))
                sp.dma_start(out.rearrange("(f p) e -> p f e", p=FT)[:, 2 * k:2 * k + 2, :],
                             acc[:, 2 * k:2 * k + 2, :]).then_inc(stored, 16)
            sp.wait_ge(stored, 16 * (NF // 2))

        @block.tensor
        def _(pe):
            def chunk_turn(c, par):
                pe.wait_ge(staged, c + 1)
                wait(pe, quad_made, c)
                nc.tensor.transpose(chunk_ps[0:CHUNK_SAMPLES, 0:P], stage[:, par, :], id_f[:, :]).then_inc(stage_turned, 1)

            def chunk_gram(c):
                pe.wait_ge(stage_copied, c + 1)
                nc.tensor.matmul(chunk_ps[:, :], stageT[:, :], gband[:, :],
                                 start=True, stop=True).then_inc(gram_x, 1)

            def batch_turn(b, m, chunks, read):
                pe.wait_ge(split_step, SPLIT_STEPS * chunks)
                pe.wait_ge(quad_made, read)
                wait(pe, terms_copied, m)
                t0 = BATCH_T * (b % 5)
                for k in range(BATCH_T // 2):
                    last = nc.tensor.transpose(term_ps[:, P * k:P * k + P],
                                               terms[:, t0 + 2 * k:t0 + 2 * k + 2, :].rearrange("p t k -> p (t k)"), id_b[:, :])
                last.then_inc(terms_turned, 1)

            def batch_multiply(m):
                pe.wait_ge(terms_copied, m + 1)
                wait(pe, act0_done, m)
                nc.tensor.matmul(c0_ps[:, 0, :], w0_stack[0:64, :], termsT[0:64, :], start=True, stop=True)
                nc.tensor.matmul(c0_ps[:, 1, :], w0_stack[64:128, :], termsT[64:128, :],
                                 start=True, stop=True).then_inc(conv0_done, 1)

            def multiply(g, between=None):
                if g.batch is not None:
                    pe.wait_ge(act0_done, g.batch)
                for n in g.fed:
                    pe.wait_ge(act_done, n + 1)
                if g.bank_free is not None:
                    pe.wait_ge(norm_done, g.bank_free + 1)
                src, taps = acts[g.layer - 1], TAPS[g.layer]
                for t, first in enumerate(g.inputs):
                    if between is not None and t == g.tiles // 2:
                        batch_turn(*between)
                    for k in range(taps):
                        at = (first + k) % g.wrap if g.wrap else first + k
                        last = nc.tensor.matmul(prod[g.bank][:, P * t:P * t + P], src[:, P * at:P * at + P],
                                                cw[:, BLOCK0[g.layer] + k, :], start=(k == 0), stop=(k == taps - 1))
                last.then_inc(conv_done, 1)

            def turn_group(g):
                pe.wait_ge(norm_done, g.n + 1)
                wait(pe, act_done, g.n)
                for t in range(g.tiles):
                    last = nc.tensor.transpose(turn[:, P * t:P * t + P], yn[:, g.par, P * t:P * t + P], id_f[:, :])
                last.then_inc(turned, 1)

            def step(i, s, last):
                m = 5 * i + BATCH[s] if s in BATCH and not (last and BATCH[s] == 5) else None
                between = None
                if m is not None:
                    b = BATCH[s]
                    read = 2 if last else 2 + sum(z < s for z in CH_GRAM)
                    between = (b, m, 2 * i + (1 if b < 2 else 2 if b < 5 else 3), 2 * i + read)
                g = group(i, s)
                if g is None and m is not None:
                    batch_turn(*between)
                if g is not None:
                    multiply(g, between)
                    g2 = back(i, s, 2)
                    if g2 is not None:
                        turn_group(g2)
                if m is not None:
                    batch_multiply(m)
                if not last:
                    if s in CH_STAGE:
                        chunk_turn(2 * i + CH_STAGE[s], CH_STAGE[s] % 2)
                    if s in CH_GRAM:
                        chunk_gram(2 * i + CH_GRAM[s])

            pe.wait_ge(w0_in, 2 * 16)
            pe.wait_ge(w0_step, 3)
            nc.tensor.transpose(setup_ps[:, 0:GROW], w0[0:GROW, :], id_f[0:GROW, 0:GROW]).then_inc(w0_turned, 1)
            pe.wait_ge(gram_made, 1)
            nc.tensor.matmul(setup_ps[0:GROW, 64:64 + GROW], w0T[:, :], w0T[:, :], start=True, stop=True).then_inc(w0_turned, 1)
            pe.wait_ge(gram_made, 2)
            for t in range(0, CHUNK, SECTIONS):
                at, n = SHIFT_AT - STRIDE0 * t, TAPS0 * min(SECTIONS, CHUNK - t)
                last = nc.tensor.matmul(setup_ps[0:CHUNK_SAMPLES, P + TAPS0 * t:P + TAPS0 * t + n],
                                        shift_sb[0:n, at:at + CHUNK_SAMPLES], gram[0:n, 0:n], start=True, stop=True)
            last.then_inc(gband_made, 1)
            pe.wait_ge(gband_ready, 1)
            chunk_turn(0, 0)
            chunk_gram(0)
            chunk_turn(1, 1)
            chunk_gram(1)
            pe.wait_ge(w0_step, W0_SPLIT)
            batch_turn(0, 0, 1, 2)
            batch_multiply(0)
            pe.wait_ge(consts, CONSTS)
            pe.wait_ge(cw_ready, 1)
            for s in range(NS):
                step(0, s, False)
            with pe.Fori(1, ITERS - 1) as i:
                for s in range(NS):
                    step(i, s, False)
            for s in range(NS):
                step(ITERS - 1, s, True)
            pe.wait_ge(cw_ready, 2)
            turned_to = BEFORE_TAIL - 2
            every = [group(ITERS - 1, NS - 2), group(ITERS - 1, NS - 1)] + TAIL
            for k, g in enumerate(TAIL):
                while turned_to <= max(g.fed):
                    turn_group(every[turned_to - BEFORE_TAIL + 2])
                    turned_to += 1
                multiply(g)
                while turned_to <= g.n - 2:
                    turn_group(every[turned_to - BEFORE_TAIL + 2])
                    turned_to += 1
            while turned_to < GROUPS:
                turn_group(every[turned_to - BEFORE_TAIL + 2])
                turned_to += 1


            pe.wait_ge(act_done, GROUPS)
            for j in range(6):
                last = nc.tensor.transpose(ps[:, j // 4, P * (j % 4):P * (j % 4) + P], x6[:, P * j:P * j + P], id_f[:, :])
                if j in (3, 5):
                    last.then_inc(fln_turned, 1)
            pe.wait_ge(fln_norm, 1)
            for j in range(6):
                last = nc.tensor.transpose(ps[:, 2 + j // 4, P * (j % 4):P * (j % 4) + P],
                                           yn[:, j // 4, P * (j % 4):P * (j % 4) + P], id_f[:, :])
                if j in (3, 5):
                    last.then_inc(fln_back, 1)
            pe.wait_ge(fln_done, 2)
            pe.wait_ge(proj_in, 32)
            for a in range(NT):
                o = ps[0:TT, 4 + a // 2, E * (a % 2):E * (a % 2) + E]
                last = nc.tensor.matmul(o, nT[:, TT * a:TT * a + TT], proj_sb[:, :], start=True, stop=True)
                if a % 2:
                    last.then_inc(proj_done, 1)

            def turn_tokens(which):
                for t in range(2):
                    pe.wait_ge(ln_norm, NT * which + 4 * (t + 1))
                    for a in range(4 * t, 4 * t + 4):
                        at = TT * (a % 4)
                        nc.tensor.transpose(ps[:, t, at:at + TT], y[:, a, 0:P], id_f[0:TT, 0:TT])
                        last = nc.tensor.transpose(ps[0:E - P, 2 + t, at:at + TT], y[:, a, P:E], id_f[0:TT, 0:TT])
                    last.then_inc(ln_turned, 1)
            turn_tokens(0)
            pe.wait_ge(att_in, ATT_LOADS * 16)
            pe.wait_ge(yTa_ready, 2)
            pe.wait_ge(yTb_ready, 2)
            for g in range(QKV_GROUPS):
                o = ps[:, (4 + g) % 8, :]
                if g < 4:
                    pe.wait_ge(h1_ready, g + 1)
                if g >= 8:
                    pe.wait_ge(qkv_by_act if g % 2 == 0 else qkv_by_dve, (g - 8) // 2 + 1)
                if g < 12:
                    w = wq_sb if g < 6 else wk_sb
                    c, t = (g % 6) // 2, g % 2
                    tok = slice(HALF * t, HALF * t + HALF)
                    nc.tensor.matmul(o[:, 0:HALF], w[0][:, P * c:P * c + P], yT_a[:, tok], start=True, stop=False)
                    last = nc.tensor.matmul(o[:, 0:HALF], w[1][:, P * c:P * c + P], yT_m[:, tok], start=False, stop=True)
                else:
                    for a in (2 * (g - 12), 2 * (g - 12) + 1):
                        v = o[0:TT, E * (a % 2):E * (a % 2) + E]
                        nc.tensor.matmul(v, yT_a[:, TT * a:TT * a + TT], wv_sb[0][:, :], start=True, stop=False)
                        last = nc.tensor.matmul(v, yT_b[:, TT * a:TT * a + TT], wv_sb[1][:, :], start=False, stop=True)
                last.then_inc(qkv_done, 1)
            pe.wait_ge(qkv_by_act, QKV_GROUPS // 2)
            pe.wait_ge(qkv_by_dve, QKV_GROUPS // 2)
            for step_a in range(NT + 5):
                a = step_a
                if a < NT:
                    wait(pe, shifted, a)
                    tok = slice(TT * a, TT * a + TT)
                    for c in range(3):
                        for r in range(4):
                            last = nc.tensor.matmul(ps[0:TT, r, TT * c:TT * c + TT], qT[32 * r:32 * r + 32, c, tok],
                                                    kT[32 * r:32 * r + 32, c, tok], start=True, stop=True)
                    last.then_inc(scores_done, 1)
                a = step_a - 5
                if a >= 0:
                    pe.wait_ge(values_copied, a + 1)
                    for c in range(3):
                        last = nc.tensor.matmul(ps[0:TT, 7, AT_OUT:AT_OUT + E], qT[:, c, TT * a:TT * a + TT], wo_sb[:, c, :],
                                                start=(c == 0), stop=(c == 2))
                    last.then_inc(out_done, 1)
                a = step_a - 3
                if 0 <= a < NT:
                    pe.wait_ge(scaled, a + 1)
                    wait(pe, att_copied, a)
                    for h in range(HEADS):
                        last = nc.tensor.transpose(ps[0:TT, 4 + h // 4, TT * (h % 4):TT * (h % 4) + TT],
                                                   att[:, a % 4, h, :], id_f[0:TT, 0:TT])
                    last.then_inc(att_turned, 1)
                a = step_a - 4
                if 0 <= a < NT:
                    pe.wait_ge(att_copied, a + 1)
                    wait(pe, values_copied, a)
                    wait(pe, h2_ready, a)
                    for h in range(HEADS):
                        r, c = h // 3, h % 3
                        last = nc.tensor.matmul(ps[32 * r:32 * r + 32, 7, TT * c:TT * c + TT], vext[:, a, 4 * c + r, :],
                                                attT[:, h, :], start=True, stop=True)
                    last.then_inc(values_done, 1)
            pe.wait_ge(h2_ready, NT)
            turn_tokens(1)
            pe.wait_ge(yTa_ready, 4)
            pe.wait_ge(yTb_ready, 4)
            for f in range(NF):
                o = ps[:, 4, (EXPERTS + 1) * f:(EXPERTS + 1) * (f + 1)]
                nc.tensor.matmul(o, yT_a[:, FT * f:FT * f + FT], wr_sb[0][:, :], start=True, stop=False)
                last = nc.tensor.matmul(o, yT_b[:, FT * f:FT * f + FT], wr_sb[1][:, :], start=False, stop=True)
            last.then_inc(router_done, 1)
            pe.wait_ge(ffn_in, 64)
            pe.wait_ge(down_in, 16)

            def hidden_units(v):
                c, t = CHUNK_ORDER[v // 2], v % 2
                wait(pe, hid_ready, v - 1)
                tok = slice(HALF * t, HALF * t + HALF)
                for k, w in enumerate((wg_sb, wu_sb)):
                    o = ps[:, 2 * (v % 2) + k, 0:HALF]
                    nc.tensor.matmul(o, w[0][:, P * c:P * c + P], yT_a[:, tok], start=True, stop=False)
                    last = nc.tensor.matmul(o, w[1][:, P * c:P * c + P], yT_b[:, tok], start=False, stop=True)
                last.then_inc(hid_done, 1)

            def down_products(d):
                chunks, blocks, need = DOWN[d]
                pe.wait_ge(hid_ready, need)
                for f in range(NF):
                    if f % 2 == 0:
                        if d == 0:
                            pe.wait_ge(router_step, 1)
                        else:
                            pe.wait_ge(acc_done, NF * (d - 1) + f + 2)
                    o = ps[:, 4 + f // 2, E * (f % 2):E * (f % 2) + E]
                    for k, (c, b) in enumerate(zip(chunks, blocks)):
                        last = nc.tensor.matmul(o, hidden[:, c, FT * f:FT * f + FT], wd_sb[:, b, :],
                                                start=(k == 0), stop=(k == len(chunks) - 1))
                    if f % 2:
                        last.then_inc(down_done, 1)
            for kind, k in FFN_ORDER:
                (hidden_units if kind == "hidden" else down_products)(k)

        @block.scalar
        def _(act):
            def square(g):
                act.wait_ge(conv_done, g.n + 1)
                wait(act, var_done, g.n - 1)
                nc.scalar.activation(sq[:, g.par, 0:g.tiles * P], prod[g.bank][:, 0:g.tiles * P], ACT.Square,
                                     scale=P ** -0.5).then_inc(sq_done, 1)

            def gelu(g):
                act.wait_ge(turned, g.n + 1)
                for n in g.out_free:
                    act.wait_ge(conv_done, n + 1)
                nc.scalar.activation(tiles(acts[g.layer], g.out, g.tiles), turn[:, 0:g.tiles * P], ACT.Gelu,
                                     bias=col[:, 8 + g.layer:9 + g.layer], scale=col[:, g.layer:g.layer + 1]).then_inc(act_done, 1)

            def gelu0(b, m, free):
                act.wait_ge(conv0_done, m + 1)
                if free is not None:
                    act.wait_ge(conv_done, free + 1)
                t0 = BATCH_T * (b % 5)
                ring = early[:, t0 * P:(t0 + BATCH_T) * P].rearrange("p (k two l) -> p two k l", two=2, l=P)
                nc.scalar.activation(ring, c0_ps[:, :, :].rearrange("p two (k l) -> p two k l", l=P), ACT.Gelu,
                                     bias=col[:, 8:9], scale=col[:, 0:1]).then_inc(act0_done, 1)

            def step(i, s, last):
                g = group(i, s)
                if g is not None and (g1 := back(i, s, 1)) is not None:
                    square(g1)
                z = s - 1
                if z in BATCH and not (last and BATCH[z] == 5):
                    b = BATCH[z]
                    if b == 5:
                        free = number(i, C1_SLOT[1])
                    elif b == 4:
                        free = number(i, C1_SLOT[0])
                    else:
                        free = None if isinstance(i, int) and i == 0 else number_before(i, C1_SLOT[b + 1])
                    gelu0(b, 5 * i + b, free)
                if g is not None and (g3 := back(i, s, 3)) is not None:
                    gelu(g3)

            act.wait_ge(consts, CONSTS)
            nc.scalar.activation(table_warm[:, :], neg_half[:, 0:1], ACT.Gelu)
            act.wait_ge(col_in, 16)
            gelu0(0, 0, None)
            for s in range(NS):
                step(0, s, False)
            with act.Fori(1, ITERS - 1) as i:
                for s in range(NS):
                    step(i, s, False)
            for s in range(NS):
                step(ITERS - 1, s, True)
            squared, acted = BEFORE_TAIL - 1, BEFORE_TAIL - 3
            every = [group(ITERS - 1, NS - 3 + k) for k in range(3)] + TAIL
            for g in TAIL:
                while squared < g.n:
                    square(every[squared - BEFORE_TAIL + 3])
                    squared += 1
                while acted <= max(max(g.fed), g.n - 3):
                    gelu(every[acted - BEFORE_TAIL + 3])
                    acted += 1
            square(TAIL[-1])
            while acted < GROUPS:
                gelu(every[acted - BEFORE_TAIL + 3])
                acted += 1


            ordered = nT.rearrange("p (b h j) -> p j h b", h=2, j=6)
            for t, (a, b) in enumerate(((0, 4), (4, 6))):
                act.wait_ge(fln_back, t + 1)
                for j in range(a, b):
                    last = nc.scalar.activation(ordered[:, j, :, :],
                                                ps[:, 2 + t, P * (j - a):P * (j - a) + P].rearrange("p (h b) -> p h b", h=2),
                                                ACT.Identity, bias=col[:, 15:16], scale=col[:, 7:8])
                last.then_inc(fln_done, 1)
            def copy_tokens(which):
                for t in range(2):
                    act.wait_ge(ln_turned, 2 * which + t + 1)
                    nc.scalar.activation(yT_a[:, HALF * t:HALF * t + HALF], ps[:, t, 0:HALF], ACT.Copy).then_inc(yTa_ready, 1)
            copy_tokens(0)
            for g in range(0, QKV_GROUPS, 2):
                act.wait_ge(qkv_done, g + 1)
                qkv_copy(g, lambda o, i: nc.scalar.activation(o, i, ACT.Copy)).then_inc(qkv_by_act, 1)
            for step_a in range(NT + 5):
                a = step_a - 4
                if 0 <= a < NT:
                    act.wait_ge(values_done, a + 1)
                    nc.scalar.activation(qT[:, :, TT * a:TT * a + TT], ps[:, 7, 0:3 * TT].rearrange("p (c t) -> p c t", t=TT),
                                         ACT.Copy).then_inc(values_copied, 1)
                a = step_a - 3
                if 0 <= a < NT:
                    act.wait_ge(att_turned, a + 1)
                    wait(act, values_done, a)
                    nc.scalar.activation(attT[:, :, :].rearrange("p (b h) k -> p b (h k)", b=3), ps[0:TT, 4:7, 0:4 * TT],
                                         ACT.Copy).then_inc(att_copied, 1)
                a = step_a
                if a < NT:
                    act.wait_ge(shifted, a + 1)
                    nc.scalar.activation(att[:, a % 4, :, :], att[:, a % 4, :, :], ACT.Exp, scale=HD ** -0.5).then_inc(exp_done, 1)
            copy_tokens(1)
            act.wait_ge(router_step, 3)
            nc.scalar.activation(prob[:, :, :], prob[:, :, :], ACT.Exp).then_inc(router_exp, 1)
            nc.scalar.activation(small[:, 1, :], logits[:, :, EXPERTS], ACT.Exp, scale=-1.0).then_inc(router_exp, 1)
            for v in range(2 * HC):
                act.wait_ge(hid_done, v + 1)
                wait(act, hid_ready, v - 1)
                nc.scalar.activation(silu[:, v % 2, :], ps[:, 2 * (v % 2), 0:HALF], ACT.Silu).then_inc(silu_done, 1)

        @block.gpsimd
        def _(pool):
            def stage_chunk(c, par):
                wait(pool, split_step, SPLIT_STEPS * (c - 2) + 1)
                pool.tensor_copy(stage[:, par, :], x_sb[:, bass.ds(c * CHUNK_STEP, CHUNK_SAMPLES)]
                                 if not isinstance(c, int) else x_sb[:, c * CHUNK_STEP:c * CHUNK_STEP + CHUNK_SAMPLES]).then_inc(staged, 1)

            def rstd_chunk(c, half):
                pool.wait_ge(vare0_made, c + 1)
                wait(pool, split_step, SPLIT_STEPS * (c - 1) + 1)
                v = slice(CHUNK // 2 * half, CHUNK // 2 * (half + 1))
                pool.tensor_tensor(rstd0[:, v], vare0[:, v], neg_half[:, v], ALU.pow).then_inc(rstd0_made, 1)

            def rstd_group(g):
                pool.wait_ge(var_done, g.n + 1)
                t = g.tiles
                pool.tensor_tensor(vare[:, g.par, 0:t], var[:, g.par, 0:t], eps[:, 0:t], ALU.add).then_inc(rstd_step, 1)
                pool.wait_ge(rstd_step, g.n + 1)
                wait(pool, norm_done, g.n - 1)
                pool.tensor_tensor(rstd[:, g.par, 0:t], vare[:, g.par, 0:t], neg_half[:, 0:t], ALU.pow).then_inc(rstd_done, 1)

            def step(i, s, last):
                if not last and s in CH_STAGE:
                    stage_chunk(2 * i + CH_STAGE[s], CH_STAGE[s] % 2)
                if group(i, s) is not None and (g1 := back(i, s, 1)) is not None:
                    rstd_group(g1)
                if not last and s in CH_RSTD:
                    rstd_chunk(2 * i + CH_RSTD[s][0], CH_RSTD[s][1])

            pool.memset(neg_half[:, :], -0.5).then_inc(consts, 1)
            pool.memset(eps[:, :], EPS).then_inc(consts, 1)
            pool.memset(terms[:, :, :], 0.0).then_inc(consts, 1)
            pool.memset(early[:, (RING0 - 2) * P:RING0 * P], 0.0).then_inc(consts, 1)
            pool.memset(x1[:, (RING1 - 1) * P:RING1 * P], 0.0).then_inc(consts, 1)
            pool.wait_ge(x_in, 32)
            pool.wait_ge(consts, CONSTS)
            stage_chunk(0, 0)
            stage_chunk(1, 1)
            for c in range(2):
                for half in range(2):
                    rstd_chunk(c, half)
            pool.wait_ge(x_rest_in, 32)
            for s in range(NS):
                step(0, s, False)
            with pool.Fori(1, ITERS - 1) as i:
                for s in range(NS):
                    step(i, s, False)
            for s in range(NS):
                step(ITERS - 1, s, True)
            for g in [group(ITERS - 1, NS - 1)] + TAIL:
                rstd_group(g)


            pool.wait_ge(act_done, GROUPS)
            pool.memset(vext, 1.0).then_inc(v_ones, 1)

            def rstd_tokens(k, sem_in, at, rows, n):
                pool.wait_ge(sem_in, at)
                pool.tensor_scalar(vtok[0:rows, 0:n], mv[0:rows, 0:n, 1], 1.0, EPS, ALU.mult, ALU.add).then_inc(tok_var, 1)
                pool.wait_ge(tok_var, k + 1)
                pool.tensor_tensor(rtok[0:rows, 0:n], vtok[0:rows, 0:n], neg_half[0:rows, 0:n], ALU.pow).then_inc(tok_rstd, 1)
            rstd_tokens(0, fln_stats, 2, P, 6)
            rstd_tokens(1, ln_stats, 2, TT, NT)
            for a in range(NT):
                pool.wait_ge(rsum_done, a + 1)
                pool.tensor_tensor(att[:, a % 4, :, :], att[:, a % 4, :, :],
                                   rsum[:, :].unsqueeze(2).to_broadcast([TT, HEADS, TT]), ALU.mult).then_inc(scaled, 1)
            rstd_tokens(2, ln_stats, 4, TT, NT)

        @block.vector
        def _(dve):
            def copy_terms(m):
                dve.wait_ge(terms_turned, m + 1)
                wait(dve, conv0_done, m)
                nc.vector.tensor_copy(termsT[:, :], term_ps[:, 0:512]).then_inc(terms_copied, 1)

            def copy_stage(c):
                dve.wait_ge(stage_turned, c + 1)
                wait(dve, gram_x, c)
                nc.vector.tensor_copy(stageT[:, :], chunk_ps[0:CHUNK_SAMPLES, 0:P]).then_inc(stage_copied, 1)

            def quad_chunk(c, par):
                dve.wait_ge(gram_x, c + 1)
                wait(dve, vare0_made, c)
                nc.vector.tensor_tensor(quad[:, :, :], chunk_ps[:, :].rearrange("p (t k) -> p t k", k=TAPS0),
                                        window(par), ALU.mult).then_inc(quad_made, 1)

            def var_chunk(c):
                dve.wait_ge(quad_made, c + 1)
                nc.vector.tensor_reduce(var0[:, :], quad[:, :, :], AX.X, ALU.add).then_inc(var0_made, 1)
                dve.wait_ge(var0_made, c + 1)
                wait(dve, rstd0_made, 2 * c)
                nc.vector.tensor_scalar(vare0[:, :], var0[:, :], 0.0, EPS, ALU.max, ALU.add).then_inc(vare0_made, 1)

            def split_chunk(c, par, used):
                dve.wait_ge(rstd0_made, 2 * c + 2)
                k = SPLIT_STEPS * c
                wait(dve, split_step, k)
                nc.vector.tensor_tensor(xs[:, :, :], window(par), rstd0[:, :].unsqueeze(2).to_broadcast([P, CHUNK, TAPS0]),
                                        ALU.mult).then_inc(split_step, 1)
                dve.wait_ge(split_step, k + 1)
                if used is not None:
                    dve.wait_ge(terms_turned, used)
                t = terms[:, CHUNK * par:CHUNK * par + CHUNK, :]

                def section(a, n):
                    return t[:, :, TAPS0 * a:TAPS0 * (a + n)].rearrange("p t (s k) -> p t s k", k=TAPS0)

                def again(v, n):
                    return v[:, :, :].unsqueeze(2).to_broadcast([P, CHUNK, n, TAPS0])
                nc.vector.tensor_copy(section(0, 3), again(xs, 3)).then_inc(split_step, 1)
                dve.wait_ge(split_step, k + 2)
                nc.vector.tensor_tensor(xrest[:, :, :], xs[:, :, :], t[:, :, 0:TAPS0], ALU.subtract).then_inc(split_step, 1)
                dve.wait_ge(split_step, k + 3)
                nc.vector.tensor_copy(section(3, 2), again(xrest, 2)).then_inc(split_step, 1)
                dve.wait_ge(split_step, k + 4)
                nc.vector.tensor_tensor(t[:, :, 5 * TAPS0:6 * TAPS0], xrest[:, :, :], t[:, :, 3 * TAPS0:4 * TAPS0],
                                        ALU.subtract).then_inc(split_step, 1)

            def sum_group(g):
                dve.wait_ge(sq_done, g.n + 1)
                wait(dve, rstd_step, g.n - 1)
                nc.vector.tensor_reduce(var[:, g.par, 0:g.tiles], sq[:, g.par, 0:g.tiles * P].rearrange("p (t c) -> p t c", c=P),
                                        AX.X, ALU.add).then_inc(var_done, 1)

            def norm_group(g):
                dve.wait_ge(rstd_done, g.n + 1)
                wait(dve, turned, g.n - 1)
                t = g.tiles
                nc.vector.tensor_tensor(yn[:, g.par, 0:t * P].rearrange("p (t c) -> p t c", c=P),
                                        prod[g.bank][:, 0:t * P].rearrange("p (t c) -> p t c", c=P),
                                        rstd[:, g.par, 0:t].unsqueeze(2).to_broadcast([P, t, P]), ALU.mult).then_inc(norm_done, 1)

            def step(i, s, last):
                if not last and s in CH_GRAM:
                    copy_stage(2 * i + CH_GRAM[s])
                if not last and s in CH_QUAD:
                    quad_chunk(2 * i + CH_QUAD[s], CH_QUAD[s] % 2)
                g = group(i, s)
                if g is not None and (g2 := back(i, s, 2)) is not None:
                    norm_group(g2)
                if s in BATCH and not (last and BATCH[s] == 5):
                    copy_terms(5 * i + BATCH[s])
                if g is not None and (g1 := back(i, s, 1)) is not None:
                    sum_group(g1)
                if not last:
                    if s in CH_QUAD:
                        var_chunk(2 * i + CH_QUAD[s])
                    if s in CH_SPLIT:
                        c = CH_SPLIT[s]
                        split_chunk(2 * i + c, c % 2, 5 * i + (3 if c == 2 else 5))

            dve.wait_ge(w0_in, 2 * 16)
            done = [0]

            def w0_next(ins):
                done[0] += 1
                ins.then_inc(w0_step, 1)
                dve.wait_ge(w0_step, done[0])
            w0_next(nc.vector.tensor_reduce(w0mean[:, :], w0[:, :], AX.X, ALU.add))
            w0_next(nc.vector.tensor_scalar(w0mean[:, :], w0mean[:, :], -1.0 / P, None, ALU.mult))
            w0_next(nc.vector.tensor_scalar(w0[:, :], w0[:, :], w0mean[:, 0:1], None, ALU.add))
            dve.wait_ge(w0_turned, 1)
            nc.vector.tensor_copy(w0T[:, :], setup_ps[:, 0:GROW]).then_inc(gram_made, 1)
            dve.wait_ge(tables_in, 4 * 16)
            dve.wait_ge(w0_turned, 2)
            nc.vector.scalar_tensor_tensor(gram[:, :], setup_ps[0:GROW, 64:64 + GROW], 1.0 / P, diagonal_sb[:, :],
                                           ALU.mult, ALU.mult).then_inc(gram_made, 1)
            w0_next(nc.vector.tensor_copy(w0term[:, 0, :], w0[:, :]))
            w0_next(nc.vector.tensor_tensor(w0rest[:, :], w0[:, :], w0term[:, 0, :], ALU.subtract))
            w0_next(nc.vector.tensor_copy(w0term[:, 1, :], w0rest[:, :]))
            dve.wait_ge(gband_made, 1)
            nc.vector.tensor_copy(gband[:, :], setup_ps[0:CHUNK_SAMPLES, P:P + CHUNK * TAPS0]).then_inc(gband_ready, 1)
            w0_next(nc.vector.tensor_tensor(w0term[:, 2, :], w0rest[:, :], w0term[:, 1, :], ALU.subtract))
            copy_stage(0)
            w0_next(nc.vector.tensor_scalar(w0_stack[:, :], w0term[:, 0, :], pick_sb[:, 0:1], None, ALU.mult))
            quad_chunk(0, 0)
            var_chunk(0)
            copy_stage(1)
            for k in (1, 2):
                w0_next(nc.vector.scalar_tensor_tensor(w0_stack[:, :], w0term[:, k, :], pick_sb[:, k:k + 1], w0_stack[:, :],
                                                       ALU.mult, ALU.add))
            assert done[0] == W0_SPLIT
            quad_chunk(1, 1)
            dve.wait_ge(consts, CONSTS)
            split_chunk(0, 0, None)
            var_chunk(1)

            def centre(a, b, base):
                nc.vector.tensor_reduce(cmean[:, a:b], cw[:, a:b, :], AX.X, ALU.add).then_inc(cmean_step, 1)
                dve.wait_ge(cmean_step, base + 1)
                nc.vector.tensor_scalar(cmean[:, a:b], cmean[:, a:b], -1.0 / P, None, ALU.mult).then_inc(cmean_step, 1)
                dve.wait_ge(cmean_step, base + 2)
                for k in range(a, b):
                    last = nc.vector.tensor_scalar(cw[:, k, :], cw[:, k, :], cmean[:, k:k + 1], None, ALU.add)
                last.then_inc(cw_ready, 1)
            copy_terms(0)
            dve.wait_ge(cw_in, 16)
            centre(0, EARLY_BLOCKS, 0)
            split_chunk(1, 1, None)
            for s in range(NS):
                step(0, s, False)
            dve.wait_ge(cw2_in, 16)
            centre(EARLY_BLOCKS, BLOCKS, 2)
            with dve.Fori(1, ITERS - 1) as i:
                for s in range(NS):
                    step(i, s, False)
            for s in range(NS):
                step(ITERS - 1, s, True)
            every = [group(ITERS - 1, NS - 2), group(ITERS - 1, NS - 1)] + TAIL
            normed = 0
            for k, g in enumerate(every):
                after = max(every[k + 1].fed) if 1 <= k + 1 < len(every) and every[k + 1].fed else 0
                if k > 0:
                    sum_group(g)
                while normed <= k and (normed < k or after >= g.n - 2 or g is every[-1]):
                    norm_group(every[normed])
                    normed += 1

            for j in range(6):
                if j in (0, 4):
                    dve.wait_ge(fln_turned, 1 + j // 4)
                last = nc.vector.bn_stats(stat[:, j, :], ps[:, j // 4, P * (j % 4):P * (j % 4) + P])
            last.then_inc(fln_stats, 1)
            dve.wait_ge(fln_stats, 1)
            for j in range(6):
                last = nc.vector.bn_aggr(mv[:, j, :], stat[:, j, :])
            last.then_inc(fln_stats, 1)
            dve.wait_ge(tok_rstd, 1)
            for j in range(6):
                last = nc.vector.tensor_scalar(yn[:, j // 4, P * (j % 4):P * (j % 4) + P],
                                               ps[:, j // 4, P * (j % 4):P * (j % 4) + P], mv[:, j, 0:1], rtok[:, j:j + 1],
                                               ALU.subtract, ALU.mult)
            last.then_inc(fln_norm, 1)

            for k in range(NT // 2):
                dve.wait_ge(proj_done, k + 1)
                if k == 0:
                    dve.wait_ge(proj_in, 32)
                nc.vector.tensor_tensor(h1[:, 2 * k:2 * k + 2, :], ps[0:TT, 4 + k, 0:2 * E].rearrange("p (a e) -> p a e", e=E),
                                        proj_b_sb[:, :].unsqueeze(1).to_broadcast([TT, 2, E]), ALU.add).then_inc(h1_ready, 1)
            for a in range(NT):
                dve.wait_ge(h1_ready, a // 2 + 1)
                last = nc.vector.bn_stats(stat[0:TT, a, :], h1[:, a, :])
            last.then_inc(ln_stats, 1)

            def norm_tokens(which, h):
                dve.wait_ge(ln_stats, 2 * which + 1)
                for a in range(NT):
                    last = nc.vector.bn_aggr(mv[0:TT, a, :], stat[0:TT, a, :])
                last.then_inc(ln_stats, 1)
                dve.wait_ge(tok_rstd, which + 2)
                for a in range(NT):
                    nc.vector.tensor_scalar(y[:, a, :], h[:, a, :], mv[0:TT, a, 0:1], rtok[0:TT, a:a + 1],
                                            ALU.subtract, ALU.mult).then_inc(ln_norm, 1)
                for t in range(2):
                    dve.wait_ge(ln_turned, 2 * which + t + 1)
                    nc.vector.tensor_copy(yT_b[0:E - P, HALF * t:HALF * t + HALF], ps[0:E - P, 2 + t, 0:HALF]).then_inc(yTb_ready, 1)
            norm_tokens(0, h1)
            dve.wait_ge(v_ones, 1)
            for g in range(1, QKV_GROUPS, 2):
                dve.wait_ge(qkv_done, g + 1)
                qkv_copy(g, nc.vector.tensor_copy).then_inc(qkv_by_dve, 1)
            for step_a in range(NT + 5):
                a = step_a
                s4 = ps[0:TT, 0:4, 0:3 * TT].rearrange("p r (c k) -> p r c k", k=TT)
                t4 = top[:, :].rearrange("p (r c) -> p r c", c=3)
                if a < NT:
                    dve.wait_ge(scores_done, a + 1)
                    wait(dve, shifted, a)
                    nc.vector.tensor_reduce(t4, s4, AX.X, ALU.max).then_inc(top_done, 1)
                a = step_a - 5
                if a >= 0:
                    dve.wait_ge(out_done, a + 1)
                    nc.vector.tensor_tensor(h2[:, a, :], ps[0:TT, 7, AT_OUT:AT_OUT + E], h1[:, a, :], ALU.add).then_inc(h2_ready, 1)
                a = step_a
                if a < NT:
                    dve.wait_ge(top_done, a + 1)
                    wait(dve, att_turned, a - 3)
                    nc.vector.tensor_tensor(att[:, a % 4, :, :].rearrange("p (r c) k -> p r c k", c=3), s4,
                                            t4.unsqueeze(3).to_broadcast([TT, 4, 3, TT]), ALU.subtract).then_inc(shifted, 1)
                a = step_a - 5
                if a >= 0:
                    dve.wait_ge(h2_ready, a + 1)
                    last = nc.vector.bn_stats(stat[0:TT, a, :], h2[:, a, :])
                a = step_a - 1
                if 0 <= a < NT:
                    dve.wait_ge(exp_done, a + 1)
                    wait(dve, rsum_done, a)
                    nc.vector.tensor_reduce(total[:, :], att[:, a % 4, :, :], AX.X, ALU.add).then_inc(total_done, 1)
                    dve.wait_ge(total_done, a + 1)
                    wait(dve, scaled, a)
                    nc.vector.reciprocal(rsum[:, :], total[:, :]).then_inc(rsum_done, 1)
            last.then_inc(ln_stats, 1)
            norm_tokens(1, h2)

            steps = [0]

            def router_next(ins):
                steps[0] += 1
                ins.then_inc(router_step, 1)
                dve.wait_ge(router_step, steps[0])

            def wide(v):
                return v.unsqueeze(2).to_broadcast([P, NF, EXPERTS])
            ranks = rank_sb[:, :].rearrange("p (f e) -> p f e", e=EXPERTS)
            best, alpha, m1, k1, m2, k2, rest = (small[:, k, :] for k in (0, 1, 2, 3, 4, 5, 6))
            dve.wait_ge(router_done, 1)
            router_next(nc.vector.tensor_copy(logits[:, :, :], ps[:, 4, 0:NF * (EXPERTS + 1)].rearrange("p (f e) -> p f e", e=EXPERTS + 1)))
            router_next(nc.vector.tensor_reduce(best, logits[:, :, 0:EXPERTS], AX.X, ALU.max))
            router_next(nc.vector.tensor_tensor(prob[:, :, :], logits[:, :, 0:EXPERTS], wide(best), ALU.subtract))
            dve.wait_ge(router_exp, 2)
            router_next(nc.vector.tensor_scalar(alpha, alpha, 1.0, None, ALU.add))
            router_next(nc.vector.reciprocal(alpha, alpha))
            for value, k, chosen, left in ((m1, k1, first, prob), (m2, k2, second, key)):
                router_next(nc.vector.tensor_reduce(value, left[:, :, :], AX.X, ALU.max))
                router_next(nc.vector.tensor_tensor(chosen[:, :, :], left[:, :, :], wide(value), ALU.is_ge))
                router_next(nc.vector.tensor_tensor(chosen[:, :, :], chosen[:, :, :], ranks, ALU.mult))
                router_next(nc.vector.tensor_reduce(k, chosen[:, :, :], AX.X, ALU.max))
                router_next(nc.vector.tensor_tensor(chosen[:, :, :], chosen[:, :, :], wide(k), ALU.is_equal))
                if chosen is first:
                    router_next(nc.vector.scalar_tensor_tensor(key[:, :, :], first[:, :, :], -2.0, prob[:, :, :], ALU.mult, ALU.add))
            router_next(nc.vector.tensor_tensor(rest, m1, m2, ALU.add))
            router_next(nc.vector.reciprocal(rest, rest))
            router_next(nc.vector.tensor_scalar(best, alpha, -1.0, 1.0, ALU.mult, ALU.add))
            router_next(nc.vector.tensor_tensor(rest, rest, best, ALU.mult))
            router_next(nc.vector.tensor_tensor(first[:, :, :], first[:, :, :], second[:, :, :], ALU.add))
            router_next(nc.vector.tensor_tensor(gates[:, :, :], first[:, :, :], prob[:, :, :], ALU.mult))
            router_next(nc.vector.tensor_tensor(gates[:, :, :], gates[:, :, :], wide(rest), ALU.mult))

            def gate_units(v):
                c, t = CHUNK_ORDER[v // 2], v % 2
                dve.wait_ge(silu_done, v + 1)
                nc.vector.tensor_tensor(hidden[:, c, HALF * t:HALF * t + HALF], ps[:, 2 * (v % 2) + 1, 0:HALF], silu[:, v % 2, :],
                                        ALU.mult).then_inc(hid_ready, 1)

            def add_down(d):
                for f in range(NF):
                    if f % 2 == 0:
                        dve.wait_ge(down_done, NF // 2 * d + f // 2 + 1)
                    if d == 0:
                        dve.wait_ge(h2_moved, 32)
                        weight = small[:, 1, f:f + 1]
                    else:
                        dve.wait_ge(acc_done, NF * (d - 1) + f + 1)
                        weight = gates[:, f, d - 1:d]
                    nc.vector.scalar_tensor_tensor(acc[:, f, :], ps[:, 4 + f // 2, E * (f % 2):E * (f % 2) + E], weight, acc[:, f, :],
                                                   ALU.mult, ALU.add).then_inc(acc_done, 1)
            for kind, k in FFN_ORDER:
                (gate_units if kind == "hidden" else add_down)(k)


def layout(a):
    f, b16 = np.float32, mybir.dt.np(BF16)
    w0 = a["L0_tok_conv_w0"][:, 0, :].T
    rows, pick = np.zeros((P, P), f), np.zeros((P, 3), f)
    for side in (0, 64):
        for section, term in enumerate((0, 1, 2, 0, 1, 0)):
            at = side + TAPS0 * section
            rows[at:at + TAPS0] = w0
            pick[at:at + TAPS0, term] = 1
    shift = np.zeros((GROW, SHIFT_AT + CHUNK_SAMPLES), f)
    for t in range(SECTIONS):
        for j in range(TAPS0):
            shift[TAPS0 * t + j, SHIFT_AT + STRIDE0 * t + j] = 1
    names = [f"ln_g{k}" for k in range(7)] + ["fln_g"] + [f"ln_b{k}" for k in range(7)] + ["fln_b"]

    def with_bias(w, bias):
        return np.concatenate([w, bias[None, :]])

    def by_head(w):
        out = np.zeros((w.shape[0], HEADS, 32), f)
        out[:, :, 0:HD] = w.reshape(w.shape[0], HEADS, HD)
        return out.reshape(w.shape[0], HEADS * 32)

    def beside(w, shared):
        w = np.concatenate([w.transpose(1, 0, 2).reshape(E, EXPERTS * E), shared], axis=1)
        return np.concatenate([w, np.zeros((1, w.shape[1]), f)])

    router = np.concatenate([a["L0_ffn_router_w"], a["L0_ffn_sg_w"]], axis=1)
    router_bias = np.concatenate([np.zeros(EXPERTS, f), a["L0_ffn_sg_b"]])
    down = np.zeros((P, DOWN_BLOCKS, E), f)
    routed = a["L0_ffn_w_down"].reshape(ROUTED_HC, P, E)
    for pair in range(EXPERTS // 2):
        down[:, 4 * pair] = routed[3 * pair]
        down[0:64, 4 * pair + 1] = routed[3 * pair + 1, 0:64]
        down[64:, 4 * pair + 2] = routed[3 * pair + 1, 64:]
        down[:, 4 * pair + 3] = routed[3 * pair + 2]
    down[:, 4 * (EXPERTS // 2):] = a["L0_ffn_ws_down"].reshape(HC - ROUTED_HC, P, E).transpose(1, 0, 2)
    same = (np.arange(TOK) // FRAMES % CLIPS_T)[None, :] == np.arange(CLIPS_T)[:, None]
    pick_clip = np.zeros((CLIPS_T, HEADS, 32), f)
    pick_clip[np.arange(CLIPS_T), :, HD + np.arange(CLIPS_T)] = 1
    pick_clip = pick_clip.reshape(CLIPS_T, HEADS * 32)
    wq = by_head(with_bias(a["L0_attn_Wq"].T, a["L0_attn_bq"]))
    wk = by_head(with_bias(a["L0_attn_Wk"].T, a["L0_attn_bk"]))
    wk[E] = np.where(pick_clip.any(axis=0), f(MASK), wk[E])
    wo = np.zeros((3, 4, 32, E), f)
    wo[:, :, 0:HD] = a["L0_attn_Wo"].T.reshape(3, 4, HD, E)
    wo[0, 0, HD] = a["L0_attn_bo"]
    return {
        "x": a["x"],
        "conv_w": np.concatenate([a[f"L0_tok_conv_w{k}"].transpose(1, 2, 0) for k in range(1, 7)], axis=1),
        "w0_rows": rows, "pick_term": pick, "shift": shift,
        "diagonal": np.kron(np.eye(SECTIONS, dtype=f), np.ones((TAPS0, TAPS0), f)),
        "columns": np.stack([a[f"L0_tok_{n}"] for n in names], axis=1),
        "ident": np.eye(P, dtype=f), "ident_b": np.eye(P, dtype=b16),
        "proj": a["L0_tok_proj_w"], "proj_b": np.tile(a["L0_tok_proj_b"], (TT, 1)),
        "wq": np.concatenate([wq, pick_clip]),
        "wk": np.concatenate([wk, np.where(pick_clip == 1, f(-MASK), f(0))]),
        "wv": with_bias(a["L0_attn_Wv"].T, a["L0_attn_bv"]),
        "wo": wo.reshape(3, P, E).transpose(1, 0, 2),
        "router": with_bias(router, router_bias),
        "gate": beside(a["L0_ffn_w_gate"], a["L0_ffn_ws_gate"]),
        "up": beside(a["L0_ffn_w_up"], a["L0_ffn_ws_up"]),
        "down": down,
        "token_rows": np.concatenate([np.ones((1, TOK), f), same.astype(f)]),
        "rank": np.tile(np.arange(EXPERTS, 0, -1, dtype=f), (P, NF)),
    }


def kernel(**inputs):
    import concourse.bacc as bacc
    from concourse.bass_utils import run_bass_kernel_spmd as run
    arrays = {k: np.ascontiguousarray(v) for k, v in layout({k: np.asarray(v) for k, v in inputs.items()}).items()}
    nc = bacc.Bacc("TRN2", target_bir_lowering=False, num_devices=1)
    ins = {k: nc.dram_tensor(f"in_{k}", v.shape, mybir.dt.from_np(v.dtype), kind="ExternalInput").ap()
           for k, v in arrays.items()}
    out = nc.dram_tensor("out", (TOK, E), F32, kind="ExternalOutput").ap()
    audio_tower(nc, **ins, out=out)
    r = run(nc, [{f"in_{k}": v for k, v in arrays.items()}], core_ids=[0])
    return r.results[0]["out"].reshape(CLIPS, FRAMES, E)
```

```python
from contextlib import ExitStack
from typing import NamedTuple

import concourse.bass as bass
import numpy as np
from concourse import mybir

F32 = mybir.dt.float32
BF16 = mybir.dt.bfloat16
F32R = mybir.dt.float32r
ALU = mybir.AluOpType
ACT = mybir.ActivationFunctionType
AX = mybir.AxisListType

P = 128
CLIPS, SAMPLES, FRAMES = 64, 4000, 12
TAPS0, STRIDE0 = 10, 5
HALF_START = 1920
HALF_SAMPLES = 2005
FIRST_SAMPLES = 205
CHUNK = 20
CHUNK_SAMPLES = STRIDE0 * (CHUNK - 1) + TAPS0
CHUNK_STEP = STRIDE0 * CHUNK
SHIFT_AT = (CHUNK // 6) * 6 * STRIDE0
ITERS = 10
RING0, RING1, STEP2 = 40, 20, 10
BATCH_T = 8
TAPS = {1: 3, 2: 3, 3: 3, 4: 3, 5: 2, 6: 2}
TILES = {3: 49, 4: 24, 5: 12, 6: 6}
BLOCK0 = {1: 0, 2: 3, 3: 6, 4: 9, 5: 12, 6: 14}
BLOCKS, EARLY_BLOCKS = 16, 6
EPS = 1e-5
E, HEADS, HD = 192, 12, 16
TOK = CLIPS * FRAMES
CLIPS_T = 8
TT, NT = 96, 8
MASK = -2.0 ** 100
T_ROWS = E - P + 1 + CLIPS_T
AT_OUT = 3 * TT
FT, NF = 128, 6
HALF = TOK // 2
EXPERTS = 8
HC, ROUTED_HC = 18, 12

SLOTS = [(1, 0, 4, 0), (2, 4, 4, 1), (1, 4, 4, 0), (2, 8, 2, 1),
         (1, 8, 4, 0), (1, 12, 4, 0), (2, 0, 4, 0), (1, 16, 4, 0)]
NS = len(SLOTS)
C1_SLOT = [0, 2, 4, 5, 7]
C2_FIRST, C2_MID, C2_LAST = 6, 1, 3
BANKS = 4
BATCH = {0: 1, 2: 2, 3: 3, 5: 4, 6: 5}
FIRST_SLOTS = [s for s in range(NS) if SLOTS[s][3] == 0]
CH_STAGE, CH_GRAM, CH_QUAD, CH_SPLIT = {0: 2, 3: 3}, {1: 2, 4: 3}, {2: 2, 5: 3}, {
    4: ((2, (0, 1)),), 5: ((2, (2, 3, 4)),), 7: ((3, (0, 1, 2, 3, 4)),)}
CH_RSTD = {2: (2, 0), 3: (2, 1), 5: (3, 0), 6: (3, 1)}
SPLIT_STEPS = 5
CONSTS = 5
SECTIONS = 6
GROW = SECTIONS * TAPS0

ATT_LOADS = 11
QKV_FIRST = 6
QKV_REST = (4, 3, 2, 1)
REST_BANK = [4, 5, 6, 7, 4, 5, 6, 7, 4, 7]
LN2_STEP = 10
FLN_PARTS = ((0, 4), (4, 6))

HIDDEN_SLOTS = 12
PIECES = 2
PIECE = HC * P // PIECES
CHUNK_ORDER = list(range(ROUTED_HC, HC)) + list(range(ROUTED_HC))
EARLY_UNITS = 4
UNITS = [(c, t) for t in range(2) for c in CHUNK_ORDER[:EARLY_UNITS]] + [
    (c, t) for c in CHUNK_ORDER[EARLY_UNITS:] for t in range(2)]
DOWN_BLOCKS = ROUTED_HC // 3 * 4 + HC - ROUTED_HC
DOWN = [(list(range(ROUTED_HC, HC)), list(range(DOWN_BLOCKS - (HC - ROUTED_HC), DOWN_BLOCKS)), 2 * (HC - ROUTED_HC))]
for _e in range(EXPERTS):
    _c, _b = 3 * (_e // 2) + _e % 2, 4 * (_e // 2) + 2 * (_e % 2)
    DOWN.append(([_c, _c + 1], [_b, _b + 1], 2 * (HC - ROUTED_HC) + 2 * (_c + 2)))


def hidden_slot(c):
    return c - ROUTED_HC if c >= ROUTED_HC else (c + HC - ROUTED_HC) % HIDDEN_SLOTS


def ffn_order():
    out, down = [], 0
    for v in range(2 * HC):
        out.append(("hidden", v))
        if down < len(DOWN) and DOWN[down][2] + 1 <= v:
            out.append(("down", down))
            down += 1
    return out + [("down", d) for d in range(down, len(DOWN))]


FFN_ORDER = ffn_order()


def number(i, s):
    if isinstance(i, int) and i == 0:
        return FIRST_SLOTS.index(s)
    return i * NS + (s - (NS - len(FIRST_SLOTS)))


class Group(NamedTuple):
    n: object
    layer: int
    inputs: list
    wrap: int
    out: object
    tiles: int
    bank: int
    par: int
    fed: tuple
    bank_free: object
    out_free: tuple
    batch: object


def group(i, s):
    first = isinstance(i, int) and i == 0
    if first and s not in FIRST_SLOTS:
        return None
    layer, t0, tiles, back = SLOTS[s]
    n = number(i, s)
    used = n - BANKS
    if first:
        used = n - BANKS if n >= BANKS else None
    at = n if first else s + len(FIRST_SLOTS)
    par, bank = at % 2, at % BANKS
    if layer == 1:
        q = t0 // 4
        inputs = [(2 * t - 2) % RING0 for t in range(t0, t0 + 4)]
        if q == 4:
            free = (number(i, C2_FIRST),)
        elif first:
            free = ()
        else:
            free = (number_before(i, C2_FIRST) if q == 0 else number(i, C2_MID if q < 3 else C2_LAST),)
        return Group(n, 1, inputs, RING0, t0, tiles, bank, par, (), used, free, 5 * i + q + 1)
    inputs = [(2 * m - 1) % RING1 for m in range(t0, t0 + tiles)]
    q = (2 * (t0 + tiles - 1) + 1) // 4
    fed = number(i, C1_SLOT[q]) if back == 0 else number_before(i, C1_SLOT[q])
    return Group(n, 2, inputs, RING1, (i - back) * STEP2 + t0, tiles, bank, par, (fed,), used, (), None)


def number_before(i, s):
    if isinstance(i, int):
        return number(i - 1, s)
    return i * NS + (s - (NS - len(FIRST_SLOTS)) - NS)


BEFORE_TAIL = len(FIRST_SLOTS) + NS * (ITERS - 1)


TAIL_TILES = {3: [4] * 11 + [3, 2], 4: [4] * 5 + [2, 2], 5: [4, 4, 2, 2], 6: [4, 1, 1]}


def tail():
    late = 4
    todo = [(2, 4, 4), (2, 8, 2)] + [(k, sum(TAIL_TILES[k][:j]), n) for k in (3, 4, 5, 6)
                                     for j, n in enumerate(TAIL_TILES[k])]
    made = {}
    for it in range(ITERS):
        for m in range(STEP2):
            s = C2_FIRST if m < 4 else (C2_MID if m < 8 else C2_LAST)
            if s == C2_FIRST or it < ITERS - 1:
                made[2, STEP2 * it + m] = number(it if s == C2_FIRST else it + 1, s)
    order = []
    while todo:
        best = None
        for k, (layer, t, tiles) in enumerate(todo):
            if any(z[0] == layer for z in todo[:k]):
                continue
            if layer == 2:
                need = number(ITERS - 1, C1_SLOT[3 if t == 4 else 4])
            else:
                top = 2 * (t + tiles - 1) + TAPS[layer] - 1 + (layer == 3)
                need = made.get((layer - 1, top))
            if need is None:
                continue
            age = BEFORE_TAIL + len(order) - need
            rank = (age >= late, layer if age >= late else age)
            if best is None or rank > best[0]:
                best = (rank, k, need)
        _, k, need = best
        layer, t, tiles = todo.pop(k)
        n = BEFORE_TAIL + len(order)
        base = STEP2 * (ITERS - 1) if layer == 2 else 0
        if layer == 2:
            inputs = [(2 * m - 1) % RING1 for m in range(t, t + tiles)]
        else:
            inputs = [2 * m + (layer == 3) for m in range(t, t + tiles)]
        order.append(Group(n, layer, inputs, RING1 if layer == 2 else 0, base + t, tiles,
                           n % BANKS, n % 2, (need,), n - BANKS, (), None))
        for m in range(tiles):
            made[layer, base + t + m] = n
    return order


TAIL = tail()
GROUPS = BEFORE_TAIL + len(TAIL)
FLN_BANK = [GROUPS % BANKS, (GROUPS + 1) % BANKS]
FLN_FED = [next(g.n for g in TAIL if g.layer == 6 and g.out + g.tiles >= b) for _, b in FLN_PARTS]


def back(i, s, d):
    if isinstance(i, int) and i == 0:
        at = FIRST_SLOTS.index(s) - d
        return group(0, FIRST_SLOTS[at]) if at >= 0 else None
    z = (s - d) % NS
    if z <= s:
        return group(i, z)
    if isinstance(i, int):
        return group(i - 1, z)
    g = group(i, z)
    less = lambda v: None if v is None else v - NS
    return g._replace(n=number_before(i, z), fed=tuple(map(less, g.fed)), bank_free=less(g.bank_free),
                      out_free=tuple(map(less, g.out_free)),
                      out=g.out - STEP2 if g.layer == 2 else g.out)


def audio_tower(nc: bass.Bass, x, conv_w, w0_rows, pick_term, diagonal, shift, columns, ident, ident_b, proj, proj_b, wq, wk, wv, wo,
                router, gate, up, down, token_rows, rank, out):
    with ExitStack() as ctx:
        def sb(name, shape, dt=F32):
            return ctx.enter_context(nc.sbuf_tensor(name, shape, dt))

        def sem(name):
            return ctx.enter_context(nc.semaphore(name))

        shared = sb("shared", [P, DOWN_BLOCKS * E])
        wd_sb = shared[:, :].rearrange("p (b e) -> p b e", e=E)
        cw = shared[:, 0:BLOCKS * P].rearrange("p (k c) -> p k c", c=P)
        x_sb = shared[:, BLOCKS * P:BLOCKS * P + HALF_SAMPLES]
        cmean = sb("cmean", [P, BLOCKS])
        w0 = sb("w0", [P, P])
        w0mean = sb("w0mean", [P, 1])
        w0rest = sb("w0rest", [P, P])
        w0term = sb("w0term", [P, 3, P], BF16)
        w0_stack = sb("w0_stack", [P, P], BF16)
        pick_sb = sb("pick_sb", [P, 3])
        w0T = sb("w0T", [P, GROW])
        diagonal_sb = sb("diagonal_sb", [GROW, GROW])
        gram = sb("gram", [GROW, GROW])
        shift_sb = sb("shift_sb", [GROW, SHIFT_AT + CHUNK_SAMPLES])
        table_warm = sb("table_warm", [P, 1])
        gband = sb("gband", [CHUNK_SAMPLES, CHUNK * TAPS0])
        col = sb("col", [P, 16])
        id_f = sb("id_f", [P, P])
        id_b = sb("id_b", [P, P], BF16)
        neg_half, eps = sb("neg_half", [P, CHUNK]), sb("eps", [P, 4])
        stage = sb("stage", [P, 2, CHUNK_SAMPLES])
        stageT = sb("stageT", [CHUNK_SAMPLES, P])
        quad = sb("quad", [P, CHUNK, TAPS0])
        var0 = sb("var0", [P, CHUNK])
        vare0 = sb("vare0", [P, CHUNK])
        rstd0 = sb("rstd0", [P, CHUNK])
        xs = sb("xs", [P, CHUNK, TAPS0])
        xrest = sb("xrest", [P, CHUNK, TAPS0])
        terms = sb("terms", [P, RING0, 64], BF16)
        termsT = sb("termsT", [P, 512], BF16)
        sq = sb("sq", [P, 2, 512])
        var = sb("var", [P, 2, 4])
        vare = sb("vare", [P, 2, 4])
        rstd = sb("rstd", [P, 2, 4])
        early = sb("early", [P, RING0 * P])
        x3 = sb("x3", [P, TILES[3] * P])
        x6 = sb("x6", [P, TILES[6] * P])

        proj_sb, proj_b_sb = sb("proj_sb", [P, E]), sb("proj_b_sb", [TT, E])
        wo_sb = sb("wo_sb", [P, 3, E])
        wq_sb, wk_sb, wv_sb, wr_sb = (
            (sb(n + "_a", [P, w]), sb(n + "_b", [T_ROWS if n in ("wq", "wk") else E - P + 1, w])) for n, w in
            (("wq", 3 * P), ("wk", 3 * P), ("wv", E), ("wr", EXPERTS + 1)))
        rank_sb = sb("rank_sb", [P, NF * EXPERTS])
        places = (("x1", RING1 * P), ("yn", 2 * 512), ("x2", HC * TOK), ("wg_a", HC * P), ("wg_b", HC * P),
                  ("wu_a", HC * P), ("wu_b", HC * P))
        with ExitStack() as first_use:
            x1, yn2, x2, wg_a, wg_b, wu_a, wu_b = (
                first_use.enter_context(nc.sbuf_tensor(n, [P, w], F32)) for n, w in places)
        x1_r, yn_r, x2_r, wg_a_r, wg_b_r, wu_a_r, wu_b_r = (sb(n + "_r", [P, w], F32R) for n, w in places)
        yn = yn2[:, :].rearrange("p (two c) -> p two c", two=2)
        acts = {0: early, 1: x1, 2: x2, 3: x3, 4: early[:, 0:TILES[4] * P],
                5: early[:, TILES[4] * P:(TILES[4] + TILES[5]) * P], 6: x6}

        stat, mv = sb("stat", [P, NT, 6]), sb("mv", [P, NT, 2])
        vtok, rtok = sb("vtok", [P, NT]), sb("rtok", [P, NT])
        nT = x3[:, 0:TOK]
        h1, h2 = (x3[0:TT, TOK + k * NT * E:TOK + (k + 1) * NT * E].rearrange("p (a e) -> p a e", e=E) for k in range(2))
        y = x3[0:TT, TOK + 2 * NT * E:TOK + 2 * NT * E + NT * 2 * P].rearrange("p (a e) -> p a e", e=2 * P)
        acc = early[:, 0:NF * E].rearrange("p (f e) -> p f e", e=E)
        qT = early[:, NF * E:NF * E + 3 * TOK].rearrange("p (c t) -> p c t", t=TOK)
        yT_a = early[:, NF * E + 3 * TOK:NF * E + 4 * TOK]
        yT_m = sb("yT_m", [T_ROWS, TOK])
        yT_b = yT_m[0:E - P + 1, :]
        kT = x1[:, 0:3 * TOK].rearrange("p (c t) -> p c t", t=TOK)
        att = x2[0:TT, 0:4 * HEADS * TT].rearrange("p (four h k) -> p four h k", four=4, k=TT)
        attT = x2[0:TT, 4 * HEADS * TT:5 * HEADS * TT].rearrange("p (h k) -> p h k", k=TT)
        vext = x2[0:TT, 5 * HEADS * TT:5 * HEADS * TT + NT * HEADS * 32].rearrange(
            "p (a h d) -> p a h d", h=HEADS, d=32)
        hidden = x2[:, 0:HIDDEN_SLOTS * TOK].rearrange("p (c t) -> p c t", t=TOK)
        gu_raw = ((wg_a, wg_b), (wu_a, wu_b))
        gu_high = [x2_r[:, HIDDEN_SLOTS * TOK + HC * P * k:HIDDEN_SLOTS * TOK + HC * P * (k + 1)] for k in range(2)]
        gu_low = [wg_a_r[:, :], wu_a_r[:, :]]
        gu_rest = [wg_b_r[:, :], wu_b_r[:, :]]
        rest_high = x2_r[:, 0:2 * HC * P].rearrange("p (k w) -> p k w", k=2)
        yT_high, yT_low, yT_rest = (x1_r[:, k * TOK:(k + 1) * TOK] for k in range(3))
        yT_rest_low = yn_r[0:E - P, :].rearrange("p (two c) -> p two c", two=2)[:, :, 0:HALF]
        top, total, rsum = sb("top", [TT, HEADS]), sb("total", [TT, HEADS]), sb("rsum", [TT, HEADS])
        logits = sb("logits", [P, NF, EXPERTS + 1])
        prob, key, first, second, gates = (sb(n, [P, NF, EXPERTS]) for n in ("prob", "key", "first", "second", "gates"))
        small = sb("small", [P, 8, NF])
        silu = sq[:, :, 0:HALF]

        ps = ctx.enter_context(nc.psum_tensor("ps", [P, 8, 512], F32))
        prod = [ps[:, b, :] for b in range(BANKS)]
        turn = ps[:, 4, :]
        c0_ps = ps[:, 5:7, :]
        chunk_ps = ps[:, 7, 0:CHUNK * TAPS0]
        term_ps = ps[:, 7, :].bitcast(BF16)[:, 512:]
        setup_ps = ps[:, 7, :]

        x_in, x_rest_in, w0_in, tables_in, cw_in, cw2_in, col_in = (sem(n) for n in ("x_in", "x_rest_in", "w0_in", "tables_in", "cw_in", "cw2_in", "col_in"))
        consts = sem("consts")
        w0_step = sem("w0_step")
        w0_turned, gram_made, gband_made, gband_ready = (
            sem(n) for n in ("w0_turned", "gram_made", "gband_made", "gband_ready"))
        cmean_step, cw_ready = sem("cmean_step"), sem("cw_ready")
        staged, stage_turned, stage_copied, gram_x = (
            sem(n) for n in ("staged", "stage_turned", "stage_copied", "gram_x"))
        quad_made, var0_made, vare0_made, rstd0_made, split_step = (
            sem(n) for n in ("quad_made", "var0_made", "vare0_made", "rstd0_made", "split_step"))
        terms_turned, terms_copied, conv0_done, act0_done = (
            sem(n) for n in ("terms_turned", "terms_copied", "conv0_done", "act0_done"))
        conv_done, sq_done, var_done, rstd_step, rstd_done, norm_done, turned, act_done = (
            sem(n) for n in ("conv_done", "sq_done", "var_done", "rstd_step", "rstd_done", "norm_done",
                             "turned", "act_done"))
        proj_in, att_in, ffn_in, down_in = (sem(n) for n in ("proj_in", "att_in", "ffn_in", "down_in"))
        fln_turned, fln_stats, fln_norm, fln_back, fln_done = (
            sem(n) for n in ("fln_turned", "fln_stats", "fln_norm", "fln_back", "fln_done"))
        v_ones, tok_var, tok_rstd = sem("v_ones"), sem("tok_var"), sem("tok_rstd")
        proj_done, h1_ready, h2_ready = sem("proj_done"), sem("h1_ready"), sem("h2_ready")
        ln_stats, ln_norm, ln_turned, yTa_ready, yTb_ready = (
            sem(n) for n in ("ln_stats", "ln_norm", "ln_turned", "yTa_ready", "yTb_ready"))
        qkv_done, qk_by_act, qk_by_dve, rest_copied = (
            sem(n) for n in ("qkv_done", "qk_by_act", "qk_by_dve", "rest_copied"))
        scores_done, top_done, shifted, exp_done = (sem(n) for n in ("scores_done", "top_done", "shifted", "exp_done"))
        total_done, rsum_done, scaled, att_turned, att_copied, values_done, values_copied = (
            sem(n) for n in ("total_done", "rsum_done", "scaled", "att_turned", "att_copied", "values_done",
                             "values_copied"))
        out_done = sem("out_done")
        router_done, router_step, router_exp, gates_ready = (
            sem(n) for n in ("router_done", "router_step", "router_exp", "gates_ready"))
        h2_moved = sem("h2_moved")
        high_made, rest_high_made, low_made = sem("high_made"), sem("rest_high_made"), sem("low_made")
        yT_high_made, yT_rest_made, yT_low_made = sem("yT_high_made"), sem("yT_rest_made"), sem("yT_low_made")
        hid_done, silu_done, hid_ready = sem("hid_done"), sem("silu_done"), sem("hid_ready")
        down_done, acc_done = sem("down_done"), sem("acc_done")
        stored = sem("stored")

        def window(c):
            s = stage[:, c, :]
            return bass.AP(tensor=s.tensor, offset=s.offset, ap=[list(s.ap[0]), [STRIDE0, CHUNK], [1, TAPS0]])

        def tiles(buf, first, n):
            return buf[:, bass.ds(first * P, n * P)] if not isinstance(first, int) else buf[:, first * P:(first + n) * P]

        def wait(eng, s, value):
            if not isinstance(value, int) or value > 0:
                eng.wait_ge(s, value)

        def qkv_group(g):
            if g < QKV_FIRST:
                return "qk"[g // 3], g % 3, 0, (4, 5, 6, 7, 0, 2)[g]
            k = g - QKV_FIRST
            return ("qk"[k // 3], k % 3, 1, REST_BANK[k]) if k < 6 else ("v", k - 6, None, REST_BANK[k])

        def qkv_copy(g, copy):
            what, c, t, b = qkv_group(g)
            if what != "v":
                return copy((qT if what == "q" else kT)[:, c, HALF * t:HALF * t + HALF], ps[:, b, 0:HALF])
            return copy(vext[:, 2 * c:2 * c + 2, :, 0:HD],
                        ps[0:TT, b, 0:2 * E].rearrange("p (a h d) -> p a h d", h=HEADS, d=HD))

        def attn_out(a):
            return ps[0:TT, 7, AT_OUT:AT_OUT + E] if a < 3 else ps[0:TT, 2 + a % 2, 0:E]

        moved = nc.dram_tensor("moved", (TOK, E), F32).ap()
        W0_SPLIT = 10
        block = ctx.enter_context(nc.Block())

        @block.sync
        def _(sp):
            def samples(lo, hi, arrived):
                for h in range(2):
                    sp.dma_start(x_sb[64 * h:64 * h + 64, lo:hi], x[:, HALF_START * h + lo:HALF_START * h + hi]).then_inc(arrived, 16)
            for t, src in ((w0, w0_rows), (id_f, ident)):
                sp.dma_start(t[:, :], src).then_inc(w0_in, 16)
            samples(0, FIRST_SAMPLES, x_in)
            for t, src in ((diagonal_sb, diagonal), (shift_sb, shift), (pick_sb, pick_term), (id_b, ident_b)):
                sp.dma_start(t[:, :], src).then_inc(tables_in, 16)
            sp.dma_start(cw[:, 0:EARLY_BLOCKS, :], conv_w[:, 0:EARLY_BLOCKS, :]).then_inc(cw_in, 16)
            sp.dma_start(col[:, :], columns).then_inc(col_in, 16)
            samples(FIRST_SAMPLES, HALF_SAMPLES, x_rest_in)
            sp.dma_start(cw[:, EARLY_BLOCKS:, :], conv_w[:, EARLY_BLOCKS:, :]).then_inc(cw2_in, 16)
            for t, src in ((proj_sb, proj), (proj_b_sb, proj_b)):
                sp.dma_start(t[:, :], src).then_inc(proj_in, 16)
            for pair, src in ((wq_sb, wq), (wk_sb, wk), (wv_sb, wv), (wr_sb, router)):
                sp.dma_start(pair[0][:, :], src[0:P, :]).then_inc(att_in, 16)
                sp.dma_start(pair[1][:, :], src[P:, :]).then_inc(att_in, 16)
            for t, src in ((wo_sb[:, :, :], wo), (yT_m[E - P:, :], token_rows), (rank_sb[:, :], rank)):
                sp.dma_start(t, src).then_inc(att_in, 16)
            for pair, src in (((wg_a, wg_b), gate), ((wu_a, wu_b), up)):
                sp.dma_start(pair[0][:, :], src[0:P, :]).then_inc(ffn_in, 16)
                sp.dma_start(pair[1][:, :], src[P:, :]).then_inc(ffn_in, 16)
            sp.wait_ge(act_done, GROUPS)
            sp.dma_start(wd_sb, down).then_inc(down_in, 16)
            sp.wait_ge(h2_ready, NT)
            sp.dma_start(moved.rearrange("(a p) e -> p a e", p=TT), h2).then_inc(h2_moved, 16)
            sp.wait_ge(h2_moved, 16)
            sp.dma_start(acc, moved.rearrange("(f p) e -> p f e", p=FT)).then_inc(h2_moved, 16)
            for k in range(NF // 2):
                sp.wait_ge(acc_done, NF * EXPERTS + 2 * (k + 1))
                sp.dma_start(out.rearrange("(f p) e -> p f e", p=FT)[:, 2 * k:2 * k + 2, :],
                             acc[:, 2 * k:2 * k + 2, :]).then_inc(stored, 16)
            sp.wait_ge(stored, 16 * (NF // 2))

        @block.tensor
        def _(pe):
            def keep_clock(n, bank):
                for _ in range(n):
                    nc.tensor.matmul(ps[:, bank, 0:P], id_f[:, :], id_f[:, :], start=True, stop=True)

            def chunk_turn(c, par):
                pe.wait_ge(staged, c + 1)
                wait(pe, quad_made, c)
                nc.tensor.transpose(chunk_ps[0:CHUNK_SAMPLES, 0:P], stage[:, par, :], id_f[:, :]).then_inc(stage_turned, 1)

            def chunk_gram(c):
                pe.wait_ge(stage_copied, c + 1)
                nc.tensor.matmul(chunk_ps[:, :], stageT[:, :], gband[:, :],
                                 start=True, stop=True).then_inc(gram_x, 1)

            def batch_turn(b, m, chunks, read):
                pe.wait_ge(split_step, SPLIT_STEPS * chunks)
                pe.wait_ge(quad_made, read)
                wait(pe, terms_copied, m)
                t0 = BATCH_T * (b % 5)
                for k in range(BATCH_T // 2):
                    last = nc.tensor.transpose(term_ps[:, P * k:P * k + P],
                                               terms[:, t0 + 2 * k:t0 + 2 * k + 2, :].rearrange("p t k -> p (t k)"), id_b[:, :])
                last.then_inc(terms_turned, 1)

            def batch_multiply(m):
                pe.wait_ge(terms_copied, m + 1)
                wait(pe, act0_done, m)
                nc.tensor.matmul(c0_ps[:, 0, :], w0_stack[0:64, :], termsT[0:64, :], start=True, stop=True)
                nc.tensor.matmul(c0_ps[:, 1, :], w0_stack[64:128, :], termsT[64:128, :],
                                 start=True, stop=True).then_inc(conv0_done, 1)

            def multiply(g, between=None):
                if g.batch is not None:
                    pe.wait_ge(act0_done, g.batch)
                for n in g.fed:
                    pe.wait_ge(act_done, n + 1)
                if g.bank_free is not None:
                    pe.wait_ge(norm_done, g.bank_free + 1)
                src, taps = acts[g.layer - 1], TAPS[g.layer]
                for t, first in enumerate(g.inputs):
                    if between is not None and t == g.tiles // 2:
                        batch_turn(*between)
                    for k in range(taps):
                        at = (first + k) % g.wrap if g.wrap else first + k
                        last = nc.tensor.matmul(prod[g.bank][:, P * t:P * t + P], src[:, P * at:P * at + P],
                                                cw[:, BLOCK0[g.layer] + k, :], start=(k == 0), stop=(k == taps - 1))
                last.then_inc(conv_done, 1)

            def turn_group(g):
                pe.wait_ge(norm_done, g.n + 1)
                wait(pe, act_done, g.n)
                for t in range(g.tiles):
                    last = nc.tensor.transpose(turn[:, P * t:P * t + P], yn[:, g.par, P * t:P * t + P], id_f[:, :])
                last.then_inc(turned, 1)

            def step(i, s, last):
                m = 5 * i + BATCH[s] if s in BATCH and not (last and BATCH[s] == 5) else None
                between = None
                if m is not None:
                    b = BATCH[s]
                    read = 2 if last else 2 + sum(z < s for z in CH_GRAM)
                    between = (b, m, 2 * i + (1 if b < 2 else 2 if b < 5 else 3), 2 * i + read)
                g = group(i, s)
                if g is None and m is not None:
                    batch_turn(*between)
                if g is not None:
                    multiply(g, between)
                    g2 = back(i, s, 2)
                    if g2 is not None:
                        turn_group(g2)
                if m is not None:
                    batch_multiply(m)
                if not last:
                    if s in CH_STAGE:
                        chunk_turn(2 * i + CH_STAGE[s], CH_STAGE[s] % 2)
                    if s in CH_GRAM:
                        chunk_gram(2 * i + CH_GRAM[s])

            pe.wait_ge(w0_in, 2 * 16)
            pe.wait_ge(w0_step, 3)
            nc.tensor.transpose(setup_ps[:, 0:GROW], w0[0:GROW, :], id_f[0:GROW, 0:GROW]).then_inc(w0_turned, 1)
            pe.wait_ge(gram_made, 1)
            nc.tensor.matmul(setup_ps[0:GROW, 64:64 + GROW], w0T[:, :], w0T[:, :], start=True, stop=True).then_inc(w0_turned, 1)
            pe.wait_ge(gram_made, 2)
            for t in range(0, CHUNK, SECTIONS):
                at, n = SHIFT_AT - STRIDE0 * t, TAPS0 * min(SECTIONS, CHUNK - t)
                last = nc.tensor.matmul(setup_ps[0:CHUNK_SAMPLES, P + TAPS0 * t:P + TAPS0 * t + n],
                                        shift_sb[0:n, at:at + CHUNK_SAMPLES], gram[0:n, 0:n], start=True, stop=True)
            last.then_inc(gband_made, 1)
            pe.wait_ge(gband_ready, 1)
            chunk_turn(0, 0)
            chunk_gram(0)
            chunk_turn(1, 1)
            chunk_gram(1)
            keep_clock(10, 0)
            pe.wait_ge(w0_step, W0_SPLIT)
            batch_turn(0, 0, 1, 2)
            batch_multiply(0)
            keep_clock(4, 0)
            pe.wait_ge(consts, CONSTS)
            pe.wait_ge(cw_ready, 1)
            for s in range(NS):
                step(0, s, False)
            with pe.Fori(1, ITERS - 1) as i:
                for s in range(NS):
                    step(i, s, False)
            for s in range(NS):
                step(ITERS - 1, s, True)
            pe.wait_ge(cw_ready, 2)
            turned_to = BEFORE_TAIL - 2
            every = [group(ITERS - 1, NS - 2), group(ITERS - 1, NS - 1)] + TAIL
            for k, g in enumerate(TAIL):
                while turned_to <= max(g.fed):
                    turn_group(every[turned_to - BEFORE_TAIL + 2])
                    turned_to += 1
                multiply(g)
                if g.n >= GROUPS - 5:
                    keep_clock(4, 7)
                while turned_to <= g.n - 2:
                    turn_group(every[turned_to - BEFORE_TAIL + 2])
                    turned_to += 1
            while turned_to < GROUPS - 1:
                turn_group(every[turned_to - BEFORE_TAIL + 2])
                turned_to += 1

            def turn_frames(part):
                pe.wait_ge(act_done, FLN_FED[part] + 1)
                pe.wait_ge(norm_done, GROUPS - BANKS + part + 1)
                a, b = FLN_PARTS[part]
                for j in range(a, b):
                    last = nc.tensor.transpose(ps[:, FLN_BANK[part], P * (j - a):P * (j - a) + P], x6[:, P * j:P * j + P], id_f[:, :])
                last.then_inc(fln_turned, 1)
            keep_clock(5, 7)
            turn_group(TAIL[-1])
            turn_frames(0)
            turn_frames(1)
            keep_clock(12, 7)
            for part, (a, b) in enumerate(FLN_PARTS):
                pe.wait_ge(fln_norm, part + 1)
                for j in range(a, b):
                    last = nc.tensor.transpose(ps[:, 5 + part, P * (j - a):P * (j - a) + P],
                                               sq[:, part, P * (j - a):P * (j - a) + P], id_f[:, :])
                last.then_inc(fln_back, 1)
            keep_clock(6, 7)
            pe.wait_ge(fln_done, 2)
            pe.wait_ge(proj_in, 32)
            for a in range(NT):
                o = ps[0:TT, 4 + a // 2, E * (a % 2):E * (a % 2) + E]
                last = nc.tensor.matmul(o, nT[:, TT * a:TT * a + TT], proj_sb[:, :], start=True, stop=True)
                if a % 2:
                    last.then_inc(proj_done, 1)

            def turn_tokens(which, t, bank_a, bank_b):
                pe.wait_ge(ln_norm, NT * which + 4 * (t + 1))
                for a in range(4 * t, 4 * t + 4):
                    at = TT * (a % 4)
                    nc.tensor.transpose(ps[:, bank_a, at:at + TT], y[:, a, 0:P], id_f[0:TT, 0:TT])
                    rest = (E - P) * (which + 1)
                    last = nc.tensor.transpose(ps[0:rest, bank_b, at:at + TT], y[:, a, P:P + rest], id_f[0:TT, 0:TT])
                last.then_inc(ln_turned, 1)

            def qkv(g):
                what, c, t, b = qkv_group(g)
                o = ps[:, b, :]
                if what != "v":
                    w = wq_sb if what == "q" else wk_sb
                    tok = slice(HALF * t, HALF * t + HALF)
                    nc.tensor.matmul(o[:, 0:HALF], w[0][:, P * c:P * c + P], yT_a[:, tok], start=True, stop=False)
                    last = nc.tensor.matmul(o[:, 0:HALF], w[1][:, P * c:P * c + P], yT_m[:, tok], start=False, stop=True)
                else:
                    for a in (2 * c, 2 * c + 1):
                        v = o[0:TT, E * (a % 2):E * (a % 2) + E]
                        nc.tensor.matmul(v, yT_a[:, TT * a:TT * a + TT], wv_sb[0][:, :], start=True, stop=False)
                        last = nc.tensor.matmul(v, yT_b[:, TT * a:TT * a + TT], wv_sb[1][:, :], start=False, stop=True)
                last.then_inc(qkv_done, 1)

            pe.wait_ge(att_in, ATT_LOADS * 16)
            keep_clock(16, 3)
            turn_tokens(0, 0, 0, 2)
            keep_clock(3, 3)
            pe.wait_ge(h1_ready, NT // 2)
            pe.wait_ge(yTa_ready, 1)
            pe.wait_ge(yTb_ready, 1)
            for g in range(QKV_FIRST):
                if g == 3:
                    turn_tokens(0, 1, 1, 3)
                qkv(g)
            pe.wait_ge(qk_by_act, QKV_FIRST // 2)
            pe.wait_ge(qk_by_dve, QKV_FIRST // 2)
            pe.wait_ge(yTa_ready, 2)
            pe.wait_ge(yTb_ready, 2)
            for step_a in range(NT + 5):
                a = step_a
                if a < NT:
                    if a == NT // 2:
                        pe.wait_ge(rest_copied, 6)
                    tok = slice(TT * a, TT * a + TT)
                    for half in range(2):
                        wait(pe, shifted, 2 * a - 1 + half)
                        for c in range(3):
                            for r in (2 * half, 2 * half + 1):
                                last = nc.tensor.matmul(ps[0:TT, r, TT * c:TT * c + TT], qT[32 * r:32 * r + 32, c, tok],
                                                        kT[32 * r:32 * r + 32, c, tok], start=True, stop=True)
                        last.then_inc(scores_done, 1)
                if step_a < len(QKV_REST):
                    first = sum(QKV_REST[:step_a])
                    for k in range(first, first + QKV_REST[step_a]):
                        before = [j + 1 for j in range(k) if REST_BANK[j] == REST_BANK[k]]
                        wait(pe, rest_copied, before[-1] if before else 0)
                        qkv(QKV_FIRST + k)
                a = step_a - 5
                if a >= 0:
                    pe.wait_ge(values_copied, a + 1)
                    if a == 3:
                        pe.wait_ge(shifted, 2 * NT)
                    elif a > 4:
                        pe.wait_ge(h2_ready, a - 1)
                    for c in range(3):
                        last = nc.tensor.matmul(attn_out(a), qT[:, c, TT * a:TT * a + TT], wo_sb[:, c, :],
                                                start=(c == 0), stop=(c == 2))
                    last.then_inc(out_done, 1)
                if step_a == LN2_STEP + 1:
                    pe.wait_ge(shifted, 2 * NT)
                    turn_tokens(1, 0, 0, 1)
                a = step_a - 3
                if 0 <= a < NT:
                    pe.wait_ge(scaled, a + 1)
                    if a == 0:
                        pe.wait_ge(rest_copied, sum(b != 7 or k < 8 for k, b in enumerate(REST_BANK)))
                    wait(pe, att_copied, a)
                    for h in range(HEADS):
                        last = nc.tensor.transpose(ps[0:TT, 4 + h // 4, TT * (h % 4):TT * (h % 4) + TT],
                                                   att[:, a % 4, h, :], id_f[0:TT, 0:TT])
                    last.then_inc(att_turned, 1)
                a = step_a - 4
                if 0 <= a < NT:
                    pe.wait_ge(att_copied, a + 1)
                    wait(pe, values_copied, a)
                    if 0 < a <= 3:
                        pe.wait_ge(h2_ready, a)
                    if a == 0:
                        pe.wait_ge(rest_copied, sum(QKV_REST))
                    for h in range(HEADS):
                        r, c = h // 3, h % 3
                        last = nc.tensor.matmul(ps[32 * r:32 * r + 32, 7, TT * c:TT * c + TT], vext[:, a, 4 * c + r, :],
                                                attT[:, h, :], start=True, stop=True)
                    last.then_inc(values_done, 1)
            def hidden_units(v):
                c, t = UNITS[v]
                wait(pe, hid_ready, v - 1)
                tok = slice(HALF * t, HALF * t + HALF)
                for k in range(2):
                    o, w = ps[:, 2 * (v % 2) + k, 0:HALF], slice(P * c, P * c + P)
                    nc.tensor.matmul(o, gu_high[k][:, w], yT_high[:, tok], start=True, stop=False)
                    nc.tensor.matmul(o, gu_low[k][:, w], yT_high[:, tok], start=False, stop=False)
                    nc.tensor.matmul(o, gu_high[k][:, w], yT_low[:, tok], start=False, stop=False)
                    nc.tensor.matmul(o, gu_rest[k][:, w], yT_rest[:, tok], start=False, stop=False)
                    last = nc.tensor.matmul(o, gu_rest[k][0:E - P, w], yT_rest_low[:, t, :], start=False, stop=True)
                last.then_inc(hid_done, 1)

            def down_products(d):
                chunks, blocks, need = DOWN[d]
                pe.wait_ge(hid_ready, need)
                for f in range(NF):
                    if f % 2 == 0:
                        if d == 0:
                            pe.wait_ge(router_step, 1)
                        else:
                            pe.wait_ge(acc_done, NF * (d - 1) + f + 2)
                    o = ps[:, 4 + f // 2, E * (f % 2):E * (f % 2) + E]
                    for k, (c, b) in enumerate(zip(chunks, blocks)):
                        last = nc.tensor.matmul(o, hidden[:, hidden_slot(c), FT * f:FT * f + FT], wd_sb[:, b, :],
                                                start=(k == 0), stop=(k == len(chunks) - 1))
                    if f % 2:
                        last.then_inc(down_done, 1)
            pe.wait_ge(yT_low_made, 1)
            pe.wait_ge(low_made, 4 * PIECES)
            pe.wait_ge(high_made, 2 * PIECES)
            pe.wait_ge(rest_high_made, 4 * PIECES)
            for v in range(EARLY_UNITS - 1):
                if v == 1:
                    pe.wait_ge(h2_ready, NT)
                hidden_units(v)
            pe.wait_ge(att_copied, NT)
            turn_tokens(1, 1, 4, 5)
            hidden_units(EARLY_UNITS - 1)
            pe.wait_ge(yTa_ready, 4)
            pe.wait_ge(yTb_ready, 4)
            pe.wait_ge(yT_low_made, 2)
            for f in range(NF):
                o = ps[:, 6, (EXPERTS + 1) * f:(EXPERTS + 1) * (f + 1)]
                nc.tensor.matmul(o, yT_a[:, FT * f:FT * f + FT], wr_sb[0][:, :], start=True, stop=False)
                last = nc.tensor.matmul(o, yT_b[:, FT * f:FT * f + FT], wr_sb[1][:, :], start=False, stop=True)
            last.then_inc(router_done, 1)
            pe.wait_ge(down_in, 16)
            for kind, k in FFN_ORDER[EARLY_UNITS:]:
                (hidden_units if kind == "hidden" else down_products)(k)

        @block.scalar
        def _(act):
            def square(g):
                act.wait_ge(conv_done, g.n + 1)
                wait(act, var_done, g.n - 1)
                nc.scalar.activation(sq[:, g.par, 0:g.tiles * P], prod[g.bank][:, 0:g.tiles * P], ACT.Square,
                                     scale=P ** -0.5).then_inc(sq_done, 1)

            def gelu(g):
                act.wait_ge(turned, g.n + 1)
                for n in g.out_free:
                    act.wait_ge(conv_done, n + 1)
                nc.scalar.activation(tiles(acts[g.layer], g.out, g.tiles), turn[:, 0:g.tiles * P], ACT.Gelu,
                                     bias=col[:, 8 + g.layer:9 + g.layer], scale=col[:, g.layer:g.layer + 1]).then_inc(act_done, 1)

            def gelu0(b, m, free):
                act.wait_ge(conv0_done, m + 1)
                if free is not None:
                    act.wait_ge(conv_done, free + 1)
                t0 = BATCH_T * (b % 5)
                ring = early[:, t0 * P:(t0 + BATCH_T) * P].rearrange("p (k two l) -> p two k l", two=2, l=P)
                nc.scalar.activation(ring, c0_ps[:, :, :].rearrange("p two (k l) -> p two k l", l=P), ACT.Gelu,
                                     bias=col[:, 8:9], scale=col[:, 0:1]).then_inc(act0_done, 1)

            def step(i, s, last):
                g = group(i, s)
                if g is not None and (g1 := back(i, s, 1)) is not None:
                    square(g1)
                if g is not None and (g3 := back(i, s, 3)) is not None:
                    gelu(g3)
                z = s - 1
                if z in BATCH and not (last and BATCH[z] == 5):
                    b = BATCH[z]
                    if b == 5:
                        free = number(i, C1_SLOT[1])
                    elif b == 4:
                        free = number(i, C1_SLOT[0])
                    else:
                        free = None if isinstance(i, int) and i == 0 else number_before(i, C1_SLOT[b + 1])
                    gelu0(b, 5 * i + b, free)

            act.wait_ge(consts, CONSTS)
            nc.scalar.activation(table_warm[:, :], neg_half[:, 0:1], ACT.Gelu)
            act.wait_ge(col_in, 16)
            gelu0(0, 0, None)
            for s in range(NS):
                step(0, s, False)
            with act.Fori(1, ITERS - 1) as i:
                for s in range(NS):
                    step(i, s, False)
            for s in range(NS):
                step(ITERS - 1, s, True)
            squared, acted = BEFORE_TAIL - 1, BEFORE_TAIL - 3
            every = [group(ITERS - 1, NS - 3 + k) for k in range(3)] + TAIL
            for g in TAIL:
                while squared < g.n:
                    square(every[squared - BEFORE_TAIL + 3])
                    squared += 1
                while acted <= max(max(g.fed), g.n - 3):
                    gelu(every[acted - BEFORE_TAIL + 3])
                    acted += 1
            square(TAIL[-1])
            while acted < GROUPS:
                gelu(every[acted - BEFORE_TAIL + 3])
                acted += 1


            act.wait_ge(conv_done, GROUPS)
            act.wait_ge(ffn_in, 64)
            for k in range(2):
                for p in range(PIECES):
                    w = slice(PIECE * p, PIECE * (p + 1))
                    nc.scalar.activation(gu_high[k][:, w], gu_raw[k][0][:, w], ACT.Copy).then_inc(high_made, 1)

            ordered = nT.rearrange("p (b h j) -> p j h b", h=2, j=6)
            for part, (a, b) in enumerate(FLN_PARTS):
                act.wait_ge(fln_back, part + 1)
                for j in range(a, b):
                    last = nc.scalar.activation(ordered[:, j, :, :],
                                                ps[:, 5 + part, P * (j - a):P * (j - a) + P].rearrange("p (h b) -> p h b", h=2),
                                                ACT.Identity, bias=col[:, 15:16], scale=col[:, 7:8])
                last.then_inc(fln_done, 1)

            low, high = slice(E - P, 2 * (E - P)), slice(0, E - P)
            for rows in (low, high):
                for k in range(2):
                    for p in range(PIECES):
                        w = slice(PIECE * p, PIECE * (p + 1))
                        nc.scalar.activation(rest_high[low, k, w] if rows is low else gu_rest[k][high, w],
                                             gu_raw[k][1][rows, w], ACT.Copy).then_inc(rest_high_made, 1)

            def copy_tokens(which, t, bank):
                tok = slice(HALF * t, HALF * t + HALF)
                act.wait_ge(ln_turned, 2 * which + t + 1)
                nc.scalar.activation(yT_a[:, tok], ps[:, bank, 0:HALF], ACT.Copy).then_inc(yTa_ready, 1)
                if which == 1:
                    nc.scalar.activation(yT_high[:, tok], ps[:, bank, 0:HALF], ACT.Copy).then_inc(yT_high_made, 1)
                    act.wait_ge(yTb_ready, 2 + t + 1)
                    nc.scalar.activation(yT_rest[:, tok], ps[:, bank + 1, 0:HALF], ACT.Copy).then_inc(yT_rest_made, 1)

            def copy_group(g, copied):
                act.wait_ge(qkv_done, g + 1)
                qkv_copy(g, lambda o, i: nc.scalar.activation(o, i, ACT.Copy)).then_inc(copied, 1)
            copy_tokens(0, 0, 0)
            copy_group(0, qk_by_act)
            copy_group(2, qk_by_act)
            copy_tokens(0, 1, 1)
            copy_group(4, qk_by_act)
            for step_a in range(NT + 5):
                if step_a < len(QKV_REST):
                    first = sum(QKV_REST[:step_a])
                    for k in range(first, first + QKV_REST[step_a]):
                        if k == 6:
                            act.wait_ge(v_ones, 1)
                        copy_group(QKV_FIRST + k, rest_copied)
                if step_a == LN2_STEP + 1:
                    copy_tokens(1, 0, 0)
                a = step_a - 4
                if 0 <= a < NT:
                    act.wait_ge(values_done, a + 1)
                    nc.scalar.activation(qT[:, :, TT * a:TT * a + TT], ps[:, 7, 0:3 * TT].rearrange("p (c t) -> p c t", t=TT),
                                         ACT.Copy).then_inc(values_copied, 1)
                a = step_a - 3
                if 0 <= a < NT:
                    act.wait_ge(att_turned, a + 1)
                    wait(act, values_done, a)
                    nc.scalar.activation(attT[:, :, :].rearrange("p (b h) k -> p b (h k)", b=3), ps[0:TT, 4:7, 0:4 * TT],
                                         ACT.Copy).then_inc(att_copied, 1)
                a = step_a
                if a < NT:
                    act.wait_ge(shifted, 2 * a + 2)
                    nc.scalar.activation(att[:, a % 4, :, :], att[:, a % 4, :, :], ACT.Exp, scale=HD ** -0.5).then_inc(exp_done, 1)

            def silu_unit(v):
                act.wait_ge(hid_done, v + 1)
                wait(act, hid_ready, v - 1)
                nc.scalar.activation(silu[:, v % 2, :], ps[:, 2 * (v % 2), 0:HALF], ACT.Silu).then_inc(silu_done, 1)
            for v in range(EARLY_UNITS - 1):
                silu_unit(v)
            copy_tokens(1, 1, 4)
            silu_unit(EARLY_UNITS - 1)
            act.wait_ge(router_step, 3)
            nc.scalar.activation(prob[:, :, :], prob[:, :, :], ACT.Exp).then_inc(router_exp, 1)
            nc.scalar.activation(small[:, 1, :], logits[:, :, EXPERTS], ACT.Exp, scale=-1.0).then_inc(router_exp, 1)
            for v in range(EARLY_UNITS, 2 * HC):
                silu_unit(v)

        @block.gpsimd
        def _(pool):
            def stage_chunk(c, par):
                wait(pool, split_step, SPLIT_STEPS * (c - 2) + 1)
                pool.tensor_copy(stage[:, par, :], x_sb[:, bass.ds(c * CHUNK_STEP, CHUNK_SAMPLES)]
                                 if not isinstance(c, int) else x_sb[:, c * CHUNK_STEP:c * CHUNK_STEP + CHUNK_SAMPLES]).then_inc(staged, 1)

            def rstd_chunk(c, half):
                pool.wait_ge(vare0_made, c + 1)
                wait(pool, split_step, SPLIT_STEPS * (c - 1) + 1)
                v = slice(CHUNK // 2 * half, CHUNK // 2 * (half + 1))
                pool.tensor_tensor(rstd0[:, v], vare0[:, v], neg_half[:, v], ALU.pow).then_inc(rstd0_made, 1)

            def rstd_group(g):
                pool.wait_ge(var_done, g.n + 1)
                t = g.tiles
                pool.tensor_tensor(vare[:, g.par, 0:t], var[:, g.par, 0:t], eps[:, 0:t], ALU.add).then_inc(rstd_step, 1)
                pool.wait_ge(rstd_step, g.n + 1)
                wait(pool, norm_done, g.n - 1)
                pool.tensor_tensor(rstd[:, g.par, 0:t], vare[:, g.par, 0:t], neg_half[:, 0:t], ALU.pow).then_inc(rstd_done, 1)

            def step(i, s, last):
                if not last and s in CH_STAGE:
                    stage_chunk(2 * i + CH_STAGE[s], CH_STAGE[s] % 2)
                if group(i, s) is not None and (g1 := back(i, s, 1)) is not None:
                    rstd_group(g1)
                if not last and s in CH_RSTD:
                    rstd_chunk(2 * i + CH_RSTD[s][0], CH_RSTD[s][1])

            pool.memset(neg_half[:, :], -0.5).then_inc(consts, 1)
            pool.memset(eps[:, :], EPS).then_inc(consts, 1)
            pool.memset(terms[:, :, :], 0.0).then_inc(consts, 1)
            pool.memset(early[:, (RING0 - 2) * P:RING0 * P], 0.0).then_inc(consts, 1)
            pool.memset(x1[:, (RING1 - 1) * P:RING1 * P], 0.0).then_inc(consts, 1)
            pool.wait_ge(x_in, 32)
            pool.wait_ge(consts, CONSTS)
            stage_chunk(0, 0)
            stage_chunk(1, 1)
            for c in range(2):
                for half in range(2):
                    rstd_chunk(c, half)
            pool.wait_ge(x_rest_in, 32)
            for s in range(NS):
                step(0, s, False)
            with pool.Fori(1, ITERS - 1) as i:
                for s in range(NS):
                    step(i, s, False)
            for s in range(NS):
                step(ITERS - 1, s, True)
            for g in [group(ITERS - 1, NS - 1)] + TAIL:
                rstd_group(g)


            pool.wait_ge(act_done, GROUPS)
            def rstd_tokens(k, sem_in, at, rows, a, b):
                pool.wait_ge(sem_in, at)
                pool.tensor_scalar(vtok[0:rows, a:b], mv[0:rows, a:b, 1], 1.0, EPS, ALU.mult, ALU.add).then_inc(tok_var, 1)
                pool.wait_ge(tok_var, k + 1)
                pool.tensor_tensor(rtok[0:rows, a:b], vtok[0:rows, a:b], neg_half[0:rows, a:b], ALU.pow).then_inc(tok_rstd, 1)
            for part, (a, b) in enumerate(FLN_PARTS):
                rstd_tokens(part, fln_stats, 2 * part + 2, P, a, b)
            for t in range(2):
                rstd_tokens(2 + t, ln_stats, 2 * t + 2, TT, 4 * t, 4 * t + 4)
            pool.memset(vext, 1.0).then_inc(v_ones, 1)
            pool.wait_ge(tok_rstd, 4)
            pool.wait_ge(v_ones, 1)
            for rest in range(2):
                if rest == 1:
                    pool.wait_ge(low_made, 2 * PIECES)
                for k in range(2):
                    for p in range(PIECES):
                        w = slice(PIECE * p, PIECE * (p + 1))
                        if rest == 0:
                            low = slice(E - P, 2 * (E - P))
                            pool.wait_ge(rest_high_made, PIECES * k + p + 1)
                            pool.tensor_tensor(gu_rest[k][low, w], gu_raw[k][1][low, w], rest_high[low, k, w],
                                               ALU.subtract).then_inc(low_made, 1)
                        else:
                            pool.wait_ge(high_made, PIECES * k + p + 1)
                            pool.tensor_tensor(gu_low[k][:, w], gu_raw[k][0][:, w], gu_high[k][:, w],
                                               ALU.subtract).then_inc(low_made, 1)
            for a in range(NT):
                pool.wait_ge(rsum_done, a + 1)
                pool.tensor_tensor(att[:, a % 4, :, :], att[:, a % 4, :, :],
                                   rsum[:, :].unsqueeze(2).to_broadcast([TT, HEADS, TT]), ALU.mult).then_inc(scaled, 1)
            for t in range(2):
                rstd_tokens(4 + t, ln_stats, 2 * t + 6, TT, 4 * t, 4 * t + 4)

        @block.vector
        def _(dve):
            def copy_terms(m):
                dve.wait_ge(terms_turned, m + 1)
                wait(dve, conv0_done, m)
                nc.vector.tensor_copy(termsT[:, :], term_ps[:, 0:512]).then_inc(terms_copied, 1)

            def copy_stage(c):
                dve.wait_ge(stage_turned, c + 1)
                wait(dve, gram_x, c)
                nc.vector.tensor_copy(stageT[:, :], chunk_ps[0:CHUNK_SAMPLES, 0:P]).then_inc(stage_copied, 1)

            def quad_chunk(c, par):
                dve.wait_ge(gram_x, c + 1)
                wait(dve, vare0_made, c)
                nc.vector.tensor_tensor(quad[:, :, :], chunk_ps[:, :].rearrange("p (t k) -> p t k", k=TAPS0),
                                        window(par), ALU.mult).then_inc(quad_made, 1)

            def var_chunk(c):
                dve.wait_ge(quad_made, c + 1)
                nc.vector.tensor_reduce(var0[:, :], quad[:, :, :], AX.X, ALU.add).then_inc(var0_made, 1)
                dve.wait_ge(var0_made, c + 1)
                wait(dve, rstd0_made, 2 * c)
                nc.vector.tensor_scalar(vare0[:, :], var0[:, :], 0.0, EPS, ALU.max, ALU.add).then_inc(vare0_made, 1)

            def split_chunk(c, par, used, steps=range(SPLIT_STEPS)):
                t = terms[:, CHUNK * par:CHUNK * par + CHUNK, :]

                def section(a, n):
                    return t[:, :, TAPS0 * a:TAPS0 * (a + n)].rearrange("p t (s k) -> p t s k", k=TAPS0)

                def again(v, n):
                    return v[:, :, :].unsqueeze(2).to_broadcast([P, CHUNK, n, TAPS0])
                for step in steps:
                    wait(dve, split_step, SPLIT_STEPS * c + step)
                    if step == 0:
                        dve.wait_ge(rstd0_made, 2 * c + 2)
                        made = nc.vector.tensor_tensor(xs[:, :, :], window(par),
                                                       rstd0[:, :].unsqueeze(2).to_broadcast([P, CHUNK, TAPS0]), ALU.mult)
                    elif step == 1:
                        if used is not None:
                            dve.wait_ge(terms_turned, used)
                        made = nc.vector.tensor_copy(section(0, 3), again(xs, 3))
                    elif step == 2:
                        made = nc.vector.tensor_tensor(xrest[:, :, :], xs[:, :, :], t[:, :, 0:TAPS0], ALU.subtract)
                    elif step == 3:
                        made = nc.vector.tensor_copy(section(3, 2), again(xrest, 2))
                    else:
                        made = nc.vector.tensor_tensor(t[:, :, 5 * TAPS0:6 * TAPS0], xrest[:, :, :],
                                                       t[:, :, 3 * TAPS0:4 * TAPS0], ALU.subtract)
                    made.then_inc(split_step, 1)

            def sum_group(g):
                dve.wait_ge(sq_done, g.n + 1)
                wait(dve, rstd_step, g.n - 1)
                nc.vector.tensor_reduce(var[:, g.par, 0:g.tiles], sq[:, g.par, 0:g.tiles * P].rearrange("p (t c) -> p t c", c=P),
                                        AX.X, ALU.add).then_inc(var_done, 1)

            def norm_group(g):
                dve.wait_ge(rstd_done, g.n + 1)
                wait(dve, turned, g.n - 1)
                t = g.tiles
                nc.vector.tensor_tensor(yn[:, g.par, 0:t * P].rearrange("p (t c) -> p t c", c=P),
                                        prod[g.bank][:, 0:t * P].rearrange("p (t c) -> p t c", c=P),
                                        rstd[:, g.par, 0:t].unsqueeze(2).to_broadcast([P, t, P]), ALU.mult).then_inc(norm_done, 1)

            def step(i, s, last):
                if not last and s in CH_GRAM:
                    copy_stage(2 * i + CH_GRAM[s])
                if not last and s in CH_QUAD:
                    quad_chunk(2 * i + CH_QUAD[s], CH_QUAD[s] % 2)
                g = group(i, s)
                if g is not None and (g2 := back(i, s, 2)) is not None:
                    norm_group(g2)
                if g is not None and (g1 := back(i, s, 1)) is not None:
                    sum_group(g1)
                if s in BATCH and not (last and BATCH[s] == 5):
                    copy_terms(5 * i + BATCH[s])
                if not last:
                    if s in CH_QUAD:
                        var_chunk(2 * i + CH_QUAD[s])
                    for c, steps in CH_SPLIT.get(s, ()):
                        split_chunk(2 * i + c, c % 2, 5 * i + (3 if c == 2 else 5), steps)

            dve.wait_ge(w0_in, 2 * 16)
            done = [0]

            def w0_next(ins):
                done[0] += 1
                ins.then_inc(w0_step, 1)
                dve.wait_ge(w0_step, done[0])
            w0_next(nc.vector.tensor_reduce(w0mean[:, :], w0[:, :], AX.X, ALU.add))
            w0_next(nc.vector.tensor_scalar(w0mean[:, :], w0mean[:, :], -1.0 / P, None, ALU.mult))
            w0_next(nc.vector.tensor_scalar(w0[:, :], w0[:, :], w0mean[:, 0:1], None, ALU.add))
            dve.wait_ge(w0_turned, 1)
            nc.vector.tensor_copy(w0T[:, :], setup_ps[:, 0:GROW]).then_inc(gram_made, 1)
            dve.wait_ge(tables_in, 4 * 16)
            dve.wait_ge(w0_turned, 2)
            nc.vector.scalar_tensor_tensor(gram[:, :], setup_ps[0:GROW, 64:64 + GROW], 1.0 / P, diagonal_sb[:, :],
                                           ALU.mult, ALU.mult).then_inc(gram_made, 1)
            w0_next(nc.vector.tensor_copy(w0term[:, 0, :], w0[:, :]))
            w0_next(nc.vector.tensor_tensor(w0rest[:, :], w0[:, :], w0term[:, 0, :], ALU.subtract))
            w0_next(nc.vector.tensor_copy(w0term[:, 1, :], w0rest[:, :]))
            dve.wait_ge(gband_made, 1)
            nc.vector.tensor_copy(gband[:, :], setup_ps[0:CHUNK_SAMPLES, P:P + CHUNK * TAPS0]).then_inc(gband_ready, 1)
            w0_next(nc.vector.tensor_tensor(w0term[:, 2, :], w0rest[:, :], w0term[:, 1, :], ALU.subtract))
            copy_stage(0)
            w0_next(nc.vector.tensor_scalar(w0_stack[:, :], w0term[:, 0, :], pick_sb[:, 0:1], None, ALU.mult))
            quad_chunk(0, 0)
            var_chunk(0)
            copy_stage(1)
            for k in (1, 2):
                w0_next(nc.vector.scalar_tensor_tensor(w0_stack[:, :], w0term[:, k, :], pick_sb[:, k:k + 1], w0_stack[:, :],
                                                       ALU.mult, ALU.add))
            assert done[0] == W0_SPLIT
            quad_chunk(1, 1)
            dve.wait_ge(consts, CONSTS)
            split_chunk(0, 0, None)
            var_chunk(1)

            def centre(a, b, base):
                nc.vector.tensor_reduce(cmean[:, a:b], cw[:, a:b, :], AX.X, ALU.add).then_inc(cmean_step, 1)
                dve.wait_ge(cmean_step, base + 1)
                nc.vector.tensor_scalar(cmean[:, a:b], cmean[:, a:b], -1.0 / P, None, ALU.mult).then_inc(cmean_step, 1)
                dve.wait_ge(cmean_step, base + 2)
                for k in range(a, b):
                    last = nc.vector.tensor_scalar(cw[:, k, :], cw[:, k, :], cmean[:, k:k + 1], None, ALU.add)
                last.then_inc(cw_ready, 1)
            copy_terms(0)
            dve.wait_ge(cw_in, 16)
            centre(0, EARLY_BLOCKS, 0)
            split_chunk(1, 1, None)
            for s in range(NS):
                step(0, s, False)
            dve.wait_ge(cw2_in, 16)
            centre(EARLY_BLOCKS, BLOCKS, 2)
            with dve.Fori(1, ITERS - 1) as i:
                for s in range(NS):
                    step(i, s, False)
            for s in range(NS):
                step(ITERS - 1, s, True)
            every = [group(ITERS - 1, NS - 2), group(ITERS - 1, NS - 1)] + TAIL
            normed = 0
            for k, g in enumerate(every):
                after = max(every[k + 1].fed) if 1 <= k + 1 < len(every) and every[k + 1].fed else 0
                if k > 0:
                    sum_group(g)
                while normed <= k and (normed < k or after >= g.n - 2 or g is every[-1]):
                    norm_group(every[normed])
                    normed += 1

            for part, (a, b) in enumerate(FLN_PARTS):
                dve.wait_ge(fln_turned, part + 1)
                for j in range(a, b):
                    last = nc.vector.bn_stats(stat[:, j, :], ps[:, FLN_BANK[part], P * (j - a):P * (j - a) + P])
                last.then_inc(fln_stats, 1)
                dve.wait_ge(fln_stats, 2 * part + 1)
                for j in range(a, b):
                    last = nc.vector.bn_aggr(mv[:, j, :], stat[:, j, :])
                last.then_inc(fln_stats, 1)
            for part, (a, b) in enumerate(FLN_PARTS):
                dve.wait_ge(tok_rstd, part + 1)
                for j in range(a, b):
                    last = nc.vector.tensor_scalar(sq[:, part, P * (j - a):P * (j - a) + P],
                                                   ps[:, FLN_BANK[part], P * (j - a):P * (j - a) + P], mv[:, j, 0:1],
                                                   rtok[:, j:j + 1], ALU.subtract, ALU.mult)
                last.then_inc(fln_norm, 1)

            def add_bias(k):
                dve.wait_ge(proj_done, k + 1)
                nc.vector.tensor_tensor(h1[:, 2 * k:2 * k + 2, :], ps[0:TT, 4 + k, 0:2 * E].rearrange("p (a e) -> p a e", e=E),
                                        proj_b_sb[:, :].unsqueeze(1).to_broadcast([TT, 2, E]), ALU.add).then_inc(h1_ready, 1)

            def join_stats(which, t):
                dve.wait_ge(ln_stats, 4 * which + 2 * t + 1)
                for a in range(4 * t, 4 * t + 4):
                    last = nc.vector.bn_aggr(mv[0:TT, a, :], stat[0:TT, a, :])
                last.then_inc(ln_stats, 1)

            def norm_tokens(which, t, h):
                dve.wait_ge(tok_rstd, 3 + 2 * which + t)
                for a in range(4 * t, 4 * t + 4):
                    last = nc.vector.tensor_scalar(y[:, a, 0:E], h[:, a, :], mv[0:TT, a, 0:1], rtok[0:TT, a:a + 1],
                                                   ALU.subtract, ALU.mult)
                    if which == 1:
                        last = nc.vector.tensor_scalar(y[:, a, E:2 * P], h[:, a, P:E], mv[0:TT, a, 0:1], rtok[0:TT, a:a + 1],
                                                       ALU.subtract, ALU.mult)
                    last.then_inc(ln_norm, 1)

            def copy_tokens(which, t, bank):
                dve.wait_ge(ln_turned, 2 * which + t + 1)
                tok = slice(HALF * t, HALF * t + HALF)
                nc.vector.tensor_copy(yT_b[0:E - P, tok], ps[0:E - P, bank, 0:HALF]).then_inc(yTb_ready, 1)
                if which == 1:
                    dve.wait_ge(yT_high_made, t + 1)
                    nc.vector.tensor_tensor(yT_low[:, tok], ps[:, bank - 1, 0:HALF], yT_high[:, tok], ALU.subtract)
                    dve.wait_ge(yT_rest_made, t + 1)
                    nc.vector.tensor_tensor(yT_rest_low[:, t, :], ps[0:E - P, bank, 0:HALF], yT_rest[0:E - P, tok],
                                            ALU.subtract).then_inc(yT_low_made, 1)

            def copy_group(g):
                dve.wait_ge(qkv_done, g + 1)
                qkv_copy(g, nc.vector.tensor_copy).then_inc(qk_by_dve, 1)
            dve.wait_ge(proj_in, 32)
            for t in range(2):
                add_bias(2 * t)
                add_bias(2 * t + 1)
                for a in range(4 * t, 4 * t + 4):
                    dve.wait_ge(h1_ready, a // 2 + 1)
                    last = nc.vector.bn_stats(stat[0:TT, a, :], h1[:, a, :])
                last.then_inc(ln_stats, 1)
                join_stats(0, t)
            norm_tokens(0, 0, h1)
            norm_tokens(0, 1, h1)
            dve.wait_ge(att_in, ATT_LOADS * 16)
            copy_tokens(0, 0, 2)
            copy_group(1)
            copy_tokens(0, 1, 3)
            copy_group(3)
            copy_group(5)
            for step_a in range(NT + 5):
                a = step_a

                def scores(half):
                    return ps[0:TT, 2 * half:2 * half + 2, 0:3 * TT].rearrange("p r (c k) -> p r c k", k=TT)

                def tops(half):
                    return top[:, 6 * half:6 * half + 6].rearrange("p (r c) -> p r c", c=3)

                def largest(a, half):
                    dve.wait_ge(scores_done, 2 * a + half + 1)
                    wait(dve, shifted, 2 * a - 1 + half)
                    nc.vector.tensor_reduce(tops(half), scores(half), AX.X, ALU.max).then_inc(top_done, 1)
                if a < NT:
                    largest(a, 0)
                if step_a == LN2_STEP + 2:
                    copy_tokens(1, 0, 1)
                a = step_a - 5
                if a >= 0:
                    dve.wait_ge(out_done, a + 1)
                    nc.vector.tensor_tensor(h2[:, a, :], attn_out(a), h1[:, a, :], ALU.add).then_inc(h2_ready, 1)
                a = step_a
                if a < NT:
                    largest(a, 1)
                    if a == 0:
                        dve.wait_ge(low_made, 2 * PIECES)
                    wait(dve, att_turned, a - 3)
                    for half in range(2):
                        dve.wait_ge(top_done, 2 * a + half + 1)
                        nc.vector.tensor_tensor(att[:, a % 4, 6 * half:6 * half + 6, :].rearrange("p (r c) k -> p r c k", c=3),
                                                scores(half), tops(half).unsqueeze(3).to_broadcast([TT, 2, 3, TT]),
                                                ALU.subtract).then_inc(shifted, 1)
                a = step_a - 5
                if a >= 0:
                    dve.wait_ge(h2_ready, a + 1)
                    last = nc.vector.bn_stats(stat[0:TT, a, :], h2[:, a, :])
                    if a % 4 == 3:
                        last.then_inc(ln_stats, 1)
                        join_stats(1, a // 4)
                if step_a == LN2_STEP:
                    norm_tokens(1, 0, h2)
                a = step_a - 1
                if 0 <= a < NT:
                    dve.wait_ge(exp_done, a + 1)
                    wait(dve, rsum_done, a)
                    nc.vector.tensor_reduce(total[:, :], att[:, a % 4, :, :], AX.X, ALU.add).then_inc(total_done, 1)
                    dve.wait_ge(total_done, a + 1)
                    wait(dve, scaled, a)
                    nc.vector.reciprocal(rsum[:, :], total[:, :]).then_inc(rsum_done, 1)

            def gate_units(v):
                c, t = UNITS[v]
                dve.wait_ge(silu_done, v + 1)
                nc.vector.tensor_tensor(hidden[:, hidden_slot(c), HALF * t:HALF * t + HALF], ps[:, 2 * (v % 2) + 1, 0:HALF], silu[:, v % 2, :],
                                        ALU.mult).then_inc(hid_ready, 1)
            gate_units(0)
            norm_tokens(1, 1, h2)
            gate_units(1)
            copy_tokens(1, 1, 5)
            gate_units(2)
            gate_units(3)

            steps = [0]

            def router_next(ins):
                steps[0] += 1
                ins.then_inc(router_step, 1)
                dve.wait_ge(router_step, steps[0])

            def wide(v):
                return v.unsqueeze(2).to_broadcast([P, NF, EXPERTS])
            ranks = rank_sb[:, :].rearrange("p (f e) -> p f e", e=EXPERTS)
            best, alpha, m1, k1, m2, k2, rest = (small[:, k, :] for k in (0, 1, 2, 3, 4, 5, 6))
            dve.wait_ge(router_done, 1)
            router_next(nc.vector.tensor_copy(logits[:, :, :], ps[:, 6, 0:NF * (EXPERTS + 1)].rearrange("p (f e) -> p f e", e=EXPERTS + 1)))
            router_next(nc.vector.tensor_reduce(best, logits[:, :, 0:EXPERTS], AX.X, ALU.max))
            router_next(nc.vector.tensor_tensor(prob[:, :, :], logits[:, :, 0:EXPERTS], wide(best), ALU.subtract))
            dve.wait_ge(router_exp, 2)
            router_next(nc.vector.tensor_scalar(alpha, alpha, 1.0, None, ALU.add))
            router_next(nc.vector.reciprocal(alpha, alpha))
            for value, k, chosen, left in ((m1, k1, first, prob), (m2, k2, second, key)):
                router_next(nc.vector.tensor_reduce(value, left[:, :, :], AX.X, ALU.max))
                router_next(nc.vector.tensor_tensor(chosen[:, :, :], left[:, :, :], wide(value), ALU.is_ge))
                router_next(nc.vector.tensor_tensor(chosen[:, :, :], chosen[:, :, :], ranks, ALU.mult))
                router_next(nc.vector.tensor_reduce(k, chosen[:, :, :], AX.X, ALU.max))
                router_next(nc.vector.tensor_tensor(chosen[:, :, :], chosen[:, :, :], wide(k), ALU.is_equal))
                gate_units(EARLY_UNITS + (chosen is second))
                if chosen is first:
                    router_next(nc.vector.scalar_tensor_tensor(key[:, :, :], first[:, :, :], -2.0, prob[:, :, :], ALU.mult, ALU.add))
            router_next(nc.vector.tensor_tensor(rest, m1, m2, ALU.add))
            router_next(nc.vector.reciprocal(rest, rest))
            router_next(nc.vector.tensor_scalar(best, alpha, -1.0, 1.0, ALU.mult, ALU.add))
            router_next(nc.vector.tensor_tensor(rest, rest, best, ALU.mult))
            gate_units(EARLY_UNITS + 2)
            router_next(nc.vector.tensor_tensor(first[:, :, :], first[:, :, :], second[:, :, :], ALU.add))
            router_next(nc.vector.tensor_tensor(gates[:, :, :], first[:, :, :], prob[:, :, :], ALU.mult))
            router_next(nc.vector.tensor_tensor(gates[:, :, :], gates[:, :, :], wide(rest), ALU.mult))

            def add_down(d):
                for f in range(NF):
                    if f % 2 == 0:
                        dve.wait_ge(down_done, NF // 2 * d + f // 2 + 1)
                    if d == 0:
                        dve.wait_ge(h2_moved, 32)
                        weight = small[:, 1, f:f + 1]
                    else:
                        dve.wait_ge(acc_done, NF * (d - 1) + f + 1)
                        weight = gates[:, f, d - 1:d]
                    nc.vector.scalar_tensor_tensor(acc[:, f, :], ps[:, 4 + f // 2, E * (f % 2):E * (f % 2) + E], weight, acc[:, f, :],
                                                   ALU.mult, ALU.add).then_inc(acc_done, 1)
            for kind, k in FFN_ORDER[EARLY_UNITS + 3:]:
                (gate_units if kind == "hidden" else add_down)(k)


def layout(a):
    f, b16 = np.float32, mybir.dt.np(BF16)
    w0 = a["L0_tok_conv_w0"][:, 0, :].T
    rows, pick = np.zeros((P, P), f), np.zeros((P, 3), f)
    for side in (0, 64):
        for section, term in enumerate((0, 1, 2, 0, 1, 0)):
            at = side + TAPS0 * section
            rows[at:at + TAPS0] = w0
            pick[at:at + TAPS0, term] = 1
    shift = np.zeros((GROW, SHIFT_AT + CHUNK_SAMPLES), f)
    for t in range(SECTIONS):
        for j in range(TAPS0):
            shift[TAPS0 * t + j, SHIFT_AT + STRIDE0 * t + j] = 1
    names = [f"ln_g{k}" for k in range(7)] + ["fln_g"] + [f"ln_b{k}" for k in range(7)] + ["fln_b"]

    def with_bias(w, bias):
        return np.concatenate([w, bias[None, :]])

    def by_head(w):
        out = np.zeros((w.shape[0], HEADS, 32), f)
        out[:, :, 0:HD] = w.reshape(w.shape[0], HEADS, HD)
        return out.reshape(w.shape[0], HEADS * 32)

    def beside(w, shared):
        w = np.concatenate([w.transpose(1, 0, 2).reshape(E, EXPERTS * E), shared], axis=1)
        return np.concatenate([w, w[P:]])

    router = np.concatenate([a["L0_ffn_router_w"], a["L0_ffn_sg_w"]], axis=1)
    router_bias = np.concatenate([np.zeros(EXPERTS, f), a["L0_ffn_sg_b"]])
    down = np.zeros((P, DOWN_BLOCKS, E), f)
    routed = a["L0_ffn_w_down"].reshape(ROUTED_HC, P, E)
    for pair in range(EXPERTS // 2):
        down[:, 4 * pair] = routed[3 * pair]
        down[0:64, 4 * pair + 1] = routed[3 * pair + 1, 0:64]
        down[64:, 4 * pair + 2] = routed[3 * pair + 1, 64:]
        down[:, 4 * pair + 3] = routed[3 * pair + 2]
    down[:, 4 * (EXPERTS // 2):] = a["L0_ffn_ws_down"].reshape(HC - ROUTED_HC, P, E).transpose(1, 0, 2)
    same = (np.arange(TOK) // FRAMES % CLIPS_T)[None, :] == np.arange(CLIPS_T)[:, None]
    pick_clip = np.zeros((CLIPS_T, HEADS, 32), f)
    pick_clip[np.arange(CLIPS_T), :, HD + np.arange(CLIPS_T)] = 1
    pick_clip = pick_clip.reshape(CLIPS_T, HEADS * 32)
    wq = by_head(with_bias(a["L0_attn_Wq"].T, a["L0_attn_bq"]))
    wk = by_head(with_bias(a["L0_attn_Wk"].T, a["L0_attn_bk"]))
    wk[E] = np.where(pick_clip.any(axis=0), f(MASK), wk[E])
    wo = np.zeros((3, 4, 32, E), f)
    wo[:, :, 0:HD] = a["L0_attn_Wo"].T.reshape(3, 4, HD, E)
    wo[0, 0, HD] = a["L0_attn_bo"]
    return {
        "x": a["x"],
        "conv_w": np.concatenate([a[f"L0_tok_conv_w{k}"].transpose(1, 2, 0) for k in range(1, 7)], axis=1),
        "w0_rows": rows, "pick_term": pick, "shift": shift,
        "diagonal": np.kron(np.eye(SECTIONS, dtype=f), np.ones((TAPS0, TAPS0), f)),
        "columns": np.stack([a[f"L0_tok_{n}"] for n in names], axis=1),
        "ident": np.eye(P, dtype=f), "ident_b": np.eye(P, dtype=b16),
        "proj": a["L0_tok_proj_w"], "proj_b": np.tile(a["L0_tok_proj_b"], (TT, 1)),
        "wq": np.concatenate([wq, pick_clip]),
        "wk": np.concatenate([wk, np.where(pick_clip == 1, f(-MASK), f(0))]),
        "wv": with_bias(a["L0_attn_Wv"].T, a["L0_attn_bv"]),
        "wo": wo.reshape(3, P, E).transpose(1, 0, 2),
        "router": with_bias(router, router_bias),
        "gate": beside(a["L0_ffn_w_gate"], a["L0_ffn_ws_gate"]),
        "up": beside(a["L0_ffn_w_up"], a["L0_ffn_ws_up"]),
        "down": down,
        "token_rows": np.concatenate([np.ones((1, TOK), f), same.astype(f)]),
        "rank": np.tile(np.arange(EXPERTS, 0, -1, dtype=f), (P, NF)),
    }


def kernel(**inputs):
    import concourse.bacc as bacc
    from concourse.bass_utils import run_bass_kernel_spmd as run
    arrays = {k: np.ascontiguousarray(v) for k, v in layout({k: np.asarray(v) for k, v in inputs.items()}).items()}
    nc = bacc.Bacc("TRN2", target_bir_lowering=False, num_devices=1)
    ins = {k: nc.dram_tensor(f"in_{k}", v.shape, mybir.dt.from_np(v.dtype), kind="ExternalInput").ap()
           for k, v in arrays.items()}
    out = nc.dram_tensor("out", (TOK, E), F32, kind="ExternalOutput").ap()
    audio_tower(nc, **ins, out=out)
    r = run(nc, [{f"in_{k}": v for k, v in arrays.items()}], core_ids=[0])
    return r.results[0]["out"].reshape(CLIPS, FRAMES, E)
```
